# Optimizing a Trainium2 kernel written in Bass

```python
import numpy as np
import jax
import jax.numpy as jnp

def _softmax(x, axis=-1):
    return jax.nn.softmax(x, axis=axis)

def _gelu(x):
    return jax.nn.gelu(x, approximate=True)

def _silu(x):
    return jax.nn.silu(x)

def _sigmoid(x):
    return jax.nn.sigmoid(x)

def _layernorm(x, axis=-1, eps=1e-05):
    m = jnp.mean(x, axis=axis, keepdims=True)
    v = jnp.var(x, axis=axis, keepdims=True)
    return (x - m) / jnp.sqrt(v + eps)

def _scatter_add(tgt, idx, src, axis=0):
    return tgt.at[idx].add(src)

def _segment_sum(src, seg, n):
    return jax.ops.segment_sum(src, seg, n)
kernel_name = 'mk_perceiver_d2_seqx_r8_351592'

def setup_inputs(seed: int=0):
    np.random.seed(seed)
    _w = jnp.asarray

    def _rec_inputs():
        import jax
        import jax.numpy as jnp
        _rk = jax.random.key(seed)
        x = -0.0002928 + 1 * jax.random.normal(jax.random.fold_in(_rk, 1), (64, 32, 128), jnp.float32)
        _lenS = 32 - jax.random.randint(jax.random.fold_in(_rk, 7), (64,), 0, max(1, 32 // 4) + 1, jnp.int32)
        _lenS2 = 257 - jax.random.randint(jax.random.fold_in(_rk, 8), (64,), 0, max(1, 257 // 4) + 1, jnp.int32)
        _ctx_1024P = jax.random.normal(jax.random.fold_in(_rk, 11), (64, 16, 128), jnp.float32)
        _ctx_1024c = jax.random.dirichlet(jax.random.fold_in(_rk, 511), 0.3 * jnp.ones((16,), jnp.float32), (64, 257))
        _ctx_1024t = jnp.einsum('bsk,bkd->bsd', _ctx_1024c, _ctx_1024P)
        _ctx_1024t = _ctx_1024t * jax.lax.rsqrt(jnp.mean(jnp.square(_ctx_1024t)) + 1e-12) * 0.953939
        ctx_1024 = -1.39393e-06 + 0.999914 * (_ctx_1024t + 0.3 * jax.random.normal(jax.random.fold_in(_rk, 611), (64, 257, 128), jnp.float32))
        _validS = jnp.arange(32)[None, :] < _lenS[:, None]
        _validS2 = jnp.arange(257)[None, :] < _lenS2[:, None]
        _causal = jnp.tril(jnp.ones((32, 32), dtype=bool))
        mask_Bx1xSxS2_ik1 = jnp.where(jnp.broadcast_to(_validS2[:, None, None, :], (64, 1, 32, 257)), 1, 0).astype(jnp.int32)
        return (x, ctx_1024, mask_Bx1xSxS2_ik1)
    x, ctx_1024, mask_Bx1xSxS2_ik1 = _rec_inputs()

    def _L0_xattn_setup():
        import jax, jax.numpy as jnp
        import numpy as np
        D_MODEL = 128
        NUM_HEADS = 16
        DEPTH = D_MODEL // NUM_HEADS
        NORM = 1.0 / np.sqrt(DEPTH)
        B, S = (2, 256)

        def _split_heads(x):
            b, s, _ = x.shape
            return x.reshape(b, s, NUM_HEADS, DEPTH).transpose(0, 2, 1, 3)
        key = jax.random.key(seed)
        ks = jax.random.split(key, 12)
        std = 1.0 / np.sqrt(D_MODEL)
        inp = {'Q': jax.random.normal(ks[0], (B, S, D_MODEL), jnp.float32), 'K': jax.random.normal(ks[1], (B, S, D_MODEL), jnp.float32), 'V': jax.random.normal(ks[2], (B, S, D_MODEL), jnp.float32), 'mask': jax.random.randint(ks[3], (B, 1, S, S), 0, 2, jnp.int32), 'Wq': jax.random.normal(ks[4], (D_MODEL, D_MODEL), jnp.float32) * std, 'bq': jax.random.normal(ks[5], (D_MODEL,), jnp.float32) * std, 'Wk': jax.random.normal(ks[6], (D_MODEL, D_MODEL), jnp.float32) * std, 'bk': jax.random.normal(ks[7], (D_MODEL,), jnp.float32) * std, 'Wv': jax.random.normal(ks[8], (D_MODEL, D_MODEL), jnp.float32) * std, 'bv': jax.random.normal(ks[9], (D_MODEL,), jnp.float32) * std, 'Wo': jax.random.normal(ks[10], (D_MODEL, D_MODEL), jnp.float32) * std, 'bo': jax.random.normal(ks[11], (D_MODEL,), jnp.float32) * std}
        return inp
    _L0_xattn_all = _L0_xattn_setup()
    _L0_xattn_in = {k: v for k, v in _L0_xattn_all.items() if k in ('Wq', 'bq', 'Wk', 'bk', 'Wv', 'bv', 'Wo', 'bo')}
    del _L0_xattn_all

    def _L0_attn_setup():
        import jax, jax.numpy as jnp
        import numpy as np
        _J6 = jnp.array([[0, 0, 0, 0, 0, 1], [0, 0, 0, 0, -1, 0], [0, 0, 0, 1, 0, 0], [0, 0, 1, 0, 0, 0], [0, -1, 0, 0, 0, 0], [1, 0, 0, 0, 0, 0]], dtype=jnp.float32)
        _PI = np.array([0, 0, 0, 1, 1, 2])
        _PJ = np.array([1, 2, 3, 2, 3, 3])

        def plucker_lines(p1, p2):
            lines = p1[..., _PI] * p2[..., _PJ] - p1[..., _PJ] * p2[..., _PI]
            n = jnp.linalg.norm(lines, axis=-1, keepdims=True)
            return lines / jnp.maximum(n, 1e-12)
        key = jax.random.key(seed)
        ks = jax.random.split(key, 6)
        B, T, D, H = (1, 256, 128, 16)
        s = D ** (-0.5)
        x = jax.random.normal(ks[0], (B, T, D), jnp.float32)
        Wqkv = jax.random.normal(ks[1], (D, 3 * D), jnp.float32) * s
        bqkv = jnp.zeros((3 * D,), jnp.float32)
        W1p = jax.random.normal(ks[2], (D, 4 * H), jnp.float32) * s
        W2p = jax.random.normal(ks[3], (D, 4 * H), jnp.float32) * s
        plucker_scale = jnp.full((H,), 0.1, jnp.float32)
        Wout = jax.random.normal(ks[4], (D, D), jnp.float32) * s
        bout = jnp.zeros((D,), jnp.float32)
        return {'x': x, 'Wqkv': Wqkv, 'bqkv': bqkv, 'W1p': W1p, 'W2p': W2p, 'plucker_scale': plucker_scale, 'Wout': Wout, 'bout': bout}
    _L0_attn_all = _L0_attn_setup()
    _L0_attn_in = {k: v for k, v in _L0_attn_all.items() if k in ('Wqkv', 'bqkv', 'W1p', 'W2p', 'plucker_scale', 'Wout', 'bout')}
    del _L0_attn_all

    def _L0_ffn_setup():
        import jax, jax.numpy as jnp
        import numpy as np
        N_EXPERTS = 8
        N_GROUP = 4
        TOPK_GROUP = 2
        TOP_K = 2
        HIDDEN = 128
        INTER = 256
        B, S = (1, 128)

        def _grouped_topk(scores):
            T, E = scores.shape
            per_group = E // N_GROUP
            group_scores = scores.reshape(T, N_GROUP, per_group).max(-1)
            _, gidx = jax.lax.top_k(group_scores, TOPK_GROUP)
            gmask = jnp.zeros((T, N_GROUP), scores.dtype).at[jnp.arange(T)[:, None], gidx].set(1.0)
            smask = jnp.repeat(gmask, per_group, axis=1)
            masked = jnp.where(smask > 0, scores, 0.0)
            topk_w, topk_ids = jax.lax.top_k(masked, TOP_K)
            topk_w = topk_w / topk_w.sum(-1, keepdims=True)
            return (topk_ids, topk_w)
        key = jax.random.key(seed)
        k1, k2, k3, k4 = jax.random.split(key, 4)
        return {'hidden_states': jax.random.normal(k1, (B, S, HIDDEN), jnp.float32), 'gate_w': jax.random.normal(k2, (N_EXPERTS, HIDDEN), jnp.float32) * 0.02, 'w13_weight': jax.random.normal(k3, (N_EXPERTS, 2 * INTER, HIDDEN), jnp.float32) * 0.02, 'w2_weight': jax.random.normal(k4, (N_EXPERTS, HIDDEN, INTER), jnp.float32) * 0.02}
    _L0_ffn_all = _L0_ffn_setup()
    _L0_ffn_in = {k: v for k, v in _L0_ffn_all.items() if k in ('gate_w', 'w13_weight', 'w2_weight')}
    del _L0_ffn_all

    def _L1_xattn_setup():
        import jax, jax.numpy as jnp
        import numpy as np
        D_MODEL = 128
        NUM_HEADS = 16
        HEAD_DIM = D_MODEL // NUM_HEADS
        key = jax.random.key(seed)
        ks = jax.random.split(key, 11)
        B, S = (4, 256)
        s = 1.0 / np.sqrt(D_MODEL)
        inp = {'query': jax.random.normal(ks[0], (B, S, D_MODEL), jnp.float32), 'key': jax.random.normal(ks[1], (B, S, D_MODEL), jnp.float32), 'value': jax.random.normal(ks[2], (B, S, D_MODEL), jnp.float32), 'W_q': jax.random.normal(ks[3], (D_MODEL, D_MODEL), jnp.float32) * s, 'b_q': jnp.zeros((D_MODEL,), jnp.float32), 'W_k': jax.random.normal(ks[4], (D_MODEL, D_MODEL), jnp.float32) * s, 'b_k': jnp.zeros((D_MODEL,), jnp.float32), 'W_v': jax.random.normal(ks[5], (D_MODEL, D_MODEL), jnp.float32) * s, 'b_v': jnp.zeros((D_MODEL,), jnp.float32), 'W_o': jax.random.normal(ks[6], (D_MODEL, D_MODEL), jnp.float32) * s, 'b_o': jnp.zeros((D_MODEL,), jnp.float32)}
        return inp
    _L1_xattn_all = _L1_xattn_setup()
    _L1_xattn_in = {k: v for k, v in _L1_xattn_all.items() if k in ('W_q', 'b_q', 'W_k', 'b_k', 'W_v', 'b_v', 'W_o', 'b_o')}
    del _L1_xattn_all

    def _L1_attn_setup():
        import jax, jax.numpy as jnp
        import numpy as np
        EMBED_DIM = 128
        NUM_HEAD = 16
        NEG_BIG = 10000000000.0
        key = jax.random.key(seed)
        k_x, k_w1, k_b1, k_w2, k_b2 = jax.random.split(key, 5)
        B, S, E = (4, 256, EMBED_DIM)
        std = 1.0 / np.sqrt(E)
        return {'x': jax.random.normal(k_x, (B, S, E), dtype=jnp.float32), 'W1': jax.random.uniform(k_w1, (E, 3 * E), dtype=jnp.float32, minval=-std, maxval=std), 'b1': jax.random.uniform(k_b1, (3 * E,), dtype=jnp.float32, minval=-std, maxval=std), 'W2': jax.random.uniform(k_w2, (E, E), dtype=jnp.float32, minval=-std, maxval=std), 'b2': jax.random.uniform(k_b2, (E,), dtype=jnp.float32, minval=-std, maxval=std)}
    _L1_attn_all = _L1_attn_setup()
    _L1_attn_in = {k: v for k, v in _L1_attn_all.items() if k in ('W1', 'b1', 'W2', 'b2')}
    del _L1_attn_all

    def _L1_ffn_setup():
        import jax, jax.numpy as jnp
        import numpy as np
        N_EMBD = 128
        NUM_EXPERTS = 8
        TOP_K = 2
        D_FF = 4 * N_EMBD
        B, S = (4, 256)
        key = jax.random.key(seed)
        ks = jax.random.split(key, 7)
        scale = lambda fan_in: 1.0 / np.sqrt(fan_in)
        x = jax.random.normal(ks[0], (B, S, N_EMBD), dtype=jnp.float32)
        W_router = jax.random.normal(ks[1], (N_EMBD, NUM_EXPERTS), dtype=jnp.float32) * scale(N_EMBD)
        b_router = jnp.zeros((NUM_EXPERTS,), dtype=jnp.float32)
        W1 = jax.random.normal(ks[2], (NUM_EXPERTS, N_EMBD, D_FF), dtype=jnp.float32) * scale(N_EMBD)
        b1 = jnp.zeros((NUM_EXPERTS, D_FF), dtype=jnp.float32)
        W2 = jax.random.normal(ks[3], (NUM_EXPERTS, D_FF, N_EMBD), dtype=jnp.float32) * scale(D_FF)
        b2 = jnpp = jnp.zeros((NUM_EXPERTS, N_EMBD), dtype=jnp.float32)
        return {'x': x, 'W_router': W_router, 'b_router': b_router, 'W1': W1, 'b1': b1, 'W2': W2, 'b2': b2}
    _L1_ffn_all = _L1_ffn_setup()
    _L1_ffn_in = {k: v for k, v in _L1_ffn_all.items() if k in ('W_router', 'b_router', 'W1', 'b1', 'W2', 'b2')}
    del _L1_ffn_all
    return {'x': x, 'ctx_1024': ctx_1024, 'mask_Bx1xSxS2_ik1': mask_Bx1xSxS2_ik1, 'L0_xattn_Wq': _L0_xattn_in['Wq'], 'L0_xattn_bq': _L0_xattn_in['bq'], 'L0_xattn_Wk': _L0_xattn_in['Wk'], 'L0_xattn_bk': _L0_xattn_in['bk'], 'L0_xattn_Wv': _L0_xattn_in['Wv'], 'L0_xattn_bv': _L0_xattn_in['bv'], 'L0_xattn_Wo': _L0_xattn_in['Wo'], 'L0_xattn_bo': _L0_xattn_in['bo'], 'L0_attn_Wqkv': _L0_attn_in['Wqkv'], 'L0_attn_bqkv': _L0_attn_in['bqkv'], 'L0_attn_W1p': _L0_attn_in['W1p'], 'L0_attn_W2p': _L0_attn_in['W2p'], 'L0_attn_plucker_scale': _L0_attn_in['plucker_scale'], 'L0_attn_Wout': _L0_attn_in['Wout'], 'L0_attn_bout': _L0_attn_in['bout'], 'L0_ffn_gate_w': _L0_ffn_in['gate_w'], 'L0_ffn_w13_weight': _L0_ffn_in['w13_weight'], 'L0_ffn_w2_weight': _L0_ffn_in['w2_weight'], 'L1_xattn_W_q': _L1_xattn_in['W_q'], 'L1_xattn_b_q': _L1_xattn_in['b_q'], 'L1_xattn_W_k': _L1_xattn_in['W_k'], 'L1_xattn_b_k': _L1_xattn_in['b_k'], 'L1_xattn_W_v': _L1_xattn_in['W_v'], 'L1_xattn_b_v': _L1_xattn_in['b_v'], 'L1_xattn_W_o': _L1_xattn_in['W_o'], 'L1_xattn_b_o': _L1_xattn_in['b_o'], 'L1_attn_W1': _L1_attn_in['W1'], 'L1_attn_b1': _L1_attn_in['b1'], 'L1_attn_W2': _L1_attn_in['W2'], 'L1_attn_b2': _L1_attn_in['b2'], 'L1_ffn_W_router': _L1_ffn_in['W_router'], 'L1_ffn_b_router': _L1_ffn_in['b_router'], 'L1_ffn_W1': _L1_ffn_in['W1'], 'L1_ffn_b1': _L1_ffn_in['b1'], 'L1_ffn_W2': _L1_ffn_in['W2'], 'L1_ffn_b2': _L1_ffn_in['b2']}

def reference(x, ctx_1024, mask_Bx1xSxS2_ik1, L0_xattn_Wq, L0_xattn_bq, L0_xattn_Wk, L0_xattn_bk, L0_xattn_Wv, L0_xattn_bv, L0_xattn_Wo, L0_xattn_bo, L0_attn_Wqkv, L0_attn_bqkv, L0_attn_W1p, L0_attn_W2p, L0_attn_plucker_scale, L0_attn_Wout, L0_attn_bout, L0_ffn_gate_w, L0_ffn_w13_weight, L0_ffn_w2_weight, L1_xattn_W_q, L1_xattn_b_q, L1_xattn_W_k, L1_xattn_b_k, L1_xattn_W_v, L1_xattn_b_v, L1_xattn_W_o, L1_xattn_b_o, L1_attn_W1, L1_attn_b1, L1_attn_W2, L1_attn_b2, L1_ffn_W_router, L1_ffn_b_router, L1_ffn_W1, L1_ffn_b1, L1_ffn_W2, L1_ffn_b2):
    import jax
    import jax.numpy as jnp

    def _L0_xattn_ref(Q, K, V, mask, Wq, bq, Wk, bk, Wv, bv, Wo, bo):
        import jax, jax.numpy as jnp
        import numpy as np
        D_MODEL = 128
        NUM_HEADS = 16
        DEPTH = D_MODEL // NUM_HEADS
        NORM = 1.0 / np.sqrt(DEPTH)
        B, S = (2, 256)

        def _split_heads(x):
            b, s, _ = x.shape
            return x.reshape(b, s, NUM_HEADS, DEPTH).transpose(0, 2, 1, 3)
        q = _split_heads(Q @ Wq.T + bq)
        k = _split_heads(K @ Wk.T + bk)
        v = _split_heads(V @ Wv.T + bv)
        scores = jnp.einsum('bhqd,bhkd->bhqk', q, k) * NORM
        scores = scores + jnp.where(mask == 0, jnp.float32(-1000000000.0), scores)
        attn = jax.nn.softmax(scores, axis=-1)
        ctx = jnp.einsum('bhqk,bhkd->bhqd', attn, v)
        b, h, s, d = ctx.shape
        ctx = ctx.transpose(0, 2, 1, 3).reshape(b, s, D_MODEL)
        return ctx @ Wo.T + bo

    def _L0_attn_ref(x, Wqkv, bqkv, W1p, W2p, plucker_scale, Wout, bout):
        import jax, jax.numpy as jnp
        import numpy as np
        _J6 = jnp.array([[0, 0, 0, 0, 0, 1], [0, 0, 0, 0, -1, 0], [0, 0, 0, 1, 0, 0], [0, 0, 1, 0, 0, 0], [0, -1, 0, 0, 0, 0], [1, 0, 0, 0, 0, 0]], dtype=jnp.float32)
        _PI = np.array([0, 0, 0, 1, 1, 2])
        _PJ = np.array([1, 2, 3, 2, 3, 3])

        def plucker_lines(p1, p2):
            lines = p1[..., _PI] * p2[..., _PJ] - p1[..., _PJ] * p2[..., _PI]
            n = jnp.linalg.norm(lines, axis=-1, keepdims=True)
            return lines / jnp.maximum(n, 1e-12)
        B, T, D = x.shape
        H = plucker_scale.shape[0]
        dh = D // H
        qkv = (x @ Wqkv + bqkv).reshape(B, T, 3, H, dh)
        q = jnp.transpose(qkv[:, :, 0], (0, 2, 1, 3))
        k = jnp.transpose(qkv[:, :, 1], (0, 2, 1, 3))
        v = jnp.transpose(qkv[:, :, 2], (0, 2, 1, 3))
        std_logits = jnp.einsum('bhid,bhjd->bhij', q, k) * dh ** (-0.5)
        p1 = (x @ W1p).reshape(B, T, H, 4)
        p2 = (x @ W2p).reshape(B, T, H, 4)
        lines_h = jnp.transpose(plucker_lines(p1, p2), (0, 2, 1, 3))
        Jlines = lines_h @ _J6.T
        plucker_bias = jnp.einsum('bhic,bhjc->bhij', lines_h, Jlines)
        logits = std_logits + plucker_bias * plucker_scale[None, :, None, None]
        causal = jnp.triu(jnp.ones((T, T), bool), 1)
        logits = jnp.where(causal[None, None], -jnp.inf, logits)
        attn = jax.nn.softmax(logits, axis=-1)
        out = jnp.einsum('bhij,bhjd->bhid', attn, v)
        out = jnp.transpose(out, (0, 2, 1, 3)).reshape(B, T, D)
        return out @ Wout + bout

    def _L0_ffn_ref(hidden_states, gate_w, w13_weight, w2_weight):
        import jax, jax.numpy as jnp
        import numpy as np
        N_EXPERTS = 8
        N_GROUP = 4
        TOPK_GROUP = 2
        TOP_K = 2
        HIDDEN = 128
        INTER = 256
        B, S = (1, 128)

        def _grouped_topk(scores):
            T, E = scores.shape
            per_group = E // N_GROUP
            group_scores = scores.reshape(T, N_GROUP, per_group).max(-1)
            _, gidx = jax.lax.top_k(group_scores, TOPK_GROUP)
            gmask = jnp.zeros((T, N_GROUP), scores.dtype).at[jnp.arange(T)[:, None], gidx].set(1.0)
            smask = jnp.repeat(gmask, per_group, axis=1)
            masked = jnp.where(smask > 0, scores, 0.0)
            topk_w, topk_ids = jax.lax.top_k(masked, TOP_K)
            topk_w = topk_w / topk_w.sum(-1, keepdims=True)
            return (topk_ids, topk_w)
        Bm, Sm, H = hidden_states.shape
        x = hidden_states.reshape(-1, H)
        T = x.shape[0]
        scores = jax.nn.softmax(x @ gate_w.T, axis=-1)
        topk_ids, topk_w = _grouped_topk(scores)
        combine = jnp.zeros((T, N_EXPERTS), x.dtype).at[jnp.arange(T)[:, None], topk_ids].add(topk_w)
        gu = jnp.einsum('th,eih->tei', x, w13_weight)
        gate, up = (gu[..., :INTER], gu[..., INTER:])
        act = jax.nn.silu(gate) * up
        act = act * combine[:, :, None]
        out = jnp.einsum('tei,ehi->th', act, w2_weight)
        return out.reshape(Bm, Sm, H)

    def _L1_xattn_ref(query, key, value, W_q, b_q, W_k, b_k, W_v, b_v, W_o, b_o):
        import jax, jax.numpy as jnp
        import numpy as np
        D_MODEL = 128
        NUM_HEADS = 16
        HEAD_DIM = D_MODEL // NUM_HEADS
        B, S, _ = query.shape
        Q = query @ W_q.T + b_q
        K = key @ W_k.T + b_k
        V = value @ W_v.T + b_v

        def split_heads(x):
            return x.reshape(B, -1, NUM_HEADS, HEAD_DIM).transpose(0, 2, 1, 3)
        Qh, Kh, Vh = (split_heads(Q), split_heads(K), split_heads(V))
        scale = 1.0 / jnp.sqrt(jnp.float32(HEAD_DIM))
        scores = jnp.einsum('bhqd,bhkd->bhqk', Qh, Kh) * scale
        attn = jax.nn.softmax(scores, axis=-1)
        out = jnp.einsum('bhqk,bhkd->bhqd', attn, Vh)
        out = out.transpose(0, 2, 1, 3).reshape(B, S, D_MODEL)
        return out @ W_o.T + b_o

    def _L1_attn_ref(x, W1, b1, W2, b2):
        import jax, jax.numpy as jnp
        import numpy as np
        EMBED_DIM = 128
        NUM_HEAD = 16
        NEG_BIG = 10000000000.0
        B, S, E = x.shape
        H = NUM_HEAD
        y = jnp.einsum('bse,ef->bsf', x, W1) + b1
        y = y.reshape(B, S, H, -1).transpose(0, 2, 1, 3)
        q, k, v = jnp.split(y, 3, axis=-1)
        dk = jnp.asarray(v.shape[-1], x.dtype) ** 0.5
        w = jnp.einsum('bhqd,bhkd->bhqk', q, k) / dk
        mask = jnp.tril(jnp.ones((S, S), dtype=x.dtype))
        w = w * mask - NEG_BIG * (1.0 - mask)
        w = jax.nn.softmax(w, axis=-1)
        attn = jnp.einsum('bhqk,bhkd->bhqd', w, v)
        attn = attn.transpose(0, 2, 1, 3).reshape(B, S, E)
        return jnp.einsum('bse,ef->bsf', attn, W2) + b2

    def _L1_ffn_ref(x, W_router, b_router, W1, b1, W2, b2):
        import jax, jax.numpy as jnp
        import numpy as np
        N_EMBD = 128
        NUM_EXPERTS = 8
        TOP_K = 2
        D_FF = 4 * N_EMBD
        B, S = (4, 256)
        Bv, Sv, D = x.shape
        flat_x = x.reshape(-1, D)
        T = flat_x.shape[0]
        logits = flat_x @ W_router + b_router
        top_vals, top_idx = jax.lax.top_k(logits, TOP_K)
        neg_inf = jnp.full_like(logits, -jnp.inf)
        sparse_logits = neg_inf.at[jnp.arange(T)[:, None], top_idx].set(top_vals)
        router_weights = jax.nn.softmax(sparse_logits, axis=-1)
        final_output = jnp.zeros_like(flat_x)
        for e in range(NUM_EXPERTS):
            expert_mask = jnp.any(top_idx == e, axis=-1)
            h = jax.nn.relu(flat_x @ W1[e] + b1[e])
            y = h @ W2[e] + b2[e]
            w = router_weights[:, e] * expert_mask.astype(x.dtype)
            final_output = final_output + y * w[:, None]
        return final_output.reshape(Bv, Sv, D)
    x = x + _L0_xattn_ref(_layernorm(x, axis=-1), ctx_1024, ctx_1024, mask_Bx1xSxS2_ik1, L0_xattn_Wq, L0_xattn_bq, L0_xattn_Wk, L0_xattn_bk, L0_xattn_Wv, L0_xattn_bv, L0_xattn_Wo, L0_xattn_bo)
    x = x + _L0_attn_ref(_layernorm(x, axis=-1), L0_attn_Wqkv, L0_attn_bqkv, L0_attn_W1p, L0_attn_W2p, L0_attn_plucker_scale, L0_attn_Wout, L0_attn_bout)
    x = x + _L0_ffn_ref(_layernorm(x, axis=-1), L0_ffn_gate_w, L0_ffn_w13_weight, L0_ffn_w2_weight)
    x = x + _L1_xattn_ref(_layernorm(x, axis=-1), ctx_1024, ctx_1024, L1_xattn_W_q, L1_xattn_b_q, L1_xattn_W_k, L1_xattn_b_k, L1_xattn_W_v, L1_xattn_b_v, L1_xattn_W_o, L1_xattn_b_o)
    x = x + _L1_attn_ref(_layernorm(x, axis=-1), L1_attn_W1, L1_attn_b1, L1_attn_W2, L1_attn_b2)
    x = x + _L1_ffn_ref(_layernorm(x, axis=-1), L1_ffn_W_router, L1_ffn_b_router, L1_ffn_W1, L1_ffn_b1, L1_ffn_W2, L1_ffn_b2)
    return x

_drawn_inputs = setup_inputs


def setup_inputs(seed=0):
    import zlib

    import numpy as np

    out = dict(_drawn_inputs(seed))
    spreads = {'L0_attn_bqkv': (0.0, 0.1),
     'L0_attn_plucker_scale': (0.10000000149011612, 0.6),
     'L0_attn_bout': (0.0, 0.1),
     'L1_xattn_b_q': (0.0, 0.287),
     'L1_xattn_b_k': (0.0, 2.0),
     'L1_xattn_b_v': (0.0, 0.1),
     'L1_xattn_b_o': (0.0, 0.1),
     'L1_ffn_b_router': (0.0, 0.1),
     'L1_ffn_b1': (0.0, 0.1),
     'L1_ffn_b2': (0.0, 0.1)}
    factors = {'L0_xattn_bk': 64.0,
     'L0_attn_W1p': 2.845,
     'L0_attn_W2p': 3.042,
     'L0_ffn_gate_w': 4.391,
     'L0_ffn_w13_weight': 4.776,
     'L0_ffn_w2_weight': 4.055}
    for name, (base, spread) in spreads.items():
        noise = np.random.default_rng([zlib.crc32(name.encode()), seed]).standard_normal(out[name].shape)
        drawn = base * np.exp(spread * noise) if base else spread * noise
        out[name] = jnp.asarray(drawn.astype(out[name].dtype))
    for name, factor in factors.items():
        out[name] = (out[name] * factor).astype(out[name].dtype)
    return out
```

```python
from contextlib import ExitStack

import concourse.bass as bass
from concourse import mybir

F32 = mybir.dt.float32
I32 = mybir.dt.int32
ALU = mybir.AluOpType
ACT = mybir.ActivationFunctionType
X = mybir.AxisListType.X

B, S, SK, D = 64, 32, 257, 128
H, DH = 16, 8
GB = 4
NG = B // GB
J = 4
NGR = H // J
U = GB * NGR
KM = 256
E_N = 8
F0, F1 = 256, 512
EPS = 1e-5
BIG = 1e9
LOWEST = 3.0e38
STREAMS = 1

CONST = {}
_at = 0
for _n, _w in (("ident", 128), ("head_q", 4), ("head_qn", 4), ("quad", 4), ("fold", 32), ("causal0", 32),
               ("tril", 32), ("causal1", 32), ("order8", 128), ("order4", 32), ("tail_block", 512),
               ("jmat", 96), ("head_p", 4), ("group_p", 4), ("half", 1), ("mhalf", 1), ("eps", 1)):
    CONST[_n] = (_at, _at + _w)
    _at += _w
NCONST = _at

BCOL = {n: k for k, n in enumerate(("bq0", "bk0", "bv0", "bq1", "bk1", "bv1",
                                    "sq0", "sk0", "sv0", "sq1", "sk1", "sv1", "plucker"))}
NBCOL = len(BCOL) + 4 * E_N
BROW = {"o0": 0, "so0": 128, "o1": 256, "so1": 384, "router": 512}
NBROW = 520


def stream_steps(s):
    out = [("mask", s, 0, 0)]
    out += [("kproj", s, l, c) for l in range(2) for c in range(2)]
    out += [("vproj", s, 0, c) for c in range(4)]
    out += [("kvtail", s, 0, 0)]
    for l in range(2):
        out += [("ln", s, l, 0), ("lnT", s, l, 0), ("qproj", s, l, 0)]
        lead = 4
        for w in range(U // 2 + 3):
            if w < U // 2:
                out += [("scores", s, l, 2 * w), ("scores", s, l, 2 * w + 1)]
            if 1 <= w <= U // 2:
                out += [("ptrans", s, l, w - 1)]
            if 2 <= w <= U // 2 + 1:
                out += [("pv", s, l, w - 2)]
            if w == U // 2:
                out += [("tailT", s, l, 0)]
        out += [("tailV", s, l, 0), ("norm", s, l, 0), ("oT", s, l, 0), ("oproj", s, l, 0)]
        out += [("ln", s, l, 1), ("lnT", s, l, 1), ("qk", s, l, 0), ("vrep", s, l, 0)]
        if l == 0:
            out += [("lines", s, l, 0), ("linesT", s, l, 0), ("jlines", s, l, 0)]
        out += [("sscore", s, l, 0), ("sptrans", s, l, 0), ("spv", s, l, 0),
                ("norm", s, l, 1), ("oT", s, l, 1), ("oproj", s, l, 1)]
        out += [("ln", s, l, 2), ("lnT", s, l, 2), ("route", s, l, 0)]
        for e in range(E_N + 1):
            if e < E_N:
                out += [("up", s, l, e)]
            if e:
                out += [("down", s, l, e - 1)]
        if l == 1:
            out += [("wT", s, l, 0), ("wb2", s, l, 0)]
    out += [("store", s, 0, 0)]
    return out


FILLS = ("kproj", "vproj", "kvtail", "lnT", "qproj", "scores", "ptrans", "tailT", "oT", "oproj", "qk", "vrep",
         "lines", "linesT", "jlines", "sscore", "sptrans", "route", "up", "down", "wT", "wb2")


def build_order():
    lists = [stream_steps(s) for s in range(STREAMS)]
    if STREAMS == 1:
        return lists[0]
    return merge(lists)


def merge(lists):
    out = []
    n = max(len(x) for x in lists)
    for k in range(n):
        for x in lists:
            if k < len(x):
                out.append(x[k])
    return out



WCOL = {}
_at = 0
for _n, _w in (("q0", 128), ("k0", 128), ("q1", 128), ("k1", 128), ("v01", 256), ("o0", 128), ("o1", 128),
               ("sq0", 128), ("sk0", 128), ("sv0", 128), ("so0", 128), ("sq1", 128), ("sk1", 128), ("sv1", 128),
               ("so1", 128), ("p4", 384), ("gate0", 8), ("gate1", 8)):
    WCOL[_n] = (_at, _at + _w)
    _at += _w
WSQ = _at
SETUP_LOADS = 5
EXPERT_LOADS = 4


def perceiver(nc, x_d, ctx_d, mask_d, wsq_d, w13_d, w2a_d, w1_d, w2b_d, const_d, bcol_d, brow_d, b2_d, out_d):
    order = build_order()
    turns = NG // STREAMS
    ring = 8 - STREAMS
    bank_of = {}
    before = {}
    last = [None] * ring
    fills = [step for step in order if step[0] in FILLS]
    for n, step in enumerate(fills):
        bank_of[step] = n % ring
        before[step] = last[n % ring]
        last[n % ring] = step

    with ExitStack() as ctx:
        def sb(name, shape, dt=F32):
            return ctx.enter_context(nc.sbuf_tensor(name, shape, dt))

        def each(name, shape, dt=F32):
            return [sb(f"{name}{s}", shape, dt) for s in range(STREAMS)]

        def sem(name):
            return ctx.enter_context(nc.semaphore(name))

        def sems(name):
            return [sem(f"{name}{s}") for s in range(STREAMS)]

        bank = [ctx.enter_context(nc.psum_tensor(f"bank{k}", [128, 512], F32)) for k in range(ring)]
        attn_out = [ctx.enter_context(nc.psum_tensor(f"attn_out{s}", [128, 512], F32)) for s in range(STREAMS)]

        cst = sb("cst", [128, NCONST])
        bcol = sb("bcol", [128, NBCOL])
        brow = sb("brow", [128, NBROW])
        wsq = sb("wsq", [128, WSQ])
        w13 = sb("w13", [128, E_N, 512])
        w2a = sb("w2a", [128, E_N, 2, 128])
        w1 = sb("w1", [128, E_N, 512])
        w2b = sb("w2b", [128, E_N, 4, 128])
        b2 = sb("b2", [E_N, 128])
        jscaled = sb("jscaled", [96, 96])

        def c(name, rows=128):
            a, b = CONST[name]
            return cst[0:rows, a:b]

        def w(name):
            a, b = WCOL[name]
            return wsq[:, a:b]

        def bc(name, rows=128):
            return bcol[0:rows, BCOL[name]:BCOL[name] + 1]

        ident = c("ident")

        xin = each("xin", [128, D])
        ctxT = each("ctxT", [128, GB * KM + GB + U])
        maskb = each("maskb", [128, GB, SK], I32)
        xs = each("xs", [128, D])
        xpb = each("xpb", [128, D])
        mbias = each("mbias", [128, GB, SK])
        mmin = each("mmin", [128, GB])
        mscale = each("mscale", [128, GB])
        KT = each("KT", [128, 2, GB, SK])
        V = each("V", [128, 2 * GB, 2, 128])
        vtl = each("vtl", [U, 2, 128])
        vtb = each("vtb", [U, 2, 512])
        st6 = each("st6", [128, 6])
        mv = each("mv", [128, 2])
        veps = each("veps", [128, 1])
        rstd = each("rstd", [128, 1])
        xn = each("xn", [128, D])
        xnT = each("xnT", [128, D])
        xnR = each("xnR", [128, GB, NGR, S])
        qs = each("qs", [128, 256])
        BQ = each("BQ", [128, GB, J, S])
        KB = each("KB", [128, GB, NGR, S])
        VB = each("VB", [128, GB, NGR, 32])
        P = each("P", [128, U, SK])
        nmax = each("nmax", [128, U])
        sums = each("sums", [128, U])
        rsum = each("rsum", [128, U])
        wsel = each("wsel", [128, U, J])
        PT = each("PT", [128, 2, 512])
        tT = each("tT", [U, 128])
        On = each("On", [128, 512])
        OT = each("OT", [128, 128])
        sS = each("sS", [128, U, S])
        sP = each("sP", [128, U, S])
        p4 = each("p4", [128, 4, 96])
        pa = each("pa", [128, 96])
        pb = each("pb", [128, 96])
        ln6 = each("ln6", [128, 96])
        lsq = each("lsq", [128, 96])
        lss = each("lss", [128, H])
        lnn = each("lnn", [128, H])
        lrn = each("lrn", [128, H])
        lT = each("lT", [96, 128])
        LQ = each("LQ", [96, GB, J, S])
        LK = each("LK", [96, GB, NGR, S])
        sc = each("sc", [128, E_N])
        sc2 = each("sc2", [128, E_N])
        col = each("col", [128, 4])
        gs = each("gs", [128, 4])
        cmp8 = each("cmp8", [128, E_N, 2, E_N])
        rank = each("rank", [128, E_N])
        comb = each("comb", [128, E_N])
        comT = each("comT", [E_N, 128])
        th = each("th", [128, 2, 256])
        HT = each("HT", [128, 2, 512])

        constants_in, experts_in, jscaled_done = sem("constants_in"), sem("experts_in"), sem("jscaled_done")
        dve_took, pool_took = sem("dve_took"), sem("pool_took")
        sums_done = sems("sums_done")
        x_in, ctx_in, mask_in, x_out = sems("x_in"), sems("ctx_in"), sems("mask_in"), sems("x_out")
        mask_bias, mask_min, mask_scale = sems("mask_bias"), sems("mask_min"), sems("mask_scale")
        kT_done, v_done, kvtail_done, vtail_done = sems("kT_done"), sems("v_done"), sems("kvtail_done"), sems("vtail_done")
        stats_done, mean_done, eps_done, rstd_done = sems("stats_done"), sems("mean_done"), sems("eps_done"), sems("rstd_done")
        xn_done, xnT_done, xnR_done = sems("xn_done"), sems("xnT_done"), sems("xnR_done")
        q_done, qk_done, bq_done, kb_done, vb_done = sems("q_done"), sems("qk_done"), sems("bq_done"), sems("kb_done"), sems("vb_done")
        max_done, exp_done = sems("max_done"), sems("exp_done")
        pt_act, pt_vec, pv_done, tail_done = sems("pt_act"), sems("pt_vec"), sems("pv_done"), sems("tail_done")
        attn_done, rsum_done, wsel_done, on_done, oT_done = (
            sems("attn_done"), sems("rsum_done"), sems("wsel_done"), sems("on_done"), sems("oT_done"))
        x_done, xpb_done = sems("x_done"), sems("xpb_done")
        p4_done, lines_step, lss_done, lrn_done, lT_done, lq_done = (
            sems("p4_done"), sems("lines_step"), sems("lss_done"), sems("lrn_done"), sems("lT_done"), sems("lq_done"))
        soft, sexp_done, spt_done = sems("softmax_step"), sems("sexp_done"), sems("spt_done")
        route_step, gate_exp, comb_done, comT_done = sems("route_step"), sems("gate_exp"), sems("comb_done"), sems("comT_done")
        th_done, t_done, h_vec, h_act = sems("th_done"), sems("t_done"), sems("h_vec"), sems("h_act")
        bank_full = [sem(f"bank_full{k}") for k in range(ring)]

        block = ctx.enter_context(nc.Block())

        def at(i, l, n, k):
            return i * (2 * n) + (l * n + k)

        def wait(eng, semaphore, value):
            if not (isinstance(value, int) and value <= 0):
                eng.wait_ge(semaphore, value)

        def fill_count(step):
            n = fills.index(step)
            return n // ring + 1, (len(fills) - 1 - n % ring) // ring + 1

        def wait_full(eng, i, step):
            k, n = fill_count(step)
            eng.wait_ge(bank_full[bank_of[step]], i * n + k)

        def read(step):
            kind, s, l, m = step
            return {
                "kproj": (kT_done[s], 4, 2 * l + m + 1), "vproj": (v_done[s], 4, m + 1),
                "kvtail": (kvtail_done[s], 3, 3), "lnT": (xnT_done[s], 6, 3 * l + m + 1),
                "qproj": (q_done[s], 2, l + 1),
                "scores": (max_done[s], 2 * U, m + 1) if l == 0 else (exp_done[s], 2 * U, U + m + 1),
                "ptrans": (pt_act[s] if m % 2 else pt_vec[s], U // 2, l * U // 4 + m // 2 + 1),
                "tailT": (tail_done[s], 2, l + 1), "oT": (oT_done[s], 4, 2 * l + m + 1),
                "oproj": (x_done[s], 21, 10 * l + m + 1), "qk": (qk_done[s], 2, l + 1),
                "vrep": (vb_done[s], 2, l + 1), "lines": (p4_done[s], 1, 1), "linesT": (lT_done[s], 1, 1),
                "jlines": (lq_done[s], 2, 2), "sscore": (soft[s], 7, 1 + 3 * l),
                "sptrans": (spt_done[s], 2, l + 1), "route": (route_step[s], ROUTE_N, 1 + l * ROUTE_0),
                "up": ((h_vec[s], 12, m + 1) if l == 0 else (h_act[s], 4, m // 2 + 1) if m % 2 else
                       (h_vec[s], 12, 8 + m // 2 + 1)),
                "down": (x_done[s], 21, 10 * l + 3 + m), "wT": (comT_done[s], 1, 1), "wb2": (x_done[s], 21, 21),
            }[kind]

        def pt_ready(i, s, l, m):
            semaphore, n, k = read(("ptrans", s, l, m))
            return semaphore, i * n + k

        def wait_empty(eng, i, step):
            if before[step] is not None:
                semaphore, n, k = read(before[step])
                eng.wait_ge(semaphore, i * n + k)
            else:
                semaphore, n, k = read(last[bank_of[step]])
                wait(eng, semaphore, i * n)

        @block.sync
        def _(sp):
            for dst, src in ((cst[:, :], const_d), (bcol[:, :], bcol_d), (brow[:, :], brow_d), (wsq[:, :], wsq_d),
                             (b2[:, :], b2_d)):
                sp.dma_start(dst, src).then_inc(constants_in, 16)

            def load(i):
                for s in range(STREAMS):
                    wait(sp, xpb_done[s], i * 4)
                    sp.dma_start(xin[s][:, :], x_d[i * STREAMS + s]).then_inc(x_in[s], 16)
                    wait(sp, kvtail_done[s], i * 3)
                    wait(sp, v_done[s], i * 4)
                    wait(sp, kT_done[s], i * 4)
                    sp.dma_start(ctxT[s][:, :], ctx_d[i * STREAMS + s]).then_inc(ctx_in[s], 16)
                    wait(sp, mask_bias[s], i)
                    for j in range(J):
                        sp.dma_start(maskb[s][32 * j:32 * j + 32, :, :],
                                     mask_d[i * STREAMS + s].rearrange("b q k -> q b k")).then_inc(mask_in[s], 16)

            load(0)
            for dst, src in ((w13[:, :, :], w13_d), (w2a[:, :, :, :], w2a_d), (w1[:, :, :], w1_d),
                             (w2b[:, :, :, :], w2b_d)):
                sp.dma_start(dst, src).then_inc(experts_in, 16)

            def store(i):
                for s in range(STREAMS):
                    sp.wait_ge(x_done[s], i * 21 + 21)
                    sp.dma_start(out_d[i * STREAMS + s], xs[s][:, :]).then_inc(x_out[s], 16)

            with sp.Fori(1, turns) as i:
                load(i)
                store(i - 1)
            store(turns - 1)
            for s in range(STREAMS):
                sp.wait_ge(x_out[s], turns * 16)

        @block.gpsimd
        def _(pool):
            pool.wait_ge(constants_in, 16 * SETUP_LOADS)
            nc.gpsimd.tensor_scalar(jscaled[:, :], c("jmat", 96), bc("plucker", 96), None,
                                    ALU.mult).then_inc(jscaled_done, 1)

            def taken():
                pool.sem_inc(pool_took, 1)

            def turn(i):
                for kind, s, l, m in order:
                    if kind == "mask":
                        pool.wait_ge(mask_in[s], i * 64 + 64)
                        wait(pool, max_done[s], i * (2 * U))
                        taken()
                        nc.gpsimd.tensor_scalar(mbias[s][:, :, :], maskb[s][:, :, :], 0, BIG, ALU.is_equal,
                                                ALU.mult).then_inc(mask_bias[s], 1)
                    elif kind == "ln":
                        pool.wait_ge(mean_done[s], at(i, l, 3, m + 1))
                        nc.gpsimd.tensor_tensor(veps[s][:, :], mv[s][:, 1:2], c("eps"), ALU.add).then_inc(eps_done[s], 1)
                        pool.wait_ge(eps_done[s], at(i, l, 3, m + 1))
                        nc.gpsimd.tensor_tensor(rstd[s][:, :], veps[s][:, :], c("mhalf"),
                                                ALU.pow).then_inc(rstd_done[s], 1)
                        if m < 2:
                            src = xin[s] if (l, m) == (0, 0) else xs[s]
                            row = BROW[("o" if m == 0 else "so") + str(l)]
                            nc.gpsimd.tensor_tensor(xpb[s][:, :], src[:, :], brow[:, row:row + D],
                                                    ALU.add).then_inc(xpb_done[s], 1)
                    elif kind == "lnT" and m == 1:
                        pool.wait_ge(xnT_done[s], at(i, l, 3, 2))
                        taken()
                        nc.gpsimd.tensor_copy(xnR[s][:, :, :, :],
                                              xnT[s][:, :].rearrange("p (b s) -> p b s", b=GB).unsqueeze(2)
                                              .broadcast_to((128, GB, NGR, S))).then_inc(xnR_done[s], 1)
                    elif kind == "lines":
                        pool.wait_ge(p4_done[s], i + 1)
                        nc.gpsimd.tensor_tensor(pa[s][:, :], p4[s][:, 0, :], p4[s][:, 1, :],
                                                ALU.mult).then_inc(lines_step[s], 1)
                        nc.gpsimd.tensor_tensor(pb[s][:, :], p4[s][:, 2, :], p4[s][:, 3, :],
                                                ALU.mult).then_inc(lines_step[s], 1)
                        pool.wait_ge(lines_step[s], i * 6 + 2)
                        nc.gpsimd.tensor_tensor(ln6[s][:, :], pa[s][:, :], pb[s][:, :],
                                                ALU.subtract).then_inc(lines_step[s], 1)
                        pool.wait_ge(lines_step[s], i * 6 + 3)
                        nc.gpsimd.tensor_tensor(lsq[s][:, :], ln6[s][:, :], ln6[s][:, :],
                                                ALU.mult).then_inc(lines_step[s], 1)
                        pool.wait_ge(lss_done[s], i + 1)
                        nc.gpsimd.tensor_tensor(lnn[s][:, :], lss[s][:, :], c("half").broadcast_to((128, H)),
                                                ALU.pow).then_inc(lines_step[s], 1)
                        pool.wait_ge(lrn_done[s], i * 2 + 2)
                        nc.gpsimd.tensor_tensor(pa[s][:, :].rearrange("p (h c) -> p h c", c=6),
                                                ln6[s][:, :].rearrange("p (h c) -> p h c", c=6),
                                                lrn[s][:, :].unsqueeze(2).broadcast_to((128, H, 6)),
                                                ALU.mult).then_inc(lines_step[s], 1)

            turn(0)
            with pool.Fori(1, turns) as i:
                turn(i)

        @block.tensor
        def _(pe):
            pe.wait_ge(constants_in, 16 * SETUP_LOADS)
            pe.wait_ge(jscaled_done, 1)

            def turn(i):
                for step in order:
                    kind, s, l, m = step
                    if kind in FILLS:
                        ps = bank[bank_of[step]]
                        wait_empty(pe, i, step)
                        full = bank_full[bank_of[step]]
                    if kind == "kproj":
                        pe.wait_ge(ctx_in[s], i * 16 + 16)
                        nc.tensor.matmul(ps[:, :], w(f"k{l}"), ctxT[s][:, m * 512:m * 512 + 512],
                                         start=True, stop=True).then_inc(full, 1)
                    elif kind == "vproj":
                        for k in range(2):
                            a = (2 * m + k) * 128
                            ins = nc.tensor.matmul(ps[:, k * 256:k * 256 + 256], ctxT[s][:, a:a + 128], w("v01"),
                                                   start=True, stop=True)
                        ins.then_inc(full, 1)
                    elif kind == "kvtail":
                        t = GB * KM
                        nc.tensor.matmul(ps[:, 0:4], w("k0"), ctxT[s][:, t:t + GB], start=True, stop=True)
                        nc.tensor.matmul(ps[:, 4:8], w("k1"), ctxT[s][:, t:t + GB], start=True, stop=True)
                        nc.tensor.matmul(ps[0:U, 16:16 + 256], ctxT[s][:, t + GB:t + GB + U], w("v01"),
                                         start=True, stop=True).then_inc(full, 1)
                    elif kind == "lnT":
                        pe.wait_ge(xn_done[s], at(i, l, 3, m + 1))
                        nc.tensor.transpose(ps[:, 0:128], xn[s][:, :], ident).then_inc(full, 1)
                    elif kind == "qproj":
                        pe.wait_ge(xnT_done[s], at(i, l, 3, 1))
                        nc.tensor.matmul(ps[:, 0:128], w(f"q{l}"), xnT[s][:, :], start=True,
                                         stop=True).then_inc(full, 1)
                    elif kind == "scores":
                        b, g = divmod(m, NGR)
                        if m == 0:
                            pe.wait_ge(bq_done[s], at(i, l, 2, 1))
                            pe.wait_ge(kT_done[s], i * 4 + 4)
                            pe.wait_ge(kvtail_done[s], i * 3 + 3)
                        a = 32 * g
                        nc.tensor.matmul(ps[:, 0:SK], BQ[s][a:a + 32, b, :, :], KT[s][a:a + 32, l, b, :],
                                         start=True, stop=True).then_inc(full, 1)
                    elif kind == "ptrans":
                        pe.wait_ge(exp_done[s], at(i, l, U, 2 * m + 2))
                        for k in range(4):
                            ins = nc.tensor.transpose(
                                ps[:, k * 128:k * 128 + 128],
                                P[s][:, 2 * m + k // 2, (k % 2) * 128:(k % 2) * 128 + 128], ident)
                        ins.then_inc(full, 1)
                    elif kind == "pv":
                        pe.wait_ge(*pt_ready(i, s, l, m))
                        if m == 0:
                            wait(pe, on_done[s], at(i, l, 2, 0))
                            pe.wait_ge(v_done[s], i * 4 + 4)
                        for k in range(4):
                            u = 2 * m + k // 2
                            b, g = divmod(u, NGR)
                            ins = nc.tensor.matmul(attn_out[s][:, u * 32:u * 32 + 32],
                                                   PT[s][:, m % 2, k * 128:k * 128 + 128],
                                                   V[s][:, 2 * b + k % 2, l, 32 * g:32 * g + 32],
                                                   start=(m == 0 and k == 0), stop=False, skip_group_check=True)
                        ins.then_inc(pv_done[s], 1)
                    elif kind == "tailT":
                        pe.wait_ge(exp_done[s], at(i, l, U, U))
                        nc.tensor.transpose(ps[0:U, 0:128], P[s][:, :, KM], ident).then_inc(full, 1)
                    elif kind == "tailV":
                        pe.wait_ge(tail_done[s], at(i, l, 1, 1))
                        pe.wait_ge(vtail_done[s], i + 1)
                        nc.tensor.matmul(attn_out[s][:, :], tT[s][:, :], vtb[s][:, l, :], start=False, stop=True,
                                         skip_group_check=True).then_inc(attn_done[s], 1)
                    elif kind == "oT":
                        pe.wait_ge(on_done[s], at(i, l, 2, m + 1))
                        for b in range(GB):
                            ins = nc.tensor.matmul(ps[:, 32 * b:32 * b + 32], On[s][:, 128 * b:128 * b + 128],
                                                   c("fold"), start=True, stop=True)
                        ins.then_inc(full, 1)
                    elif kind == "oproj":
                        pe.wait_ge(oT_done[s], at(i, l, 2, m + 1))
                        nc.tensor.matmul(ps[:, 0:128], OT[s][:, :], w(f"{'o' if m == 0 else 'so'}{l}"),
                                         start=True, stop=True).then_inc(full, 1)
                    elif kind == "qk":
                        pe.wait_ge(xnT_done[s], at(i, l, 3, 2))
                        nc.tensor.matmul(ps[:, 0:128], w(f"sq{l}"), xnT[s][:, :], start=True, stop=True)
                        nc.tensor.matmul(ps[:, 128:256], w(f"sk{l}"), xnT[s][:, :], start=True,
                                         stop=True).then_inc(full, 1)
                    elif kind == "vrep":
                        pe.wait_ge(xnR_done[s], at(i, l, 1, 1))
                        for b in range(GB):
                            ins = nc.tensor.matmul(ps[:, 128 * b:128 * b + 128], xnR[s][:, b, :, :], w(f"sv{l}"),
                                                   start=True, stop=True)
                        ins.then_inc(full, 1)
                    elif kind == "lines":
                        pe.wait_ge(xnT_done[s], at(i, l, 3, 2))
                        nc.tensor.matmul(ps[:, 0:384], xnT[s][:, :], w("p4"), start=True,
                                         stop=True).then_inc(full, 1)
                    elif kind == "linesT":
                        pe.wait_ge(lines_step[s], i * 6 + 6)
                        nc.tensor.transpose(ps[0:96, 0:128], pa[s][:, :], ident).then_inc(full, 1)
                    elif kind == "jlines":
                        pe.wait_ge(lT_done[s], i + 1)
                        nc.tensor.matmul(ps[0:96, 0:128], jscaled[:, :], lT[s][:, :], start=True,
                                         stop=True).then_inc(full, 1)
                    elif kind == "sscore":
                        pe.wait_ge(bq_done[s], at(i, l, 2, 2))
                        pe.wait_ge(kb_done[s], at(i, l, 1, 1))
                        if l == 0:
                            pe.wait_ge(lq_done[s], i * 2 + 2)
                        for b in range(GB):
                            o = ps[:, 128 * b:128 * b + 128]
                            ins = nc.tensor.matmul(o, BQ[s][:, b, :, :], KB[s][:, b, :, :], start=True, stop=(l == 1))
                            if l == 0:
                                ins = nc.tensor.matmul(o, LQ[s][:, b, :, :], LK[s][:, b, :, :], start=False,
                                                       stop=True)
                        ins.then_inc(full, 1)
                    elif kind == "sptrans":
                        pe.wait_ge(sexp_done[s], at(i, l, 1, 1))
                        for b in range(GB):
                            ins = nc.tensor.transpose(ps[:, 128 * b:128 * b + 128], sP[s][:, 4 * b:4 * b + 4, :],
                                                      ident)
                        ins.then_inc(full, 1)
                    elif kind == "spv":
                        pe.wait_ge(spt_done[s], at(i, l, 1, 1))
                        pe.wait_ge(vb_done[s], at(i, l, 1, 1))
                        pe.wait_ge(on_done[s], at(i, l, 2, 1))
                        for b in range(GB):
                            ins = nc.tensor.matmul(attn_out[s][:, 128 * b:128 * b + 128], sS[s][:, 4 * b:4 * b + 4, :],
                                                   VB[s][:, b, :, :], start=True, stop=True)
                        ins.then_inc(attn_done[s], 1)
                    elif kind == "route":
                        pe.wait_ge(xnT_done[s], at(i, l, 3, 3))
                        nc.tensor.matmul(ps[:, 0:E_N], xnT[s][:, :], w(f"gate{l}"), start=True,
                                         stop=True).then_inc(full, 1)
                    elif kind == "up":
                        if isinstance(i, int) and m == 0:
                            pe.wait_ge(experts_in, 16 * EXPERT_LOADS)
                        wt = w13 if l == 0 else w1
                        for k in range(4):
                            ins = nc.tensor.matmul(ps[:, k * 128:k * 128 + 128], wt[:, m, k * 128:k * 128 + 128],
                                                   xnT[s][:, :], start=True, stop=True)
                        ins.then_inc(full, 1)
                    elif kind == "down":
                        wt, nk = (w2a, 2) if l == 0 else (w2b, 4)
                        semaphore, n, k = read(("up", s, l, m))
                        pe.wait_ge(semaphore, i * n + k)
                        for k in range(nk):
                            ins = nc.tensor.matmul(ps[:, 0:128], HT[s][:, m % 2, k * 128:k * 128 + 128],
                                                   wt[:, m, k, :], start=(k == 0), stop=(k == nk - 1))
                        ins.then_inc(full, 1)
                    elif kind == "wT":
                        pe.wait_ge(comb_done[s], at(i, 1, 1, 1))
                        nc.tensor.transpose(ps[0:E_N, 0:128], comb[s][:, :], ident).then_inc(full, 1)
                    elif kind == "wb2":
                        pe.wait_ge(comT_done[s], i + 1)
                        nc.tensor.matmul(ps[:, 0:128], comT[s][:, :], b2[:, :], start=True,
                                         stop=True).then_inc(full, 1)

            turn(0)
            with pe.Fori(1, turns) as i:
                turn(i)

        @block.scalar
        def _(act):
            act.wait_ge(constants_in, 16 * SETUP_LOADS)

            def turn(i):
                for step in order:
                    kind, s, l, m = step
                    if kind in FILLS:
                        ps = bank[bank_of[step]]
                    if kind == "kproj":
                        wait_full(act, i, step)
                        nc.scalar.activation(KT[s][:, l, 2 * m:2 * m + 2, 0:KM],
                                             ps[:, :].rearrange("p (b k) -> p b k", b=2), ACT.Identity,
                                             bias=bc(f"bk{l}")).then_inc(kT_done[s], 1)
                    elif kind == "lnT":
                        wait_full(act, i, step)
                        nc.scalar.copy(xnT[s][:, :], ps[:, 0:128]).then_inc(xnT_done[s], 1)
                    elif kind == "qproj":
                        wait_full(act, i, step)
                        nc.scalar.activation(qs[s][:, 0:128], ps[:, 0:128], ACT.Identity,
                                             bias=bc(f"bq{l}")).then_inc(q_done[s], 1)
                    elif kind == "scores":
                        act.wait_ge(max_done[s], at(i, l, U, m + 1))
                        if l == 0:
                            nc.scalar.activation(P[s][:, m, :], P[s][:, m, :], ACT.Exp, bias=nmax[s][:, m:m + 1],
                                                 scale=-1.0, accum_out=sums[s][:, m:m + 1]).then_inc(exp_done[s], 1)
                        else:
                            nc.scalar.activation(P[s][:, m, :], ps[:, 0:SK], ACT.Exp, bias=nmax[s][:, m:m + 1],
                                                 accum_out=sums[s][:, m:m + 1]).then_inc(exp_done[s], 1)
                    elif kind == "ptrans" and m % 2:
                        wait_full(act, i, step)
                        if m >= 2:
                            act.wait_ge(pv_done[s], at(i, l, U // 2, m - 1))
                        nc.scalar.copy(PT[s][:, 1, :], ps[:, :]).then_inc(pt_act[s], 1)
                    elif kind == "tailT":
                        wait_full(act, i, step)
                        nc.scalar.copy(tT[s][:, :], ps[0:U, 0:128]).then_inc(tail_done[s], 1)
                    elif kind == "oT":
                        wait_full(act, i, step)
                        nc.scalar.activation(OT[s][:, :], ps[:, 0:128], ACT.Identity,
                                             bias=bc(f"{'b' if m == 0 else 's'}v{l}")).then_inc(oT_done[s], 1)
                    elif kind == "qk":
                        wait_full(act, i, step)
                        nc.scalar.activation(qs[s][:, 0:128], ps[:, 0:128], ACT.Identity, bias=bc(f"sq{l}"))
                        nc.scalar.activation(qs[s][:, 128:256], ps[:, 128:256], ACT.Identity,
                                             bias=bc(f"sk{l}")).then_inc(qk_done[s], 1)
                    elif kind == "lines":
                        wait_full(act, i, step)
                        nc.scalar.copy(p4[s][:, :, :], ps[:, 0:384]).then_inc(p4_done[s], 1)
                    elif kind == "linesT":
                        wait_full(act, i, step)
                        nc.scalar.copy(lT[s][:, :], ps[0:96, 0:128]).then_inc(lT_done[s], 1)
                    elif kind == "sscore":
                        act.wait_ge(soft[s], i * 7 + 3 + 4 * l)
                        nc.scalar.activation(sP[s][:, :, :], sS[s][:, :, :], ACT.Exp).then_inc(sexp_done[s], 1)
                    elif kind == "sptrans":
                        wait_full(act, i, step)
                        nc.scalar.copy(sS[s][:, :, :], ps[:, :]).then_inc(spt_done[s], 1)
                    elif kind == "route":
                        act.wait_ge(route_step[s], i * ROUTE_N + (1 if l == 0 else ROUTE_0 + 2))
                        src = ps[:, 0:E_N] if l == 0 else sc[s][:, :]
                        nc.scalar.activation(sc2[s][:, :], src, ACT.Exp,
                                             bias=col[s][:, 0:1]).then_inc(gate_exp[s], 1)
                    elif kind == "up":
                        wait_full(act, i, step)
                        if l == 0:
                            if m >= 2:
                                act.wait_ge(t_done[s], i * 8 + m - 1)
                            nc.scalar.activation(th[s][:, m % 2, :], ps[:, 0:256], ACT.Tanh,
                                                 scale=0.5).then_inc(th_done[s], 1)
                        elif m % 2:
                            if m >= 2:
                                act.wait_ge(x_done[s], i * 21 + 13 + m - 2)
                            for k in range(4):
                                n = len(BCOL) + 4 * m + k
                                ins = nc.scalar.activation(HT[s][:, 1, k * 128:k * 128 + 128],
                                                           ps[:, k * 128:k * 128 + 128], ACT.Relu,
                                                           bias=bcol[:, n:n + 1])
                            ins.then_inc(h_act[s], 1)
                    elif kind == "wT":
                        wait_full(act, i, step)
                        nc.scalar.copy(comT[s][:, :], ps[0:E_N, 0:128]).then_inc(comT_done[s], 1)

            turn(0)
            with act.Fori(1, turns) as i:
                turn(i)

        @block.vector
        def _(dve):
            dve.wait_ge(constants_in, 16 * SETUP_LOADS)

            def taken():
                dve.sem_inc(dve_took, 1)

            def ranks(i, s, start, src, n, const):
                a = src.unsqueeze(1).broadcast_to((128, n, n))
                b = src.unsqueeze(2).broadcast_to((128, n, n))
                cm = cmp8[s][:, 0:n, :, 0:n]
                nc.vector.tensor_tensor(cm[:, :, 0, :], a, b, ALU.is_ge)
                nc.vector.tensor_tensor(cm[:, :, 1, :], a, b, ALU.is_gt).then_inc(route_step[s], 1)
                dve.wait_ge(route_step[s], start + 1)
                nc.vector.tensor_tensor(cm, cm, c(const).rearrange("p (e a f) -> p e a f", e=n, a=2),
                                        ALU.mult).then_inc(route_step[s], 1)
                dve.wait_ge(route_step[s], start + 2)
                nc.vector.tensor_reduce(rank[s][:, 0:n], cm, mybir.AxisListType.XY, ALU.add).then_inc(route_step[s], 1)
                dve.wait_ge(route_step[s], start + 3)

            def turn(i):
                for step in order:
                    kind, s, l, m = step
                    if kind in FILLS:
                        ps = bank[bank_of[step]]
                    if kind == "mask":
                        dve.wait_ge(mask_bias[s], i + 1)
                        nc.vector.tensor_reduce(mmin[s][:, :], mbias[s][:, :, :], X, ALU.min).then_inc(mask_min[s], 1)
                        dve.wait_ge(mask_min[s], i + 1)
                        nc.vector.tensor_scalar(mscale[s][:, :], mmin[s][:, :], 1.0, 1.0, ALU.is_lt,
                                                ALU.add).then_inc(mask_scale[s], 1)
                    elif kind == "vproj":
                        wait_full(dve, i, step)
                        nc.vector.tensor_copy(V[s][:, 2 * m:2 * m + 2, :, :], ps[:, :]).then_inc(v_done[s], 1)
                    elif kind == "kvtail":
                        wait_full(dve, i, step)
                        for k in range(2):
                            nc.vector.tensor_scalar(KT[s][:, k, :, KM], ps[:, 4 * k:4 * k + 4], bc(f"bk{k}"), None,
                                                    ALU.add).then_inc(kvtail_done[s], 1)
                        nc.vector.tensor_copy(vtl[s][:, :, :], ps[0:U, 16:272]).then_inc(kvtail_done[s], 1)
                        dve.wait_ge(kvtail_done[s], i * 3 + 3)
                        for k in range(2):
                            ins = nc.vector.tensor_tensor(
                                vtb[s][:, k, :].rearrange("p (b f) -> p b f", b=GB),
                                vtl[s][:, k, :].unsqueeze(1).broadcast_to((U, GB, 128)),
                                c("tail_block", U).rearrange("p (b f) -> p b f", b=GB), ALU.mult)
                        ins.then_inc(vtail_done[s], 1)
                    elif kind == "ln":
                        src = xin[s] if (l, m) == (0, 0) else xs[s]
                        if (l, m) == (0, 0):
                            dve.wait_ge(x_in[s], i * 16 + 16)
                        else:
                            dve.wait_ge(x_done[s], i * 21 + (10 * l + m))
                        nc.vector.bn_stats(st6[s][:, :], src[:, :]).then_inc(stats_done[s], 1)
                        dve.wait_ge(stats_done[s], at(i, l, 3, m + 1))
                        taken()
                        nc.vector.bn_aggr(mv[s][:, :], st6[s][:, :]).then_inc(mean_done[s], 1)
                    elif kind == "lnT":
                        src = xin[s] if (l, m) == (0, 0) else xs[s]
                        dve.wait_ge(rstd_done[s], at(i, l, 3, m + 1))
                        nc.vector.tensor_scalar(xn[s][:, :], src[:, :], mv[s][:, 0:1], rstd[s][:, 0:1], ALU.subtract,
                                                ALU.mult).then_inc(xn_done[s], 1)
                    elif kind == "qproj" or kind == "qk":
                        cross = kind == "qproj"
                        dve.wait_ge(*((q_done[s], at(i, l, 1, 1)) if cross else (qk_done[s], at(i, l, 1, 1))))
                        hq = c("head_qn" if cross and l == 0 else "head_q")
                        nc.vector.tensor_tensor(
                            BQ[s][:, :, :, :],
                            qs[s][:, 0:128].rearrange("p (b s) -> p b s", b=GB).unsqueeze(2).broadcast_to((128, GB, J, S)),
                            hq.unsqueeze(1).unsqueeze(3).broadcast_to((128, GB, J, S)),
                            ALU.mult).then_inc(bq_done[s], 1)
                        if not cross:
                            nc.vector.tensor_tensor(
                                KB[s][:, :, :, :],
                                qs[s][:, 128:256].rearrange("p (b s) -> p b s", b=GB).unsqueeze(2)
                                .broadcast_to((128, GB, NGR, S)),
                                c("quad").unsqueeze(1).unsqueeze(3).broadcast_to((128, GB, NGR, S)),
                                ALU.mult).then_inc(kb_done[s], 1)
                    elif kind == "scores":
                        wait_full(dve, i, step)
                        if l == 0:
                            if m == 0:
                                dve.wait_ge(mask_scale[s], i + 1)
                            taken()
                            b = m // NGR
                            nc.vector.tensor_tensor_reduce(P[s][:, m, :], ps[:, 0:SK], mbias[s][:, b, :],
                                                           mscale[s][:, b:b + 1], LOWEST, ALU.add, ALU.min,
                                                           nmax[s][:, m:m + 1]).then_inc(max_done[s], 1)
                        else:
                            nc.vector.tensor_reduce(nmax[s][:, m:m + 1], ps[:, 0:SK], X, ALU.max,
                                                    negate=True).then_inc(max_done[s], 1)
                    elif kind == "ptrans" and m % 2 == 0:
                        wait_full(dve, i, step)
                        if m >= 2:
                            dve.wait_ge(pv_done[s], at(i, l, U // 2, m - 1))
                        nc.vector.tensor_copy(PT[s][:, 0, :], ps[:, :]).then_inc(pt_vec[s], 1)
                    elif kind == "norm":
                        if m == 0:
                            dve.wait_ge(exp_done[s], at(i, l, U, U))
                        else:
                            dve.wait_ge(soft[s], i * 7 + 3 + 4 * l)
                        if m == 1:
                            dve.wait_ge(sexp_done[s], at(i, l, 1, 1))
                            nc.vector.tensor_reduce(sums[s][:, :], sP[s][:, :, :], X, ALU.add).then_inc(sums_done[s], 1)
                            dve.wait_ge(sums_done[s], at(i, l, 1, 1))
                        nc.vector.reciprocal(rsum[s][:, :], sums[s][:, :]).then_inc(rsum_done[s], 1)
                        dve.wait_ge(rsum_done[s], at(i, l, 2, m + 1))
                        nc.vector.tensor_tensor(wsel[s][:, :, :], rsum[s][:, :].unsqueeze(2).broadcast_to((128, U, J)),
                                                c("quad").unsqueeze(1).broadcast_to((128, U, J)),
                                                ALU.mult).then_inc(wsel_done[s], 1)
                        dve.wait_ge(wsel_done[s], at(i, l, 2, m + 1))
                        dve.wait_ge(attn_done[s], at(i, l, 2, m + 1))
                        nc.vector.tensor_tensor(On[s][:, :].rearrange("p (u d) -> p u d", d=DH),
                                                attn_out[s][:, :].rearrange("p (u d) -> p u d", d=DH),
                                                wsel[s][:, :, :].rearrange("p u j -> p (u j)").unsqueeze(2)
                                                .broadcast_to((128, U * J, DH)), ALU.mult).then_inc(on_done[s], 1)
                    elif kind == "oproj":
                        wait_full(dve, i, step)
                        dve.wait_ge(xpb_done[s], at(i, l, 2, m + 1))
                        if (l, m) == (0, 0):
                            wait(dve, x_out[s], i * 16)
                        nc.vector.tensor_tensor(xs[s][:, :], ps[:, 0:128], xpb[s][:, :], ALU.add).then_inc(x_done[s], 1)
                    elif kind == "vrep":
                        wait_full(dve, i, step)
                        nc.vector.tensor_tensor(VB[s][:, :, :, :], ps[:, :].rearrange("p (b g f) -> p b g f", b=GB, g=NGR),
                                                c("quad").unsqueeze(1).unsqueeze(3).broadcast_to((128, GB, NGR, 32)),
                                                ALU.mult).then_inc(vb_done[s], 1)
                    elif kind == "lines":
                        dve.wait_ge(lines_step[s], i * 6 + 4)
                        nc.vector.tensor_reduce(lss[s][:, :], lsq[s][:, :].rearrange("p (h c) -> p h c", c=6), X,
                                                ALU.add).then_inc(lss_done[s], 1)
                        dve.wait_ge(lines_step[s], i * 6 + 5)
                        nc.vector.tensor_scalar(lnn[s][:, :], lnn[s][:, :], 1e-12, None, ALU.max).then_inc(lrn_done[s], 1)
                        dve.wait_ge(lrn_done[s], i * 2 + 1)
                        nc.vector.reciprocal(lrn[s][:, :], lnn[s][:, :]).then_inc(lrn_done[s], 1)
                    elif kind == "linesT":
                        dve.wait_ge(lT_done[s], i + 1)
                        nc.vector.tensor_tensor(
                            LQ[s][:, :, :, :],
                            lT[s][:, :].rearrange("p (b s) -> p b s", b=GB).unsqueeze(2).broadcast_to((96, GB, J, S)),
                            c("head_p", 96).unsqueeze(1).unsqueeze(3).broadcast_to((96, GB, J, S)),
                            ALU.mult).then_inc(lq_done[s], 1)
                    elif kind == "jlines":
                        wait_full(dve, i, step)
                        nc.vector.tensor_tensor(
                            LK[s][:, :, :, :],
                            ps[0:96, 0:128].rearrange("p (b s) -> p b s", b=GB).unsqueeze(2)
                            .broadcast_to((96, GB, NGR, S)),
                            c("group_p", 96).unsqueeze(1).unsqueeze(3).broadcast_to((96, GB, NGR, S)),
                            ALU.mult).then_inc(lq_done[s], 1)
                    elif kind == "sscore":
                        wait_full(dve, i, step)
                        p3 = ps[:, :].rearrange("p (u k) -> p u k", k=S)
                        base = i * 7 + 3 * l
                        if l == 0:
                            nc.vector.tensor_tensor(sS[s][:, :, :], p3,
                                                    c("causal0").unsqueeze(1).broadcast_to((128, U, S)),
                                                    ALU.add).then_inc(soft[s], 1)
                        else:
                            nc.vector.tensor_tensor(sS[s][:, :, :], p3,
                                                    c("tril").unsqueeze(1).broadcast_to((128, U, S)),
                                                    ALU.mult).then_inc(soft[s], 1)
                            dve.wait_ge(soft[s], base + 1)
                            nc.vector.tensor_tensor(sS[s][:, :, :], sS[s][:, :, :],
                                                    c("causal1").unsqueeze(1).broadcast_to((128, U, S)),
                                                    ALU.add).then_inc(soft[s], 1)
                        dve.wait_ge(soft[s], base + 1 + l)
                        nc.vector.tensor_reduce(nmax[s][:, :], sS[s][:, :, :], X, ALU.max).then_inc(soft[s], 1)
                        dve.wait_ge(soft[s], base + 2 + l)
                        nc.vector.tensor_tensor(sS[s][:, :, :], sS[s][:, :, :],
                                                nmax[s][:, :].unsqueeze(2).broadcast_to((128, U, S)),
                                                ALU.subtract).then_inc(soft[s], 1)
                    elif kind == "route":
                        wait_full(dve, i, step)
                        base = i * ROUTE_N + l * ROUTE_0
                        if l == 0:
                            nc.vector.tensor_reduce(col[s][:, 0:1], ps[:, 0:E_N], X, ALU.max,
                                                    negate=True).then_inc(route_step[s], 1)
                            dve.wait_ge(gate_exp[s], at(i, l, 1, 1))
                            nc.vector.tensor_reduce(col[s][:, 1:2], sc2[s][:, :], X, ALU.add).then_inc(route_step[s], 1)
                            dve.wait_ge(route_step[s], base + 2)
                            nc.vector.reciprocal(col[s][:, 2:3], col[s][:, 1:2]).then_inc(route_step[s], 1)
                            dve.wait_ge(route_step[s], base + 3)
                            nc.vector.tensor_scalar(sc[s][:, :], sc2[s][:, :], col[s][:, 2:3], None,
                                                    ALU.mult).then_inc(route_step[s], 1)
                            dve.wait_ge(route_step[s], base + 4)
                            nc.vector.tensor_reduce(gs[s][:, :], sc[s][:, :].rearrange("p (g e) -> p g e", e=2), X,
                                                    ALU.max).then_inc(route_step[s], 1)
                            dve.wait_ge(route_step[s], base + 5)
                            ranks(i, s, base + 5, gs[s][:, :], 4, "order4")
                            nc.vector.tensor_scalar(gs[s][:, :], rank[s][:, 0:4], 2.0, None,
                                                    ALU.is_lt).then_inc(route_step[s], 1)
                            dve.wait_ge(route_step[s], base + 9)
                            nc.vector.tensor_tensor(sc[s][:, :].rearrange("p (g e) -> p g e", e=2),
                                                    sc[s][:, :].rearrange("p (g e) -> p g e", e=2),
                                                    gs[s][:, :].unsqueeze(2).broadcast_to((128, 4, 2)),
                                                    ALU.mult).then_inc(route_step[s], 1)
                            dve.wait_ge(route_step[s], base + 10)
                            ranks(i, s, base + 10, sc[s][:, :], E_N, "order8")
                            nxt = base + 13
                            weights = sc[s]
                        else:
                            nc.vector.tensor_tensor(sc[s][:, :], ps[:, 0:E_N],
                                                    brow[:, BROW["router"]:BROW["router"] + E_N],
                                                    ALU.add).then_inc(route_step[s], 1)
                            dve.wait_ge(route_step[s], base + 1)
                            nc.vector.tensor_reduce(col[s][:, 0:1], sc[s][:, :], X, ALU.max,
                                                    negate=True).then_inc(route_step[s], 1)
                            ranks(i, s, base + 2, sc[s][:, :], E_N, "order8")
                            dve.wait_ge(gate_exp[s], at(i, l, 1, 1))
                            nxt = base + 5
                            weights = sc2[s]
                        nc.vector.tensor_scalar(rank[s][:, :], rank[s][:, :], 2.0, None,
                                                ALU.is_lt).then_inc(route_step[s], 1)
                        dve.wait_ge(route_step[s], nxt + 1)
                        nc.vector.tensor_tensor(rank[s][:, :], rank[s][:, :], weights[:, :],
                                                ALU.mult).then_inc(route_step[s], 1)
                        dve.wait_ge(route_step[s], nxt + 2)
                        nc.vector.tensor_reduce(col[s][:, 1:2], rank[s][:, :], X, ALU.add).then_inc(route_step[s], 1)
                        dve.wait_ge(route_step[s], nxt + 3)
                        nc.vector.reciprocal(col[s][:, 2:3], col[s][:, 1:2]).then_inc(route_step[s], 1)
                        dve.wait_ge(route_step[s], nxt + 4)
                        nc.vector.tensor_scalar(comb[s][:, :], rank[s][:, :], col[s][:, 2:3], 0.5 if l == 0 else 1.0,
                                                ALU.mult, ALU.mult).then_inc(comb_done[s], 1)
                    elif kind == "up":
                        if l == 0:
                            dve.wait_ge(th_done[s], i * 8 + m + 1)
                            h = HT[s][:, m % 2, 0:256]
                            if m >= 2:
                                dve.wait_ge(x_done[s], i * 21 + 3 + m - 2)
                            nc.vector.scalar_tensor_tensor(h, th[s][:, m % 2, :], 1.0, ps[:, 0:256], ALU.add,
                                                           ALU.mult).then_inc(t_done[s], 1)
                            dve.wait_ge(t_done[s], i * 8 + m + 1)
                            nc.vector.tensor_tensor(h, h, ps[:, 256:512], ALU.mult).then_inc(h_vec[s], 1)
                        elif m % 2 == 0:
                            wait_full(dve, i, step)
                            if m >= 2:
                                dve.wait_ge(x_done[s], i * 21 + 13 + m - 2)
                            for k in range(4):
                                n = len(BCOL) + 4 * m + k
                                ins = nc.vector.tensor_scalar(HT[s][:, 0, k * 128:k * 128 + 128],
                                                              ps[:, k * 128:k * 128 + 128], bcol[:, n:n + 1], 0.0,
                                                              ALU.add, ALU.max)
                            ins.then_inc(h_vec[s], 1)
                    elif kind == "down":
                        wait_full(dve, i, step)
                        if m == 0:
                            dve.wait_ge(comb_done[s], at(i, l, 1, 1))
                        dve.wait_ge(x_done[s], i * 21 + 10 * l + 2 + m)
                        nc.vector.scalar_tensor_tensor(xs[s][:, :], ps[:, 0:128], comb[s][:, m:m + 1], xs[s][:, :],
                                                       ALU.mult, ALU.add).then_inc(x_done[s], 1)
                    elif kind == "wb2":
                        wait_full(dve, i, step)
                        dve.wait_ge(x_done[s], i * 21 + 20)
                        nc.vector.tensor_tensor(xs[s][:, :], ps[:, 0:128], xs[s][:, :], ALU.add).then_inc(x_done[s], 1)

            turn(0)
            with dve.Fori(1, turns) as i:
                turn(i)


ROUTE_0, ROUTE_N = 17, 17 + 9


def constants():
    import numpy as np
    k = np.zeros((128, NCONST), np.float32)
    p = np.arange(128)

    def put(name, value):
        a, b = CONST[name]
        value = np.asarray(value, np.float32)
        k[0:value.shape[0], a:b] = value.reshape(value.shape[0], -1)

    put("ident", np.eye(128))
    own = ((p % 32)[:, None] // DH == np.arange(J)) / np.sqrt(np.float32(DH))
    put("head_q", own)
    put("head_qn", -own)
    put("quad", p[:, None] // 32 == np.arange(4))
    put("fold", p[:, None] % 32 == np.arange(32))
    tril = (np.arange(S)[None, :] <= (p % 32)[:, None]).astype(np.float32)
    put("tril", tril)
    put("causal0", (tril - 1.0) * np.float32(LOWEST))
    put("causal1", (tril - 1.0) * np.float32(1e10))
    for name, n in (("order8", E_N), ("order4", 4)):
        e, f = np.arange(n)[:, None], np.arange(n)[None, :]
        put(name, np.broadcast_to(np.stack([f < e, f > e], 1).reshape(1, -1), (128, 2 * n * n)))
    put("tail_block", np.arange(U)[:, None] == np.arange(512)[None, :] // 32)
    j6 = np.array([[0, 0, 0, 0, 0, 1], [0, 0, 0, 0, -1, 0], [0, 0, 0, 1, 0, 0], [0, 0, 1, 0, 0, 0],
                   [0, -1, 0, 0, 0, 0], [1, 0, 0, 0, 0, 0]], np.float32)
    put("jmat", np.kron(np.eye(H), j6.T))
    q = np.arange(96)
    put("head_p", (q % 24)[:, None] // 6 == np.arange(J))
    put("group_p", q[:, None] // 24 == np.arange(NGR))
    put("half", np.full((128, 1), 0.5))
    put("mhalf", np.full((128, 1), -0.5))
    put("eps", np.full((128, 1), EPS))
    return k


def kernel(**inputs):
    import numpy as np
    import concourse.bacc as bacc
    from concourse.bass_utils import run_bass_kernel_spmd

    a = {n: np.asarray(v) for n, v in inputs.items()}
    pi, pj = np.array([0, 0, 0, 1, 1, 2]), np.array([1, 2, 3, 2, 3, 3])
    head = np.arange(H)[:, None] * 3 * DH + np.arange(DH)
    part = [(head + k * DH).reshape(-1) for k in range(3)]
    w1a, b1a = a["L1_attn_W1"], a["L1_attn_b1"]
    wqkv, bqkv = a["L0_attn_Wqkv"], a["L0_attn_bqkv"]
    four = np.arange(H)[:, None] * 4
    p4 = [a[n][:, (four + k).reshape(-1)] for n, k in (("L0_attn_W1p", pi), ("L0_attn_W2p", pj), ("L0_attn_W1p", pj),
                                                      ("L0_attn_W2p", pi))]
    wsq = np.concatenate(
        [a["L0_xattn_Wq"].T, a["L0_xattn_Wk"].T, a["L1_xattn_W_q"].T, a["L1_xattn_W_k"].T, a["L0_xattn_Wv"].T,
         a["L1_xattn_W_v"].T, a["L0_xattn_Wo"].T, a["L1_xattn_W_o"].T,
         wqkv[:, 0:128], wqkv[:, 128:256], wqkv[:, 256:384], a["L0_attn_Wout"],
         w1a[:, part[0]], w1a[:, part[1]], w1a[:, part[2]], a["L1_attn_W2"], *p4, a["L0_ffn_gate_w"].T,
         a["L1_ffn_W_router"]], 1)
    bcol = np.concatenate(
        [np.stack([a["L0_xattn_bq"], a["L0_xattn_bk"], a["L0_xattn_bv"], a["L1_xattn_b_q"], a["L1_xattn_b_k"],
                   a["L1_xattn_b_v"], bqkv[0:128], bqkv[128:256], bqkv[256:384],
                   b1a[part[0]], b1a[part[1]], b1a[part[2]],
                   np.resize(np.repeat(a["L0_attn_plucker_scale"], 6), 128)], 1),
         a["L1_ffn_b1"].reshape(4 * E_N, 128).T], 1)
    brow = np.broadcast_to(np.concatenate([a["L0_xattn_bo"], a["L0_attn_bout"], a["L1_xattn_b_o"], a["L1_attn_b2"],
                                           a["L1_ffn_b_router"]])[None, :], (128, NBROW))
    cx = a["ctx_1024"].reshape(NG, GB, SK, D)
    tail = cx[:, :, KM, :].transpose(0, 2, 1)
    ctx = np.concatenate([cx[:, :, :KM, :].transpose(0, 3, 1, 2).reshape(NG, D, GB * KM), tail,
                          np.repeat(tail, NGR, axis=2)], 2)
    arrays = {
        "x": a["x"].reshape(NG, GB * S, D), "ctx": ctx, "mask": a["mask_Bx1xSxS2_ik1"].reshape(NG, GB, S, SK),
        "wsq": wsq,
        "w13": a["L0_ffn_w13_weight"].transpose(2, 0, 1),
        "w2a": a["L0_ffn_w2_weight"].reshape(E_N, D, 2, 128).transpose(3, 0, 2, 1),
        "w1": a["L1_ffn_W1"].transpose(1, 0, 2),
        "w2b": a["L1_ffn_W2"].reshape(E_N, 4, 128, D).transpose(2, 0, 1, 3),
        "const": constants(), "bcol": bcol, "brow": brow, "b2": a["L1_ffn_b2"],
    }
    arrays = {n: np.ascontiguousarray(v) for n, v in arrays.items()}
    nc = bacc.Bacc("TRN2", target_bir_lowering=False, num_devices=1)
    aps = [nc.dram_tensor(f"{n}_in", v.shape, mybir.dt.from_np(v.dtype), kind="ExternalInput").ap() for n, v in arrays.items()]
    out = nc.dram_tensor("out", (NG, GB * S, D), F32, kind="ExternalOutput").ap()
    perceiver(nc, *aps, out)
    r = run_bass_kernel_spmd(nc, [{f"{n}_in": v for n, v in arrays.items()}], core_ids=[0])
    return r.results[0]["out"].reshape(B, S, D)
```

```python
from contextlib import ExitStack

import concourse.bass as bass
from concourse import mybir

F32 = mybir.dt.float32
I32 = mybir.dt.int32
ALU = mybir.AluOpType
ACT = mybir.ActivationFunctionType
X = mybir.AxisListType.X

B, S, SK, D = 64, 32, 257, 128
H, DH = 16, 8
GB = 4
NG = B // GB
J = 4
NGR = H // J
U = GB * NGR
KM = 256
E_N = 8
F0, F1 = 256, 512
EPS = 1e-5
BIG = 1e9
LOWEST = 3.0e38
STREAMS = 2
SLOTS = 4

CONST = {}
_at = 0
for _n, _w in (("ident", 128), ("head_q", 4), ("head_x0", 16), ("head_x1", 16), ("quad", 4), ("fold", 32), ("causal0", 32),
               ("tril", 32), ("causal1", 32), ("order8", 128), ("order4", 32), ("tail_block", 512),
               ("jmat", 96), ("head_p", 4), ("group_p", 4), ("half", 1), ("mhalf", 1), ("eps", 1)):
    CONST[_n] = (_at, _at + _w)
    _at += _w
NCONST = _at

BCOL = {n: k for k, n in enumerate(("bq0", "bk0", "bv0", "bq1", "bk1", "bv1",
                                    "sq0", "sk0", "sv0", "sq1", "sk1", "sv1", "plucker"))}
NBCOL = len(BCOL) + 4 * E_N
BROW = {"o0": 0, "so0": 128, "o1": 256, "so1": 384, "router": 512}
NBROW = 520


def step_parts(kind, l, m):
    return {
        "mask": (("pool", 1.9), ("dve", 1.2)), "kproj": (("pe", .86), ("act", .6)), "vproj": (("pe", .86), ("dve", .65)),
        "kvtail": (("pe", .4), ("dve", 1.7)), "ln": (("dve", .4), ("pool", 1.1)),
        "lnT": (("dve", .3), ("pe", .11), ("act", .2 if m != 1 else .8)),
        "qproj": (("pe", .22), ("act", .3)), "bq": (("pool", .95),), "scores": (("pe", .43), ("dve", .42), ("act", .5)),
        "ptrans": (("pe", .43), ("act", .5) if m % 2 else ("dve", .65)), "pv": (("pe", .86),),
        "tailT": (("pe", .11), ("act", .2)), "tailV": (("pe", .86),),
        "norm": (("dve", .95 if m == 0 else 1.6),), "oT": (("pe", .43), ("act", .3)),
        "oproj": (("pe", .22), ("dve", .25)), "qk": (("pe", .43), ("act", .55), ("dve", 1.3)),
        "vrep": (("pe", .86), ("dve", .65)), "lines": (("pe", .65), ("act", .4), ("pool", 1.5)),
        "linesN": (("dve", .2), ("pool", 3.0)), "linesU": (("dve", .3), ("pool", .35)),
        "linesT": (("pe", .11), ("act", .2), ("dve", .65)), "jlines": (("pe", .22), ("dve", .65)),
        "sscore": (("pe", .86 * (2 - l)), ("dve", 1.9 + .6 * l), ("act", .55)), "sptrans": (("pe", .43), ("act", .5)),
        "spv": (("pe", .86),), "route": (("pe", .11), ("dve", .2), ("act", .1)), "pick": (("dve", 2.0 - l),),
        "up": ((("pe", .86), ("act", .4), ("dve", .8)) if l == 0 else
               (("pe", .86), ("act", 1.0)) if m % 2 else (("pe", .86), ("dve", 1.05))),
        "down": (("pe", .43 * (l + 1)), ("dve", .3)), "wT": (("pe", .11), ("act", .2)),
        "wb2": (("pe", .22), ("dve", .25)),
    }[kind]


def stream_steps(s):
    needs = {}

    def add(step, *after):
        needs[(step[0], s, *step[1:])] = [(x[0], s, *x[1:]) for x in after]

    add(("mask", 0, 0))
    last = None
    for l in range(2):
        for m in range(2):
            add(("kproj", l, m), *([last] if last else []))
            last = ("kproj", l, m)
    for m in range(4):
        add(("vproj", 0, m), *([("vproj", 0, m - 1)] if m else []))
    add(("kvtail", 0, 0))
    for l in range(2):
        add(("ln", l, 0), *([("down", 0, E_N - 1)] if l else []))
        add(("lnT", l, 0), ("ln", l, 0))
        add(("qproj", l, 0), ("lnT", l, 0))
        for b in range(GB):
            add(("bq", l, b), ("bq", l, b - 1) if b else ("qproj", l, 0),
                *([("scores", l, NGR * (b - 1) - 1)] if b > 1 else []))
        for u in range(U):
            add(("scores", l, u), ("bq", l, u // NGR), *([("scores", l, u - 1)] if u else
                                    [("kproj", l, 1), ("kvtail", 0, 0), ("mask", 0, 0)]))
        for w in range(U // 2):
            add(("ptrans", l, w), ("scores", l, 2 * w + 1), *([("ptrans", l, w - 1)] if w else []),
                *([("pv", l, w - 2)] if w > 1 else []))
            add(("pv", l, w), ("ptrans", l, w), *([("pv", l, w - 1)] if w else [("vproj", 0, 3)]))
        add(("tailT", l, 0), ("scores", l, U - 1))
        add(("tailV", l, 0), ("tailT", l, 0), ("pv", l, U // 2 - 1))
        for m in range(2):
            add(("norm", l, m), ("tailV", l, 0) if m == 0 else ("spv", l, 0))
            add(("oT", l, m), ("norm", l, m))
            add(("oproj", l, m), ("oT", l, m))
            add(("ln", l, m + 1), ("oproj", l, m))
            add(("lnT", l, m + 1), ("ln", l, m + 1))
        add(("qk", l, 0), ("lnT", l, 1))
        add(("vrep", l, 0), ("lnT", l, 1))
        if l == 0:
            for step, before in (("lines", "lnT"), ("linesN", "lines"), ("linesU", "linesN"), ("linesT", "linesU"),
                                 ("jlines", "linesT")):
                add((step, 0, 0), (before, 0, 1 if before == "lnT" else 0))
        add(("sscore", l, 0), ("qk", l, 0), *([("jlines", 0, 0)] if l == 0 else []))
        add(("sptrans", l, 0), ("sscore", l, 0))
        add(("spv", l, 0), ("sptrans", l, 0), ("vrep", l, 0))
        add(("route", l, 0), ("lnT", l, 2))
        add(("pick", l, 0), ("route", l, 0))
        for e in range(E_N):
            add(("up", l, e), *([("up", l, e - 1)] if e else [("lnT", l, 2)]), *([("down", l, e - SLOTS)] if e >= SLOTS else []))
            add(("down", l, e), ("up", l, e), *([("down", l, e - 1)] if e else [("pick", l, 0)]))
    add(("wT", 1, 0), ("pick", 1, 0))
    add(("wb2", 1, 0), ("wT", 1, 0), ("down", 1, E_N - 1))
    return needs


FILLS = ("kproj", "vproj", "kvtail", "lnT", "qproj", "scores", "ptrans", "tailT", "oT", "oproj", "qk", "vrep",
         "lines", "linesT", "jlines", "sscore", "sptrans", "route", "up", "down", "wT", "wb2")


LAG = 20.263
HOP = 0.08


def build_order():
    needs = {}
    for s in range(STREAMS):
        needs |= stream_steps(s)
    took = {x: sum(t + HOP for _, t in step_parts(x[0], x[2], x[3])) for x in needs}
    most = {x: max(t for _, t in step_parts(x[0], x[2], x[3])) for x in needs}
    behind = {}
    follow = {x: [] for x in needs}
    for x, before in needs.items():
        for y in before:
            follow[y].append(x)

    def chain(x):
        if x not in behind:
            behind[x] = took[x] + max((chain(y) - (took[x] - most[x] if y[0] == x[0] else 0.0) for y in follow[x]),
                                      default=0.0)
        return behind[x]

    free_from = {"pe": 0.0, "dve": 0.0, "act": 0.0, "pool": 0.0}
    ends, read, order = {}, [], []
    while len(order) < len(needs):
        best = None
        for x, before in needs.items():
            if x in ends or any(y not in ends for y in before):
                continue
            t = max([ends[y] for y in before if y[0] != x[0]], default=0.0)
            parts = step_parts(x[0], x[2], x[3])
            start = max(t, free_from[parts[0][0]])
            if parts[0][0] != "pe" and "pe" in dict(parts):
                start = max(start + parts[0][1], free_from["pe"])
            if x[0] in FILLS and len(read) >= 8 - STREAMS:
                start = max(start, read[-(8 - STREAMS)])
            late = max(start, free_from["pe"])
            key = (late - EAGER * (chain(x) - LAG * x[1]) - BONUS.get(x[0], 0.0), x[1])
            if best is None or key < best[0]:
                best = (key, x, t)
        _, x, t = best
        for engine, dur in step_parts(x[0], x[2], x[3]):
            t = max(t, free_from[engine])
            if engine == "pe" and x[0] in FILLS and len(read) >= 8 - STREAMS:
                t = max(t, read[-(8 - STREAMS)])
            t += dur
            free_from[engine] = t
            t += HOP
        ends[x] = t
        if x[0] in FILLS:
            read.append(t)
        order.append(x)
    return order


EAGER = 1.2
BONUS = {"up": -2.122, "vproj": 1.037, "ptrans": -0.036, "mask": 3.885, "down": -1.258, "lines": 1.092,
         "norm": 1.747, "pick": 0.297, "qk": -0.857, "kproj": 0.465, "linesN": 1.309, "scores": 0.176,
         "pv": -0.218, "lnT": 0.164, "ln": -0.421, "bq": 1.296, "sscore": -1.699, "vrep": 1.103,
         "route": -0.126}


WCOL = {}
_at = 0
for _n, _w in (("q0", 128), ("k0", 128), ("q1", 128), ("k1", 128), ("v01", 256), ("o0", 128), ("o1", 128),
               ("sq0", 128), ("sk0", 128), ("sv0", 128), ("so0", 128), ("sq1", 128), ("sk1", 128), ("sv1", 128),
               ("so1", 128), ("p4", 384), ("gate0", 8), ("gate1", 8)):
    WCOL[_n] = (_at, _at + _w)
    _at += _w
WSQ = _at
SETUP_LOADS = 5
EXPERT_LOADS = 4


def perceiver(nc, x_d, ctx_d, mask_d, wsq_d, w13_d, w2a_d, w1_d, w2b_d, const_d, bcol_d, brow_d, b2_d, out_d):
    order = build_order()
    turns = NG // STREAMS
    ring = 8 - STREAMS
    bank_of = {}
    before = {}
    last = [None] * ring
    fills = [step for step in order if step[0] in FILLS]
    for n, step in enumerate(fills):
        bank_of[step] = n % ring
        before[step] = last[n % ring]
        last[n % ring] = step

    with ExitStack() as ctx:
        def sb(name, shape, dt=F32):
            return ctx.enter_context(nc.sbuf_tensor(name, shape, dt))

        def each(name, shape, dt=F32):
            return [sb(f"{name}{s}", shape, dt) for s in range(STREAMS)]

        def sem(name):
            return ctx.enter_context(nc.semaphore(name))

        def sems(name):
            return [sem(f"{name}{s}") for s in range(STREAMS)]

        bank = [ctx.enter_context(nc.psum_tensor(f"bank{k}", [128, 512], F32)) for k in range(ring)]
        attn_out = [ctx.enter_context(nc.psum_tensor(f"attn_out{s}", [128, 512], F32)) for s in range(STREAMS)]

        cst = sb("cst", [128, NCONST])
        bcol = sb("bcol", [128, NBCOL])
        brow = sb("brow", [128, NBROW])
        wsq = sb("wsq", [128, WSQ])
        w13 = sb("w13", [128, E_N, 512])
        w2a = sb("w2a", [128, E_N, 2, 128])
        w1 = sb("w1", [128, E_N, 512])
        w2b = sb("w2b", [128, E_N, 4, 128])
        b2 = sb("b2", [E_N, 128])
        jscaled = sb("jscaled", [96, 96])

        def c(name, rows=128):
            a, b = CONST[name]
            return cst[0:rows, a:b]

        def w(name):
            a, b = WCOL[name]
            return wsq[:, a:b]

        def bc(name, rows=128):
            return bcol[0:rows, BCOL[name]:BCOL[name] + 1]

        ident = c("ident")

        xin = each("xin", [128, D])
        ctxT = each("ctxT", [128, GB * KM + GB + U])
        maskb = each("maskb", [128, GB, SK], I32)
        xs = each("xs", [128, D])
        xpb = each("xpb", [128, D])
        mbias = [t.bitcast(F32) for t in (m[:, :, :] for m in maskb)]
        mmin = each("mmin", [128, GB])
        mscale = each("mscale", [128, GB])
        KT = each("KT", [128, 2, GB, SK])
        V = each("V", [128, 2 * GB, 2, 128])
        vtl = each("vtl", [U, 2, 128])
        vtb = each("vtb", [U, 2, 512])
        st6 = each("st6", [128, 6])
        mv = each("mv", [128, 2])
        veps = each("veps", [128, 1])
        rstd = each("rstd", [128, 1])
        xn = each("xn", [128, D])
        xnT = each("xnT", [128, D])
        qs = each("qs", [128, 256])
        BX = each("BX", [128, 2, H, S])
        BQ = [t[:, 0, :, :].rearrange("p (b j) s -> p b j s", b=GB) for t in BX]
        P = each("P", [128, U, SK])
        def over_weights(s, k, rows, *shape):
            names = "a b c"[:2 * len(shape) - 1]
            sizes = dict(zip(names.split(), shape))
            return (P[s][0:rows, :, :].rearrange("p u k -> p (u k)")[:, 512 * k:512 * k + 512]
                    .rearrange(f"p ({names}) -> p {names}", **sizes))

        xnR = [over_weights(s, 0, 128, GB, NGR, S) for s in range(STREAMS)]
        KB = [over_weights(s, 1, 128, GB, NGR, S) for s in range(STREAMS)]
        VB = [over_weights(s, 2, 128, GB, NGR, 32) for s in range(STREAMS)]
        sS = [over_weights(s, 3, 128, U, S) for s in range(STREAMS)]
        sP = [over_weights(s, 4, 128, U, S) for s in range(STREAMS)]
        LQ = [over_weights(s, 5, 96, GB, J, S) for s in range(STREAMS)]
        LK = [over_weights(s, 6, 96, GB, NGR, S) for s in range(STREAMS)]
        th = [[over_weights(s, 4 + e // 2, 128, 2, 256)[:, e % 2, :] for e in range(SLOTS)] for s in range(STREAMS)]
        HT = [[over_weights(s, e, 128, 1, 512)[:, 0, :] for e in range(SLOTS)] for s in range(STREAMS)]
        nmax = each("nmax", [128, U])
        sums = each("sums", [128, U])
        rsum = each("rsum", [128, U])
        wsel = each("wsel", [128, U, J])
        PT = each("PT", [128, 2, 512])
        tT = each("tT", [U, 128])
        On = each("On", [128, 512])
        OT = each("OT", [128, 128])
        p4 = each("p4", [128, 4, 96])
        pa = each("pa", [128, 96])
        pb = each("pb", [128, 96])
        ln6 = each("ln6", [128, 96])
        lsq = each("lsq", [128, 96])
        lss = each("lss", [128, H])
        lnn = each("lnn", [128, H])
        lrn = each("lrn", [128, H])
        lT = each("lT", [96, 128])
        sc = each("sc", [128, E_N])
        sc2 = each("sc2", [128, E_N])
        col = each("col", [128, 4])
        gs = each("gs", [128, 4])
        cmp8 = each("cmp8", [128, E_N, 2, E_N])
        rank = each("rank", [128, E_N])
        comb = each("comb", [128, E_N])
        comT = each("comT", [E_N, 128])

        constants_in, experts_in, jscaled_done = sem("constants_in"), sem("experts_in"), sem("jscaled_done")
        dve_took, pool_took = sem("dve_took"), sem("pool_took")
        sums_done = sems("sums_done")
        x_in, ctx_in, mask_in, x_out = sems("x_in"), sems("ctx_in"), sems("mask_in"), sems("x_out")
        mask_bias, mask_min, mask_scale = sems("mask_bias"), sems("mask_min"), sems("mask_scale")
        kT_done, v_done, kvtail_done, vtail_done = sems("kT_done"), sems("v_done"), sems("kvtail_done"), sems("vtail_done")
        stats_done, mean_done, eps_done, rstd_done = sems("stats_done"), sems("mean_done"), sems("eps_done"), sems("rstd_done")
        xn_done, xnT_done, xnR_done = sems("xn_done"), sems("xnT_done"), sems("xnR_done")
        q_done, qk_done, bq_done, kb_done, vb_done = sems("q_done"), sems("qk_done"), sems("bq_done"), sems("kb_done"), sems("vb_done")
        bx_done = sems("bx_done")
        max_done, exp_done = sems("max_done"), sems("exp_done")
        pt_act, pt_vec, pv_done, tail_done = sems("pt_act"), sems("pt_vec"), sems("pv_done"), sems("tail_done")
        attn_done, rsum_done, wsel_done, on_done, oT_done = (
            sems("attn_done"), sems("rsum_done"), sems("wsel_done"), sems("on_done"), sems("oT_done"))
        x_done, xpb_done = sems("x_done"), sems("xpb_done")
        p4_done, lines_step, lss_done, lrn_done, lT_done, lq_done = (
            sems("p4_done"), sems("lines_step"), sems("lss_done"), sems("lrn_done"), sems("lT_done"), sems("lq_done"))
        soft, sexp_done, spt_done = sems("softmax_step"), sems("sexp_done"), sems("spt_done")
        route_step, gate_exp, comb_done, comT_done = sems("route_step"), sems("gate_exp"), sems("comb_done"), sems("comT_done")
        th_done, t_done, h_vec, h_act = sems("th_done"), sems("t_done"), sems("h_vec"), sems("h_act")
        bank_full = [sem(f"bank_full{k}") for k in range(ring)]

        block = ctx.enter_context(nc.Block())

        def at(i, l, n, k):
            return i * (2 * n) + (l * n + k)

        def wait(eng, semaphore, value):
            if not (isinstance(value, int) and value <= 0):
                eng.wait_ge(semaphore, value)

        def fill_count(step):
            n = fills.index(step)
            return n // ring + 1, (len(fills) - 1 - n % ring) // ring + 1

        def wait_full(eng, i, step):
            k, n = fill_count(step)
            eng.wait_ge(bank_full[bank_of[step]], i * n + k)

        def read(step):
            kind, s, l, m = step
            return {
                "kproj": (kT_done[s], 4, 2 * l + m + 1), "vproj": (v_done[s], 4, m + 1),
                "kvtail": (kvtail_done[s], 3, 3), "lnT": (xnT_done[s], 6, 3 * l + m + 1) if m != 1 else (xnR_done[s], 2, l + 1),
                "qproj": (q_done[s], 2, l + 1),
                "scores": (max_done[s], 2 * U, m + 1) if l == 0 else (exp_done[s], 2 * U, U + m + 1),
                "ptrans": (pt_act[s] if m % 2 else pt_vec[s], U // 2, l * U // 4 + m // 2 + 1),
                "tailT": (tail_done[s], 2, l + 1), "oT": (oT_done[s], 4, 2 * l + m + 1),
                "oproj": (x_done[s], 21, 10 * l + m + 1), "qk": (qk_done[s], 2, l + 1),
                "vrep": (vb_done[s], 2, l + 1), "lines": (p4_done[s], 1, 1), "linesT": (lT_done[s], 1, 1),
                "jlines": (lq_done[s], 2, 2), "sscore": (soft[s], 7, 1 + 3 * l),
                "sptrans": (spt_done[s], 2, l + 1), "route": (gate_exp[s], 2, l + 1),
                "up": ((h_vec[s], 12, m + 1) if l == 0 else (h_act[s], 4, m // 2 + 1) if m % 2 else
                       (h_vec[s], 12, 8 + m // 2 + 1)),
                "down": (x_done[s], 21, 10 * l + 3 + m), "wT": (comT_done[s], 1, 1), "wb2": (x_done[s], 21, 21),
            }[kind]

        def pt_ready(i, s, l, m):
            semaphore, n, k = read(("ptrans", s, l, m))
            return semaphore, i * n + k

        def wait_empty(eng, i, step):
            if before[step] is not None:
                semaphore, n, k = read(before[step])
                eng.wait_ge(semaphore, i * n + k)
            else:
                semaphore, n, k = read(last[bank_of[step]])
                wait(eng, semaphore, i * n - (n - k))

        @block.sync
        def _(sp):
            for dst, src in ((cst[:, :], const_d), (bcol[:, :], bcol_d), (brow[:, :], brow_d), (wsq[:, :], wsq_d),
                             (b2[:, :], b2_d)):
                sp.dma_start(dst, src).then_inc(constants_in, 16)

            def load(i):
                for s in range(STREAMS):
                    wait(sp, xpb_done[s], i * 4)
                    sp.dma_start(xin[s][:, :], x_d[i * STREAMS + s]).then_inc(x_in[s], 16)
                    wait(sp, kvtail_done[s], i * 3)
                    wait(sp, v_done[s], i * 4)
                    wait(sp, kT_done[s], i * 4)
                    sp.dma_start(ctxT[s][:, :], ctx_d[i * STREAMS + s]).then_inc(ctx_in[s], 16)
                    wait(sp, max_done[s], i * (2 * U) - U)
                    for j in range(J):
                        sp.dma_start(maskb[s][32 * j:32 * j + 32, :, :],
                                     mask_d[i * STREAMS + s].rearrange("b q k -> q b k")).then_inc(mask_in[s], 16)

            load(0)
            for dst, src in ((w13[:, :, :], w13_d), (w2a[:, :, :, :], w2a_d), (w1[:, :, :], w1_d),
                             (w2b[:, :, :, :], w2b_d)):
                sp.dma_start(dst, src).then_inc(experts_in, 16)

            def store(i):
                for s in range(STREAMS):
                    sp.wait_ge(x_done[s], i * 21 + 21)
                    sp.dma_start(out_d[i * STREAMS + s], xs[s][:, :]).then_inc(x_out[s], 16)

            with sp.Fori(1, turns) as i:
                load(i)
                store(i - 1)
            store(turns - 1)
            for s in range(STREAMS):
                sp.wait_ge(x_out[s], turns * 16)

        @block.gpsimd
        def _(pool):
            pool.wait_ge(constants_in, 16 * SETUP_LOADS)
            nc.gpsimd.tensor_scalar(jscaled[:, :], c("jmat", 96), bc("plucker", 96), None,
                                    ALU.mult).then_inc(jscaled_done, 1)

            def taken():
                pool.sem_inc(pool_took, 1)

            def turn(i):
                for kind, s, l, m in order:
                    if kind == "mask":
                        pool.wait_ge(mask_in[s], i * 64 + 64)
                        taken()
                        nc.gpsimd.tensor_scalar(mbias[s], maskb[s][:, :, :], 0, BIG, ALU.is_equal,
                                                ALU.mult).then_inc(mask_bias[s], 1)
                    elif kind == "ln":
                        pool.wait_ge(mean_done[s], at(i, l, 3, m + 1))
                        nc.gpsimd.tensor_tensor(veps[s][:, :], mv[s][:, 1:2], c("eps"), ALU.add).then_inc(eps_done[s], 1)
                        pool.wait_ge(eps_done[s], at(i, l, 3, m + 1))
                        nc.gpsimd.tensor_tensor(rstd[s][:, :], veps[s][:, :], c("mhalf"),
                                                ALU.pow).then_inc(rstd_done[s], 1)
                        if m < 2:
                            src = xin[s] if (l, m) == (0, 0) else xs[s]
                            row = BROW[("o" if m == 0 else "so") + str(l)]
                            nc.gpsimd.tensor_tensor(xpb[s][:, :], src[:, :], brow[:, row:row + D],
                                                    ALU.add).then_inc(xpb_done[s], 1)
                    elif kind == "bq":
                        pool.wait_ge(q_done[s], at(i, l, 1, 1))
                        if m > 1:
                            pool.wait_ge(max_done[s], at(i, l, U, NGR * (m - 1)))
                        nc.gpsimd.tensor_tensor(
                            BX[s][:, m % 2, :, :], qs[s][:, 32 * m:32 * m + 32].unsqueeze(1).broadcast_to((128, H, S)),
                            c(f"head_x{l}").unsqueeze(2).broadcast_to((128, H, S)), ALU.mult).then_inc(bx_done[s], 1)
                    elif kind == "lines":
                        pool.wait_ge(p4_done[s], i + 1)
                        nc.gpsimd.tensor_tensor(pa[s][:, :], p4[s][:, 0, :], p4[s][:, 1, :],
                                                ALU.mult).then_inc(lines_step[s], 1)
                        nc.gpsimd.tensor_tensor(pb[s][:, :], p4[s][:, 2, :], p4[s][:, 3, :],
                                                ALU.mult).then_inc(lines_step[s], 1)
                        pool.wait_ge(lines_step[s], i * 6 + 2)
                        nc.gpsimd.tensor_tensor(ln6[s][:, :], pa[s][:, :], pb[s][:, :],
                                                ALU.subtract).then_inc(lines_step[s], 1)
                        pool.wait_ge(lines_step[s], i * 6 + 3)
                        nc.gpsimd.tensor_tensor(lsq[s][:, :], ln6[s][:, :], ln6[s][:, :],
                                                ALU.mult).then_inc(lines_step[s], 1)
                    elif kind == "linesN":
                        pool.wait_ge(lss_done[s], i + 1)
                        nc.gpsimd.tensor_tensor(lnn[s][:, :], lss[s][:, :], c("half").broadcast_to((128, H)),
                                                ALU.pow).then_inc(lines_step[s], 1)
                    elif kind == "linesU":
                        pool.wait_ge(lrn_done[s], i * 2 + 2)
                        nc.gpsimd.tensor_tensor(pa[s][:, :].rearrange("p (h c) -> p h c", c=6),
                                                ln6[s][:, :].rearrange("p (h c) -> p h c", c=6),
                                                lrn[s][:, :].unsqueeze(2).broadcast_to((128, H, 6)),
                                                ALU.mult).then_inc(lines_step[s], 1)

            turn(0)
            with pool.Fori(1, turns) as i:
                turn(i)

        @block.tensor
        def _(pe):
            pe.wait_ge(constants_in, 16 * SETUP_LOADS)
            pe.wait_ge(jscaled_done, 1)

            def turn(i):
                for step in order:
                    kind, s, l, m = step
                    if kind in FILLS:
                        ps = bank[bank_of[step]]
                        wait_empty(pe, i, step)
                        full = bank_full[bank_of[step]]
                    if kind == "kproj":
                        pe.wait_ge(ctx_in[s], i * 16 + 16)
                        nc.tensor.matmul(ps[:, :], w(f"k{l}"), ctxT[s][:, m * 512:m * 512 + 512],
                                         start=True, stop=True).then_inc(full, 1)
                    elif kind == "vproj":
                        for k in range(2):
                            a = (2 * m + k) * 128
                            ins = nc.tensor.matmul(ps[:, k * 256:k * 256 + 256], ctxT[s][:, a:a + 128], w("v01"),
                                                   start=True, stop=True)
                        ins.then_inc(full, 1)
                    elif kind == "kvtail":
                        t = GB * KM
                        nc.tensor.matmul(ps[:, 0:4], w("k0"), ctxT[s][:, t:t + GB], start=True, stop=True)
                        nc.tensor.matmul(ps[:, 4:8], w("k1"), ctxT[s][:, t:t + GB], start=True, stop=True)
                        nc.tensor.matmul(ps[0:U, 16:16 + 256], ctxT[s][:, t + GB:t + GB + U], w("v01"),
                                         start=True, stop=True).then_inc(full, 1)
                    elif kind == "lnT":
                        pe.wait_ge(xn_done[s], at(i, l, 3, m + 1))
                        nc.tensor.transpose(ps[:, 0:128], xn[s][:, :], ident).then_inc(full, 1)
                    elif kind == "qproj":
                        pe.wait_ge(xnT_done[s], at(i, l, 3, 1))
                        nc.tensor.matmul(ps[:, 0:128], w(f"q{l}"), xnT[s][:, :], start=True,
                                         stop=True).then_inc(full, 1)
                    elif kind == "scores":
                        b, g = divmod(m, NGR)
                        if m == 0:
                            pe.wait_ge(kT_done[s], i * 4 + 2 * l + 2)
                            pe.wait_ge(kvtail_done[s], i * 3 + 3)
                        if g == 0:
                            pe.wait_ge(bx_done[s], at(i, l, GB, b + 1))
                        nc.tensor.matmul(ps[:, 0:SK], BX[s][:, b % 2, J * g:J * g + J, :], KT[s][:, l, b, :],
                                         start=True, stop=True).then_inc(full, 1)
                    elif kind == "ptrans":
                        pe.wait_ge(exp_done[s], at(i, l, U, 2 * m + 2))
                        for k in range(4):
                            ins = nc.tensor.transpose(
                                ps[:, k * 128:k * 128 + 128],
                                P[s][:, 2 * m + k // 2, (k % 2) * 128:(k % 2) * 128 + 128], ident)
                        ins.then_inc(full, 1)
                    elif kind == "pv":
                        pe.wait_ge(*pt_ready(i, s, l, m))
                        if m == 0:
                            wait(pe, on_done[s], at(i, l, 2, 0))
                            pe.wait_ge(v_done[s], i * 4 + 4)
                        for k in range(4):
                            u = 2 * m + k // 2
                            b, g = divmod(u, NGR)
                            ins = nc.tensor.matmul(attn_out[s][:, u * 32:u * 32 + 32],
                                                   PT[s][:, m % 2, k * 128:k * 128 + 128],
                                                   V[s][:, 2 * b + k % 2, l, 32 * g:32 * g + 32],
                                                   start=(m == 0 and k == 0), stop=False, skip_group_check=True)
                        ins.then_inc(pv_done[s], 1)
                    elif kind == "tailT":
                        pe.wait_ge(exp_done[s], at(i, l, U, U))
                        nc.tensor.transpose(ps[0:U, 0:128], P[s][:, :, KM], ident).then_inc(full, 1)
                    elif kind == "tailV":
                        pe.wait_ge(tail_done[s], at(i, l, 1, 1))
                        pe.wait_ge(vtail_done[s], i + 1)
                        nc.tensor.matmul(attn_out[s][:, :], tT[s][:, :], vtb[s][:, l, :], start=False, stop=True,
                                         skip_group_check=True).then_inc(attn_done[s], 1)
                    elif kind == "oT":
                        pe.wait_ge(on_done[s], at(i, l, 2, m + 1))
                        for b in range(GB):
                            ins = nc.tensor.matmul(ps[:, 32 * b:32 * b + 32], On[s][:, 128 * b:128 * b + 128],
                                                   c("fold"), start=True, stop=True)
                        ins.then_inc(full, 1)
                    elif kind == "oproj":
                        pe.wait_ge(oT_done[s], at(i, l, 2, m + 1))
                        nc.tensor.matmul(ps[:, 0:128], OT[s][:, :], w(f"{'o' if m == 0 else 'so'}{l}"),
                                         start=True, stop=True).then_inc(full, 1)
                    elif kind == "qk":
                        pe.wait_ge(xnT_done[s], at(i, l, 3, 2))
                        nc.tensor.matmul(ps[:, 0:128], w(f"sq{l}"), xnT[s][:, :], start=True, stop=True)
                        nc.tensor.matmul(ps[:, 128:256], w(f"sk{l}"), xnT[s][:, :], start=True,
                                         stop=True).then_inc(full, 1)
                    elif kind == "vrep":
                        pe.wait_ge(xnR_done[s], at(i, l, 1, 1))
                        for b in range(GB):
                            ins = nc.tensor.matmul(ps[:, 128 * b:128 * b + 128], xnR[s][:, b, :, :], w(f"sv{l}"),
                                                   start=True, stop=True)
                        ins.then_inc(full, 1)
                    elif kind == "lines":
                        pe.wait_ge(xnT_done[s], at(i, l, 3, 2))
                        nc.tensor.matmul(ps[:, 0:384], xnT[s][:, :], w("p4"), start=True,
                                         stop=True).then_inc(full, 1)
                    elif kind == "linesT":
                        pe.wait_ge(lines_step[s], i * 6 + 6)
                        nc.tensor.transpose(ps[0:96, 0:128], pa[s][:, :], ident).then_inc(full, 1)
                    elif kind == "jlines":
                        pe.wait_ge(lT_done[s], i + 1)
                        nc.tensor.matmul(ps[0:96, 0:128], jscaled[:, :], lT[s][:, :], start=True,
                                         stop=True).then_inc(full, 1)
                    elif kind == "sscore":
                        pe.wait_ge(bq_done[s], at(i, l, 1, 1))
                        pe.wait_ge(kb_done[s], at(i, l, 1, 1))
                        if l == 0:
                            pe.wait_ge(lq_done[s], i * 2 + 2)
                        for b in range(GB):
                            o = ps[:, 128 * b:128 * b + 128]
                            ins = nc.tensor.matmul(o, BQ[s][:, b, :, :], KB[s][:, b, :, :], start=True, stop=(l == 1))
                            if l == 0:
                                ins = nc.tensor.matmul(o, LQ[s][:, b, :, :], LK[s][:, b, :, :], start=False,
                                                       stop=True)
                        ins.then_inc(full, 1)
                    elif kind == "sptrans":
                        pe.wait_ge(sexp_done[s], at(i, l, 1, 1))
                        for b in range(GB):
                            ins = nc.tensor.transpose(ps[:, 128 * b:128 * b + 128], sP[s][:, 4 * b:4 * b + 4, :],
                                                      ident)
                        ins.then_inc(full, 1)
                    elif kind == "spv":
                        pe.wait_ge(spt_done[s], at(i, l, 1, 1))
                        pe.wait_ge(vb_done[s], at(i, l, 1, 1))
                        pe.wait_ge(on_done[s], at(i, l, 2, 1))
                        for b in range(GB):
                            ins = nc.tensor.matmul(attn_out[s][:, 128 * b:128 * b + 128], sS[s][:, 4 * b:4 * b + 4, :],
                                                   VB[s][:, b, :, :], start=True, stop=True)
                        ins.then_inc(attn_done[s], 1)
                    elif kind == "route":
                        pe.wait_ge(xnT_done[s], at(i, l, 3, 3))
                        nc.tensor.matmul(ps[:, 0:E_N], xnT[s][:, :], w(f"gate{l}"), start=True,
                                         stop=True).then_inc(full, 1)
                    elif kind == "up":
                        if m == 0:
                            pe.wait_ge(xnT_done[s], at(i, l, 3, 3))
                        if isinstance(i, int) and m == 0:
                            pe.wait_ge(experts_in, 16 * EXPERT_LOADS)
                        wt = w13 if l == 0 else w1
                        for k in range(4):
                            ins = nc.tensor.matmul(ps[:, k * 128:k * 128 + 128], wt[:, m, k * 128:k * 128 + 128],
                                                   xnT[s][:, :], start=True, stop=True)
                        ins.then_inc(full, 1)
                    elif kind == "down":
                        wt, nk = (w2a, 2) if l == 0 else (w2b, 4)
                        semaphore, n, k = read(("up", s, l, m))
                        pe.wait_ge(semaphore, i * n + k)
                        for k in range(nk):
                            ins = nc.tensor.matmul(ps[:, 0:128], HT[s][m % SLOTS][:, k * 128:k * 128 + 128],
                                                   wt[:, m, k, :], start=(k == 0), stop=(k == nk - 1))
                        ins.then_inc(full, 1)
                    elif kind == "wT":
                        pe.wait_ge(comb_done[s], at(i, 1, 1, 1))
                        nc.tensor.transpose(ps[0:E_N, 0:128], comb[s][:, :], ident).then_inc(full, 1)
                    elif kind == "wb2":
                        pe.wait_ge(comT_done[s], i + 1)
                        nc.tensor.matmul(ps[:, 0:128], comT[s][:, :], b2[:, :], start=True,
                                         stop=True).then_inc(full, 1)

            turn(0)
            with pe.Fori(1, turns) as i:
                turn(i)

        @block.scalar
        def _(act):
            act.wait_ge(constants_in, 16 * SETUP_LOADS)

            def turn(i):
                for step in order:
                    kind, s, l, m = step
                    if kind in FILLS:
                        ps = bank[bank_of[step]]
                    if kind == "kproj":
                        wait_full(act, i, step)
                        nc.scalar.activation(KT[s][:, l, 2 * m:2 * m + 2, 0:KM],
                                             ps[:, :].rearrange("p (b k) -> p b k", b=2), ACT.Identity,
                                             bias=bc(f"bk{l}")).then_inc(kT_done[s], 1)
                    elif kind == "lnT":
                        wait_full(act, i, step)
                        nc.scalar.copy(xnT[s][:, :], ps[:, 0:128]).then_inc(xnT_done[s], 1)
                        if m == 1:
                            nc.scalar.copy(xnR[s], ps[:, 0:128].rearrange("p (b s) -> p b s", b=GB).unsqueeze(2)
                                           .broadcast_to((128, GB, NGR, S))).then_inc(xnR_done[s], 1)
                    elif kind == "qproj":
                        wait_full(act, i, step)
                        nc.scalar.activation(qs[s][:, 0:128], ps[:, 0:128], ACT.Identity,
                                             bias=bc(f"bq{l}")).then_inc(q_done[s], 1)
                    elif kind == "scores":
                        act.wait_ge(max_done[s], at(i, l, U, m + 1))
                        if l == 0:
                            nc.scalar.activation(P[s][:, m, :], P[s][:, m, :], ACT.Exp, bias=nmax[s][:, m:m + 1],
                                                 scale=-1.0, accum_out=sums[s][:, m:m + 1]).then_inc(exp_done[s], 1)
                        else:
                            nc.scalar.activation(P[s][:, m, :], ps[:, 0:SK], ACT.Exp, bias=nmax[s][:, m:m + 1],
                                                 accum_out=sums[s][:, m:m + 1]).then_inc(exp_done[s], 1)
                    elif kind == "ptrans" and m % 2:
                        wait_full(act, i, step)
                        if m >= 2:
                            act.wait_ge(pv_done[s], at(i, l, U // 2, m - 1))
                        nc.scalar.copy(PT[s][:, 1, :], ps[:, :]).then_inc(pt_act[s], 1)
                    elif kind == "tailT":
                        wait_full(act, i, step)
                        nc.scalar.copy(tT[s][:, :], ps[0:U, 0:128]).then_inc(tail_done[s], 1)
                    elif kind == "oT":
                        wait_full(act, i, step)
                        nc.scalar.activation(OT[s][:, :], ps[:, 0:128], ACT.Identity,
                                             bias=bc(f"{'b' if m == 0 else 's'}v{l}")).then_inc(oT_done[s], 1)
                    elif kind == "qk":
                        wait_full(act, i, step)
                        nc.scalar.activation(qs[s][:, 0:128], ps[:, 0:128], ACT.Identity, bias=bc(f"sq{l}"))
                        nc.scalar.activation(qs[s][:, 128:256], ps[:, 128:256], ACT.Identity,
                                             bias=bc(f"sk{l}")).then_inc(qk_done[s], 1)
                    elif kind == "lines":
                        wait_full(act, i, step)
                        nc.scalar.copy(p4[s][:, :, :], ps[:, 0:384]).then_inc(p4_done[s], 1)
                    elif kind == "linesT":
                        wait_full(act, i, step)
                        nc.scalar.copy(lT[s][:, :], ps[0:96, 0:128]).then_inc(lT_done[s], 1)
                    elif kind == "sscore":
                        act.wait_ge(soft[s], i * 7 + 3 + 4 * l)
                        nc.scalar.activation(sP[s][:, :, :], sS[s][:, :, :], ACT.Exp).then_inc(sexp_done[s], 1)
                    elif kind == "sptrans":
                        wait_full(act, i, step)
                        nc.scalar.copy(sS[s][:, :, :], ps[:, :]).then_inc(spt_done[s], 1)
                    elif kind == "route":
                        act.wait_ge(route_step[s], i * ROUTE_N + (1 if l == 0 else ROUTE_0 + 2))
                        src = ps[:, 0:E_N] if l == 0 else sc[s][:, :]
                        nc.scalar.activation(sc2[s][:, :], src, ACT.Exp,
                                             bias=col[s][:, 0:1]).then_inc(gate_exp[s], 1)
                    elif kind == "up":
                        wait_full(act, i, step)
                        if l == 0:
                            if m >= SLOTS:
                                act.wait_ge(t_done[s], i * 8 + m - SLOTS + 1)
                            nc.scalar.activation(th[s][m % SLOTS], ps[:, 0:256], ACT.Tanh,
                                                 scale=0.5).then_inc(th_done[s], 1)
                        elif m % 2:
                            if m >= SLOTS:
                                act.wait_ge(x_done[s], i * 21 + 13 + m - SLOTS)
                            for k in range(4):
                                n = len(BCOL) + 4 * m + k
                                ins = nc.scalar.activation(HT[s][m % SLOTS][:, k * 128:k * 128 + 128],
                                                           ps[:, k * 128:k * 128 + 128], ACT.Relu,
                                                           bias=bcol[:, n:n + 1])
                            ins.then_inc(h_act[s], 1)
                    elif kind == "wT":
                        wait_full(act, i, step)
                        nc.scalar.copy(comT[s][:, :], ps[0:E_N, 0:128]).then_inc(comT_done[s], 1)

            turn(0)
            with act.Fori(1, turns) as i:
                turn(i)

        @block.vector
        def _(dve):
            dve.wait_ge(constants_in, 16 * SETUP_LOADS)

            def taken():
                dve.sem_inc(dve_took, 1)

            def ranks(i, s, start, src, n, const):
                a = src.unsqueeze(1).broadcast_to((128, n, n))
                b = src.unsqueeze(2).broadcast_to((128, n, n))
                cm = cmp8[s][:, 0:n, :, 0:n]
                nc.vector.tensor_tensor(cm[:, :, 0, :], a, b, ALU.is_ge)
                nc.vector.tensor_tensor(cm[:, :, 1, :], a, b, ALU.is_gt).then_inc(route_step[s], 1)
                dve.wait_ge(route_step[s], start + 1)
                nc.vector.tensor_tensor(cm, cm, c(const).rearrange("p (e a f) -> p e a f", e=n, a=2),
                                        ALU.mult).then_inc(route_step[s], 1)
                dve.wait_ge(route_step[s], start + 2)
                nc.vector.tensor_reduce(rank[s][:, 0:n], cm, mybir.AxisListType.XY, ALU.add).then_inc(route_step[s], 1)
                dve.wait_ge(route_step[s], start + 3)

            def turn(i):
                for step in order:
                    kind, s, l, m = step
                    if kind in FILLS:
                        ps = bank[bank_of[step]]
                    if kind == "mask":
                        dve.wait_ge(mask_bias[s], i + 1)
                        nc.vector.tensor_reduce(mmin[s][:, :], mbias[s], X, ALU.min).then_inc(mask_min[s], 1)
                        dve.wait_ge(mask_min[s], i + 1)
                        nc.vector.tensor_scalar(mscale[s][:, :], mmin[s][:, :], 1.0, 1.0, ALU.is_lt,
                                                ALU.add).then_inc(mask_scale[s], 1)
                    elif kind == "vproj":
                        wait_full(dve, i, step)
                        nc.vector.tensor_copy(V[s][:, 2 * m:2 * m + 2, :, :], ps[:, :]).then_inc(v_done[s], 1)
                    elif kind == "kvtail":
                        wait_full(dve, i, step)
                        for k in range(2):
                            nc.vector.tensor_scalar(KT[s][:, k, :, KM], ps[:, 4 * k:4 * k + 4], bc(f"bk{k}"), None,
                                                    ALU.add).then_inc(kvtail_done[s], 1)
                        nc.vector.tensor_copy(vtl[s][:, :, :], ps[0:U, 16:272]).then_inc(kvtail_done[s], 1)
                        dve.wait_ge(kvtail_done[s], i * 3 + 3)
                        for k in range(2):
                            ins = nc.vector.tensor_tensor(
                                vtb[s][:, k, :].rearrange("p (b f) -> p b f", b=GB),
                                vtl[s][:, k, :].unsqueeze(1).broadcast_to((U, GB, 128)),
                                c("tail_block", U).rearrange("p (b f) -> p b f", b=GB), ALU.mult)
                        ins.then_inc(vtail_done[s], 1)
                    elif kind == "ln":
                        src = xin[s] if (l, m) == (0, 0) else xs[s]
                        if (l, m) == (0, 0):
                            dve.wait_ge(x_in[s], i * 16 + 16)
                        else:
                            dve.wait_ge(x_done[s], i * 21 + (10 * l + m))
                        nc.vector.bn_stats(st6[s][:, :], src[:, :]).then_inc(stats_done[s], 1)
                        dve.wait_ge(stats_done[s], at(i, l, 3, m + 1))
                        taken()
                        nc.vector.bn_aggr(mv[s][:, :], st6[s][:, :]).then_inc(mean_done[s], 1)
                    elif kind == "lnT":
                        src = xin[s] if (l, m) == (0, 0) else xs[s]
                        dve.wait_ge(rstd_done[s], at(i, l, 3, m + 1))
                        nc.vector.tensor_scalar(xn[s][:, :], src[:, :], mv[s][:, 0:1], rstd[s][:, 0:1], ALU.subtract,
                                                ALU.mult).then_inc(xn_done[s], 1)
                    elif kind == "qk":
                        dve.wait_ge(qk_done[s], at(i, l, 1, 1))
                        nc.vector.tensor_tensor(
                            BQ[s],
                            qs[s][:, 0:128].rearrange("p (b s) -> p b s", b=GB).unsqueeze(2).broadcast_to((128, GB, J, S)),
                            c("head_q").unsqueeze(1).unsqueeze(3).broadcast_to((128, GB, J, S)),
                            ALU.mult).then_inc(bq_done[s], 1)
                        nc.vector.tensor_tensor(
                            KB[s],
                            qs[s][:, 128:256].rearrange("p (b s) -> p b s", b=GB).unsqueeze(2)
                            .broadcast_to((128, GB, NGR, S)),
                            c("quad").unsqueeze(1).unsqueeze(3).broadcast_to((128, GB, NGR, S)),
                            ALU.mult).then_inc(kb_done[s], 1)
                    elif kind == "scores":
                        wait_full(dve, i, step)
                        if l == 0:
                            if m == 0:
                                dve.wait_ge(mask_scale[s], i + 1)
                            taken()
                            b = m // NGR
                            nc.vector.tensor_tensor_reduce(P[s][:, m, :], ps[:, 0:SK], mbias[s][:, b, :],
                                                           mscale[s][:, b:b + 1], LOWEST, ALU.add, ALU.min,
                                                           nmax[s][:, m:m + 1]).then_inc(max_done[s], 1)
                        else:
                            nc.vector.tensor_reduce(nmax[s][:, m:m + 1], ps[:, 0:SK], X, ALU.max,
                                                    negate=True).then_inc(max_done[s], 1)
                    elif kind == "ptrans" and m % 2 == 0:
                        wait_full(dve, i, step)
                        if m >= 2:
                            dve.wait_ge(pv_done[s], at(i, l, U // 2, m - 1))
                        nc.vector.tensor_copy(PT[s][:, 0, :], ps[:, :]).then_inc(pt_vec[s], 1)
                    elif kind == "norm":
                        if m == 0:
                            dve.wait_ge(exp_done[s], at(i, l, U, U))
                        else:
                            dve.wait_ge(soft[s], i * 7 + 3 + 4 * l)
                        if m == 1:
                            dve.wait_ge(sexp_done[s], at(i, l, 1, 1))
                            nc.vector.tensor_reduce(sums[s][:, :], sP[s][:, :, :], X, ALU.add).then_inc(sums_done[s], 1)
                            dve.wait_ge(sums_done[s], at(i, l, 1, 1))
                        nc.vector.reciprocal(rsum[s][:, :], sums[s][:, :]).then_inc(rsum_done[s], 1)
                        dve.wait_ge(rsum_done[s], at(i, l, 2, m + 1))
                        nc.vector.tensor_tensor(wsel[s][:, :, :], rsum[s][:, :].unsqueeze(2).broadcast_to((128, U, J)),
                                                c("quad").unsqueeze(1).broadcast_to((128, U, J)),
                                                ALU.mult).then_inc(wsel_done[s], 1)
                        dve.wait_ge(wsel_done[s], at(i, l, 2, m + 1))
                        dve.wait_ge(attn_done[s], at(i, l, 2, m + 1))
                        nc.vector.tensor_tensor(On[s][:, :].rearrange("p (u d) -> p u d", d=DH),
                                                attn_out[s][:, :].rearrange("p (u d) -> p u d", d=DH),
                                                wsel[s][:, :, :].rearrange("p u j -> p (u j)").unsqueeze(2)
                                                .broadcast_to((128, U * J, DH)), ALU.mult).then_inc(on_done[s], 1)
                    elif kind == "oproj":
                        wait_full(dve, i, step)
                        dve.wait_ge(xpb_done[s], at(i, l, 2, m + 1))
                        if (l, m) == (0, 0):
                            wait(dve, x_out[s], i * 16)
                        nc.vector.tensor_tensor(xs[s][:, :], ps[:, 0:128], xpb[s][:, :], ALU.add).then_inc(x_done[s], 1)
                    elif kind == "vrep":
                        wait_full(dve, i, step)
                        nc.vector.tensor_tensor(VB[s][:, :, :, :], ps[:, :].rearrange("p (b g f) -> p b g f", b=GB, g=NGR),
                                                c("quad").unsqueeze(1).unsqueeze(3).broadcast_to((128, GB, NGR, 32)),
                                                ALU.mult).then_inc(vb_done[s], 1)
                    elif kind == "linesN":
                        dve.wait_ge(lines_step[s], i * 6 + 4)
                        nc.vector.tensor_reduce(lss[s][:, :], lsq[s][:, :].rearrange("p (h c) -> p h c", c=6), X,
                                                ALU.add).then_inc(lss_done[s], 1)
                    elif kind == "linesU":
                        dve.wait_ge(lines_step[s], i * 6 + 5)
                        nc.vector.tensor_scalar(lnn[s][:, :], lnn[s][:, :], 1e-12, None, ALU.max).then_inc(lrn_done[s], 1)
                        dve.wait_ge(lrn_done[s], i * 2 + 1)
                        nc.vector.reciprocal(lrn[s][:, :], lnn[s][:, :]).then_inc(lrn_done[s], 1)
                    elif kind == "linesT":
                        dve.wait_ge(lT_done[s], i + 1)
                        nc.vector.tensor_tensor(
                            LQ[s][:, :, :, :],
                            lT[s][:, :].rearrange("p (b s) -> p b s", b=GB).unsqueeze(2).broadcast_to((96, GB, J, S)),
                            c("head_p", 96).unsqueeze(1).unsqueeze(3).broadcast_to((96, GB, J, S)),
                            ALU.mult).then_inc(lq_done[s], 1)
                    elif kind == "jlines":
                        wait_full(dve, i, step)
                        nc.vector.tensor_tensor(
                            LK[s][:, :, :, :],
                            ps[0:96, 0:128].rearrange("p (b s) -> p b s", b=GB).unsqueeze(2)
                            .broadcast_to((96, GB, NGR, S)),
                            c("group_p", 96).unsqueeze(1).unsqueeze(3).broadcast_to((96, GB, NGR, S)),
                            ALU.mult).then_inc(lq_done[s], 1)
                    elif kind == "sscore":
                        wait_full(dve, i, step)
                        p3 = ps[:, :].rearrange("p (u k) -> p u k", k=S)
                        base = i * 7 + 3 * l
                        if l == 0:
                            nc.vector.tensor_tensor(sS[s][:, :, :], p3,
                                                    c("causal0").unsqueeze(1).broadcast_to((128, U, S)),
                                                    ALU.add).then_inc(soft[s], 1)
                        else:
                            nc.vector.tensor_tensor(sS[s][:, :, :], p3,
                                                    c("tril").unsqueeze(1).broadcast_to((128, U, S)),
                                                    ALU.mult).then_inc(soft[s], 1)
                            dve.wait_ge(soft[s], base + 1)
                            nc.vector.tensor_tensor(sS[s][:, :, :], sS[s][:, :, :],
                                                    c("causal1").unsqueeze(1).broadcast_to((128, U, S)),
                                                    ALU.add).then_inc(soft[s], 1)
                        dve.wait_ge(soft[s], base + 1 + l)
                        nc.vector.tensor_reduce(nmax[s][:, :], sS[s][:, :, :], X, ALU.max).then_inc(soft[s], 1)
                        dve.wait_ge(soft[s], base + 2 + l)
                        nc.vector.tensor_tensor(sS[s][:, :, :], sS[s][:, :, :],
                                                nmax[s][:, :].unsqueeze(2).broadcast_to((128, U, S)),
                                                ALU.subtract).then_inc(soft[s], 1)
                    elif kind == "route":
                        wait_full(dve, i, step)
                        base = i * ROUTE_N + l * ROUTE_0
                        if l == 0:
                            nc.vector.tensor_reduce(col[s][:, 0:1], ps[:, 0:E_N], X, ALU.max,
                                                    negate=True).then_inc(route_step[s], 1)
                        else:
                            nc.vector.tensor_tensor(sc[s][:, :], ps[:, 0:E_N],
                                                    brow[:, BROW["router"]:BROW["router"] + E_N],
                                                    ALU.add).then_inc(route_step[s], 1)
                            dve.wait_ge(route_step[s], base + 1)
                            nc.vector.tensor_reduce(col[s][:, 0:1], sc[s][:, :], X, ALU.max,
                                                    negate=True).then_inc(route_step[s], 1)
                    elif kind == "pick":
                        base = i * ROUTE_N + l * ROUTE_0
                        if l == 0:
                            dve.wait_ge(gate_exp[s], at(i, l, 1, 1))
                            nc.vector.tensor_reduce(col[s][:, 1:2], sc2[s][:, :], X, ALU.add).then_inc(route_step[s], 1)
                            dve.wait_ge(route_step[s], base + 2)
                            nc.vector.reciprocal(col[s][:, 2:3], col[s][:, 1:2]).then_inc(route_step[s], 1)
                            dve.wait_ge(route_step[s], base + 3)
                            nc.vector.tensor_scalar(sc[s][:, :], sc2[s][:, :], col[s][:, 2:3], None,
                                                    ALU.mult).then_inc(route_step[s], 1)
                            dve.wait_ge(route_step[s], base + 4)
                            nc.vector.tensor_reduce(gs[s][:, :], sc[s][:, :].rearrange("p (g e) -> p g e", e=2), X,
                                                    ALU.max).then_inc(route_step[s], 1)
                            dve.wait_ge(route_step[s], base + 5)
                            ranks(i, s, base + 5, gs[s][:, :], 4, "order4")
                            nc.vector.tensor_scalar(gs[s][:, :], rank[s][:, 0:4], 2.0, None,
                                                    ALU.is_lt).then_inc(route_step[s], 1)
                            dve.wait_ge(route_step[s], base + 9)
                            nc.vector.tensor_tensor(sc[s][:, :].rearrange("p (g e) -> p g e", e=2),
                                                    sc[s][:, :].rearrange("p (g e) -> p g e", e=2),
                                                    gs[s][:, :].unsqueeze(2).broadcast_to((128, 4, 2)),
                                                    ALU.mult).then_inc(route_step[s], 1)
                            dve.wait_ge(route_step[s], base + 10)
                            ranks(i, s, base + 10, sc[s][:, :], E_N, "order8")
                            nxt = base + 13
                            weights = sc[s]
                        else:
                            ranks(i, s, base + 2, sc[s][:, :], E_N, "order8")
                            dve.wait_ge(gate_exp[s], at(i, l, 1, 1))
                            nxt = base + 5
                            weights = sc2[s]
                        nc.vector.tensor_scalar(rank[s][:, :], rank[s][:, :], 2.0, None,
                                                ALU.is_lt).then_inc(route_step[s], 1)
                        dve.wait_ge(route_step[s], nxt + 1)
                        nc.vector.tensor_tensor(rank[s][:, :], rank[s][:, :], weights[:, :],
                                                ALU.mult).then_inc(route_step[s], 1)
                        dve.wait_ge(route_step[s], nxt + 2)
                        nc.vector.tensor_reduce(col[s][:, 1:2], rank[s][:, :], X, ALU.add).then_inc(route_step[s], 1)
                        dve.wait_ge(route_step[s], nxt + 3)
                        nc.vector.reciprocal(col[s][:, 2:3], col[s][:, 1:2]).then_inc(route_step[s], 1)
                        dve.wait_ge(route_step[s], nxt + 4)
                        nc.vector.tensor_scalar(comb[s][:, :], rank[s][:, :], col[s][:, 2:3], 0.5 if l == 0 else 1.0,
                                                ALU.mult, ALU.mult).then_inc(comb_done[s], 1)
                    elif kind == "up":
                        if l == 0:
                            dve.wait_ge(th_done[s], i * 8 + m + 1)
                            h = HT[s][m % SLOTS][:, 0:256]
                            if m >= SLOTS:
                                dve.wait_ge(x_done[s], i * 21 + 3 + m - SLOTS)
                            nc.vector.scalar_tensor_tensor(h, th[s][m % SLOTS], 1.0, ps[:, 0:256], ALU.add,
                                                           ALU.mult).then_inc(t_done[s], 1)
                            dve.wait_ge(t_done[s], i * 8 + m + 1)
                            nc.vector.tensor_tensor(h, h, ps[:, 256:512], ALU.mult).then_inc(h_vec[s], 1)
                        elif m % 2 == 0:
                            wait_full(dve, i, step)
                            if m >= SLOTS:
                                dve.wait_ge(x_done[s], i * 21 + 13 + m - SLOTS)
                            for k in range(4):
                                n = len(BCOL) + 4 * m + k
                                ins = nc.vector.tensor_scalar(HT[s][m % SLOTS][:, k * 128:k * 128 + 128],
                                                              ps[:, k * 128:k * 128 + 128], bcol[:, n:n + 1], 0.0,
                                                              ALU.add, ALU.max)
                            ins.then_inc(h_vec[s], 1)
                    elif kind == "down":
                        wait_full(dve, i, step)
                        if m == 0:
                            dve.wait_ge(comb_done[s], at(i, l, 1, 1))
                        dve.wait_ge(x_done[s], i * 21 + 10 * l + 2 + m)
                        nc.vector.scalar_tensor_tensor(xs[s][:, :], ps[:, 0:128], comb[s][:, m:m + 1], xs[s][:, :],
                                                       ALU.mult, ALU.add).then_inc(x_done[s], 1)
                    elif kind == "wb2":
                        wait_full(dve, i, step)
                        dve.wait_ge(x_done[s], i * 21 + 20)
                        nc.vector.tensor_tensor(xs[s][:, :], ps[:, 0:128], xs[s][:, :], ALU.add).then_inc(x_done[s], 1)

            turn(0)
            with dve.Fori(1, turns) as i:
                turn(i)


ROUTE_0, ROUTE_N = 17, 17 + 9


def constants():
    import numpy as np
    k = np.zeros((128, NCONST), np.float32)
    p = np.arange(128)

    def put(name, value):
        a, b = CONST[name]
        value = np.asarray(value, np.float32)
        k[0:value.shape[0], a:b] = value.reshape(value.shape[0], -1)

    put("ident", np.eye(128))
    own = ((p % 32)[:, None] // DH == np.arange(J)) / np.sqrt(np.float32(DH))
    put("head_q", own)
    whole = (p[:, None] // DH == np.arange(H)) / np.sqrt(np.float32(DH))
    put("head_x0", -whole)
    put("head_x1", whole)
    put("quad", p[:, None] // 32 == np.arange(4))
    put("fold", p[:, None] % 32 == np.arange(32))
    tril = (np.arange(S)[None, :] <= (p % 32)[:, None]).astype(np.float32)
    put("tril", tril)
    put("causal0", (tril - 1.0) * np.float32(LOWEST))
    put("causal1", (tril - 1.0) * np.float32(1e10))
    for name, n in (("order8", E_N), ("order4", 4)):
        e, f = np.arange(n)[:, None], np.arange(n)[None, :]
        put(name, np.broadcast_to(np.stack([f < e, f > e], 1).reshape(1, -1), (128, 2 * n * n)))
    put("tail_block", np.arange(U)[:, None] == np.arange(512)[None, :] // 32)
    j6 = np.array([[0, 0, 0, 0, 0, 1], [0, 0, 0, 0, -1, 0], [0, 0, 0, 1, 0, 0], [0, 0, 1, 0, 0, 0],
                   [0, -1, 0, 0, 0, 0], [1, 0, 0, 0, 0, 0]], np.float32)
    put("jmat", np.kron(np.eye(H), j6.T))
    q = np.arange(96)
    put("head_p", (q % 24)[:, None] // 6 == np.arange(J))
    put("group_p", q[:, None] // 24 == np.arange(NGR))
    put("half", np.full((128, 1), 0.5))
    put("mhalf", np.full((128, 1), -0.5))
    put("eps", np.full((128, 1), EPS))
    return k


def kernel(**inputs):
    import numpy as np
    import concourse.bacc as bacc
    from concourse.bass_utils import run_bass_kernel_spmd

    a = {n: np.asarray(v) for n, v in inputs.items()}
    pi, pj = np.array([0, 0, 0, 1, 1, 2]), np.array([1, 2, 3, 2, 3, 3])
    head = np.arange(H)[:, None] * 3 * DH + np.arange(DH)
    part = [(head + k * DH).reshape(-1) for k in range(3)]
    w1a, b1a = a["L1_attn_W1"], a["L1_attn_b1"]
    wqkv, bqkv = a["L0_attn_Wqkv"], a["L0_attn_bqkv"]
    four = np.arange(H)[:, None] * 4
    p4 = [a[n][:, (four + k).reshape(-1)] for n, k in (("L0_attn_W1p", pi), ("L0_attn_W2p", pj), ("L0_attn_W1p", pj),
                                                      ("L0_attn_W2p", pi))]
    wsq = np.concatenate(
        [a["L0_xattn_Wq"].T, a["L0_xattn_Wk"].T, a["L1_xattn_W_q"].T, a["L1_xattn_W_k"].T, a["L0_xattn_Wv"].T,
         a["L1_xattn_W_v"].T, a["L0_xattn_Wo"].T, a["L1_xattn_W_o"].T,
         wqkv[:, 0:128], wqkv[:, 128:256], wqkv[:, 256:384], a["L0_attn_Wout"],
         w1a[:, part[0]], w1a[:, part[1]], w1a[:, part[2]], a["L1_attn_W2"], *p4, a["L0_ffn_gate_w"].T,
         a["L1_ffn_W_router"]], 1)
    bcol = np.concatenate(
        [np.stack([a["L0_xattn_bq"], a["L0_xattn_bk"], a["L0_xattn_bv"], a["L1_xattn_b_q"], a["L1_xattn_b_k"],
                   a["L1_xattn_b_v"], bqkv[0:128], bqkv[128:256], bqkv[256:384],
                   b1a[part[0]], b1a[part[1]], b1a[part[2]],
                   np.resize(np.repeat(a["L0_attn_plucker_scale"], 6), 128)], 1),
         a["L1_ffn_b1"].reshape(4 * E_N, 128).T], 1)
    brow = np.broadcast_to(np.concatenate([a["L0_xattn_bo"], a["L0_attn_bout"], a["L1_xattn_b_o"], a["L1_attn_b2"],
                                           a["L1_ffn_b_router"]])[None, :], (128, NBROW))
    cx = a["ctx_1024"].reshape(NG, GB, SK, D)
    tail = cx[:, :, KM, :].transpose(0, 2, 1)
    ctx = np.concatenate([cx[:, :, :KM, :].transpose(0, 3, 1, 2).reshape(NG, D, GB * KM), tail,
                          np.repeat(tail, NGR, axis=2)], 2)
    arrays = {
        "x": a["x"].reshape(NG, GB * S, D), "ctx": ctx, "mask": a["mask_Bx1xSxS2_ik1"].reshape(NG, GB, S, SK),
        "wsq": wsq,
        "w13": a["L0_ffn_w13_weight"].transpose(2, 0, 1),
        "w2a": a["L0_ffn_w2_weight"].reshape(E_N, D, 2, 128).transpose(3, 0, 2, 1),
        "w1": a["L1_ffn_W1"].transpose(1, 0, 2),
        "w2b": a["L1_ffn_W2"].reshape(E_N, 4, 128, D).transpose(2, 0, 1, 3),
        "const": constants(), "bcol": bcol, "brow": brow, "b2": a["L1_ffn_b2"],
    }
    arrays = {n: np.ascontiguousarray(v) for n, v in arrays.items()}
    nc = bacc.Bacc("TRN2", target_bir_lowering=False, num_devices=1)
    aps = [nc.dram_tensor(f"{n}_in", v.shape, mybir.dt.from_np(v.dtype), kind="ExternalInput").ap() for n, v in arrays.items()]
    out = nc.dram_tensor("out", (NG, GB * S, D), F32, kind="ExternalOutput").ap()
    perceiver(nc, *aps, out)
    r = run_bass_kernel_spmd(nc, [{f"{n}_in": v for n, v in arrays.items()}], core_ids=[0])
    return r.results[0]["out"].reshape(B, S, D)
```

```python
from contextlib import ExitStack

import concourse.bass as bass
from concourse import mybir

F32 = mybir.dt.float32
I32 = mybir.dt.int32
ALU = mybir.AluOpType
ACT = mybir.ActivationFunctionType
X = mybir.AxisListType.X

B, S, SK, D = 64, 32, 257, 128
H, DH = 16, 8
GB = 4
NG = B // GB
J = 4
NGR = H // J
U = GB * NGR
KM = 256
E_N = 8
F0, F1 = 256, 512
EPS = 1e-5
BIG = 1e9
LOWEST = 3.0e38
STREAMS = 2
SLOTS = 4

CONST = {}
_at = 0
for _n, _w in (("ident", 128), ("head_q", 4), ("head_x0", 16), ("head_x1", 16), ("quad", 4), ("fold", 32), ("causal0", 32),
               ("tril", 32), ("causal1", 32), ("order8", 128), ("order4", 32), ("tail_block", 512),
               ("jmat", 96), ("head_p", 4), ("group_p", 4), ("half", 1), ("mhalf", 1), ("eps", 1)):
    CONST[_n] = (_at, _at + _w)
    _at += _w
NCONST = _at

BCOL = {n: k for k, n in enumerate(("bq0", "bk0", "bv0", "bq1", "bk1", "bv1",
                                    "sq0", "sk0", "sv0", "sq1", "sk1", "sv1", "plucker"))}
NBCOL = len(BCOL) + 4 * E_N
BROW = {"o0": 0, "so0": 128, "o1": 256, "so1": 384, "router": 512}
NBROW = 520


def step_parts(kind, l, m):
    return {
        "mask": (("pool", 4.5), ("dve", 1.35)), "kproj": (("pe", .86), ("act", .57)),
        "vproj": (("pe", .86), ("act", .48)), "kvtail": (("pe", .77), ("dve", 1.92)),
        "ln": (("dve", .5), ("pool", .7)), "xpb": (("pool", .42),),
        "lnT": (("dve", .26), ("pe", .11), ("act", .16)), "xnR": (("act", .48),),
        "qproj": (("pe", .22), ("act", .25)), "bq": (("pool", 1.0),),
        "scores": (("pe", .43), ("dve", .4 - .07 * l), ("act", .49)),
        "ptrans": (("pe", .43), ("act", .48) if m % 2 else ("dve", .6)), "pv": (("pe", .78),),
        "tailT": (("pe", .11), ("act", .16)), "tailV": (("pe", .86),),
        "sel": (("dve", .42 + .76 * m),), "norm": (("dve", .6),), "oT": (("pe", .78), ("act", .25)),
        "oproj": (("pe", .22), ("dve", .2)), "qk": (("pe", .43), ("act", .25), ("dve", 1.3)),
        "vrep": (("pe", .86), ("dve", .6)), "lines": (("pe", .64), ("act", .37), ("pool", 1.6)),
        "linesN": (("dve", .17), ("pool", 2.93)), "linesU": (("dve", .37), ("pool", .31)),
        "linesT": (("pe", .11), ("act", .16), ("dve", .6)), "jlines": (("pe", .22), ("dve", .6)),
        "sscore": (("pe", .87 * (2 - l)), ("dve", 2.06 + .73 * l), ("act", .52)),
        "sptrans": (("pe", .43), ("act", .48)), "spv": (("pe", .87),),
        "route": (("pe", .11), ("dve", .07 + .21 * l), ("act", .17)), "groups": (("dve", 2.3),), "pick": (("dve", 2.0),),
        "up": ((("pe", .87), ("act", .26), ("dve", .8)) if l == 0 else
               (("pe", .87), ("act", 1.0)) if m % 2 else (("pe", .87), ("dve", 1.03))),
        "down": (("pe", .43 * (l + 1)), ("dve", .26)), "wT": (("pe", .11), ("act", .16)),
        "wb2": (("pe", .22), ("dve", .2)), "store": (("act", .1),),
    }[kind]


PHASE = {k: n for n, kinds in enumerate((("qproj", "bq", "scores", "ptrans", "pv", "tailT", "tailV"),
                                         ("qk", "xnR", "vrep", "lines", "linesN", "linesU", "linesT", "jlines", "sscore",
                                          "sptrans", "spv"),
                                         ("route", "groups", "pick", "up", "down", "wT", "wb2", "store"))) for k in kinds}


def phase(step):
    kind, s, l, m = step
    return 3 * l + PHASE.get(kind, m)


def behind_by(step):
    kind, s, l, m = step
    early = kind in ("mask", "kproj", "vproj", "kvtail") or (kind, l, m) in (("ln", 0, 0), ("xpb", 0, 0))
    return 0 if early or phase(step) < CUT[step[1]] else 1


def stream_steps(s):
    needs, first = {}, {}

    def add(step, *after):
        needs[(step[0], s, *step[1:])] = [(x[0], s, *x[1:]) for x in after]

    def after_last_group(step, *after):
        first[(step[0], s, *step[1:])] = [(x[0], s, *x[1:]) for x in after]

    add(("mask", 0, 0))
    last = None
    for l in range(2):
        for m in range(2):
            add(("kproj", l, m), *([last] if last else []))
            last = ("kproj", l, m)
    for m in range(4):
        add(("vproj", 0, m), *([("vproj", 0, m - 1)] if m else []))
    add(("kvtail", 0, 0))
    for l in range(2):
        add(("ln", l, 0), *([("down", 0, E_N - 1)] if l else []))
        add(("lnT", l, 0), ("ln", l, 0))
        add(("qproj", l, 0), ("lnT", l, 0))
        for b in range(GB):
            add(("bq", l, b), ("bq", l, b - 1) if b else ("qproj", l, 0),
                *([("scores", l, NGR * (b - 1) - 1)] if b > 1 else []))
        for u in range(U):
            add(("scores", l, u), ("bq", l, u // NGR), *([("scores", l, u - 1)] if u else
                                    [("kproj", l, 1), ("kvtail", 0, 0), ("mask", 0, 0)]))
        for w in range(U // 2):
            add(("ptrans", l, w), ("scores", l, 2 * w + 1), *([("ptrans", l, w - 1)] if w else []),
                *([("pv", l, w - 2)] if w > 1 else []))
            add(("pv", l, w), ("ptrans", l, w), *([("pv", l, w - 1)] if w else [("vproj", 0, 3)]))
        add(("tailT", l, 0), ("scores", l, U - 1))
        add(("tailV", l, 0), ("tailT", l, 0), ("pv", l, U // 2 - 1))
        for m in range(2):
            add(("sel", l, m), ("scores", l, U - 1) if m == 0 else ("sscore", l, 0), *([("norm", l, 0)] if m else []))
            add(("norm", l, m), ("sel", l, m), ("tailV", l, 0) if m == 0 else ("spv", l, 0))
            add(("xpb", l, m), ("ln", l, m), *([("oproj", l, 0)] if m else []))
            add(("oT", l, m), ("norm", l, m))
            add(("oproj", l, m), ("oT", l, m), ("xpb", l, m))
            add(("ln", l, m + 1), ("oproj", l, m))
            add(("lnT", l, m + 1), ("ln", l, m + 1))
        add(("qk", l, 0), ("lnT", l, 1))
        add(("xnR", l, 0), ("lnT", l, 1))
        add(("vrep", l, 0), ("xnR", l, 0))
        if l == 0:
            for step, before in (("lines", "lnT"), ("linesN", "lines"), ("linesU", "linesN"), ("linesT", "linesU"),
                                 ("jlines", "linesT")):
                add((step, 0, 0), (before, 0, 1 if before == "lnT" else 0))
        add(("sscore", l, 0), ("qk", l, 0), *([("jlines", 0, 0)] if l == 0 else []))
        add(("sptrans", l, 0), ("sscore", l, 0))
        add(("spv", l, 0), ("sptrans", l, 0), ("vrep", l, 0))
        add(("route", l, 0), ("lnT", l, 2))
        if l == 0:
            add(("groups", 0, 0), ("route", 0, 0))
        add(("pick", l, 0), ("groups" if l == 0 else "route", l, 0))
        for e in range(E_N):
            add(("up", l, e), *([("up", l, e - 1)] if e else [("lnT", l, 2)]),
                *([("down", l, e - SLOTS)] if e >= SLOTS else []))
            add(("down", l, e), ("up", l, e), *([("down", l, e - 1)] if e else [("pick", l, 0)]))
    add(("wT", 1, 0), ("pick", 1, 0))
    add(("wb2", 1, 0), ("wT", 1, 0), ("down", 1, E_N - 1))
    add(("store", 1, 0), ("wb2", 1, 0))
    after_last_group(("mask", 0, 0), ("scores", 0, U - 1))
    after_last_group(("kproj", 0, 0), ("scores", 0, U - 1))
    after_last_group(("kproj", 1, 0), ("scores", 1, U - 1))
    after_last_group(("vproj", 0, 0), ("pv", 1, U // 2 - 1))
    after_last_group(("kvtail", 0, 0), ("tailV", 1, 0))
    after_last_group(("ln", 0, 0), ("lnT", 1, 2))
    after_last_group(("lnT", 0, 0), ("up", 1, E_N - 1), ("route", 1, 0))
    after_last_group(("xpb", 0, 0), ("oproj", 1, 1), ("ln", 1, 2))
    after_last_group(("scores", 0, 0), ("down", 1, E_N - 1))
    after_last_group(("oproj", 0, 0), ("store", 1, 0))
    after_last_group(("route", 0, 0), ("wT", 1, 0))
    return needs, first


FILLS = ("kproj", "vproj", "kvtail", "lnT", "qproj", "scores", "ptrans", "tailT", "oT", "oproj", "qk", "vrep",
         "lines", "linesT", "jlines", "sscore", "sptrans", "route", "up", "down", "wT", "wb2")


FRESH = 24
CUT = (0, 3)
LAG = (-0.05686, -4.93816, -4.33576, -0.14378, 4.13598, -12.46616,
       -0.19571, 6.7799, -11.49163, 6.06303, -2.73674, 0.74693)
HOP = 0.18


def build_order():
    needs, first = {}, {}
    for s in range(STREAMS):
        n, f = stream_steps(s)
        needs |= n
        first |= f
    took = {x: sum(t + HOP for _, t in step_parts(x[0], x[2], x[3])) for x in needs}
    most = {x: max(t for _, t in step_parts(x[0], x[2], x[3])) for x in needs}
    behind = {}
    listed = {x: [y for y in needs[x] if behind_by(y) == behind_by(x)] +
                 [y for y in first.get(x, []) if behind_by(y) > behind_by(x)] for x in needs}
    data = {x: [y for y in needs[x] if y[0] != x[0]] for x in needs}
    follow = {x: [] for x in needs}
    for x, before in listed.items():
        for y in before:
            follow[y].append(x)

    def chain(x):
        if x not in behind:
            behind[x] = took[x] + max((chain(y) - (took[x] - most[x] if y[0] == x[0] else 0.0) for y in follow[x]),
                                      default=0.0)
        return behind[x]

    ring = 8 - STREAMS
    free_from = {"pe": 0.0, "dve": 0.0, "act": 0.0, "pool": 0.0}
    ended, read = {}, []
    for _ in range(PASSES):
        ends, order = {}, []
        left = {x: len(listed[x]) for x in needs}
        frontier = [x for x in needs if left[x] == 0]
        while len(order) < len(needs):
            best = None
            for x in frontier:
                t = max([(ends if behind_by(y) == behind_by(x) else ended).get(y, 0.0) for y in data[x]], default=0.0)
                parts = step_parts(x[0], x[2], x[3])
                start = max(t, free_from[parts[0][0]])
                if parts[0][0] != "pe" and "pe" in dict(parts):
                    start = max(start + parts[0][1], free_from["pe"])
                if x[0] in FILLS and len(read) >= ring:
                    start = max(start, read[-ring])
                late = max(start, free_from["pe"])
                key = (late - EAGER * (chain(x) - LAG[6 * x[1] + phase(x)]) - BONUS.get(x[0], 0.0)
                       - SHIFT.get(x[:3], 0.0), x)
                if best is None or key < best[0]:
                    best = (key, x, t)
            _, x, t = best
            for engine, dur in step_parts(x[0], x[2], x[3]):
                t = max(t, free_from[engine])
                if engine == "pe" and x[0] in FILLS and len(read) >= ring:
                    t = max(t, read[-ring])
                t += dur
                free_from[engine] = t
                t += HOP
            ends[x] = t
            if x[0] in FILLS:
                read.append(t)
            order.append(x)
            frontier.remove(x)
            for y in follow[x]:
                left[y] -= 1
                if left[y] == 0:
                    frontier.append(y)
        ended = ends
    return order


PASSES = 3
EAGER = 0.12288
SHIFT = {("sptrans", 0, 1): 0.12556, ("sel", 1, 1): -0.3342, ("norm", 0, 0): 1.83338, ("kvtail", 0, 0): 0.71448,
         ("bq", 1, 0): 1.13442, ("wb2", 1, 0): -1.98118, ("linesN", 1, 1): 0.53781, ("qk", 0, 1): -0.51769,
         ("vproj", 1, 1): 0.13032, ("qk", 1, 0): 0.18963, ("ln", 0, 0): 1.7876, ("groups", 1, 0): 1.13864,
         ("ln", 1, 0): 0.3221, ("vproj", 1, 0): 0.84387, ("xnR", 1, 0): 0.68559, ("scores", 1, 1): -0.02756,
         ("spv", 1, 1): 0.10932, ("pick", 0, 0): -0.45785, ("lnT", 0, 0): -0.43921, ("ptrans", 1, 1): 0.03015,
         ("groups", 0, 1): -1.31372, ("wb2", 0, 1): -0.51418, ("xpb", 1, 0): -1.74777, ("wT", 0, 0): -0.97493,
         ("vrep", 1, 0): 1.14946, ("lines", 0, 0): -0.99043, ("vproj", 0, 1): -1.04698,
         ("lines", 0, 1): -0.34781, ("oproj", 0, 0): -0.62061, ("norm", 1, 1): 0.48203}
BONUS = {"vrep": -0.28486, "kvtail": 1.65414, "mask": -1.20026, "kproj": -0.38331, "wT": 1.22187,
         "down": -1.7029, "lines": 1.29648, "pick": 0.86368, "sptrans": -0.26499, "qk": 0.29744, "bq": 1.61174,
         "ln": 0.80808, "oT": 0.10737, "wb2": -0.27001, "spv": -0.19358, "route": -1.08219, "sscore": -0.79393,
         "up": -1.6467, "xpb": 1.8921, "groups": 0.35103, "linesN": 1.75174, "norm": 0.66487, "xnR": 0.68082,
         "oproj": 0.34042, "sel": -0.42584, "lnT": -0.11232}


WCOL = {}
_at = 0
for _n, _w in (("q0", 128), ("k0", 128), ("q1", 128), ("k1", 128), ("v01", 256), ("o0", 128), ("o1", 128),
               ("sq0", 128), ("sk0", 128), ("sv0", 128), ("so0", 128), ("sq1", 128), ("sk1", 128), ("sv1", 128),
               ("so1", 128), ("p4", 384), ("gate0", 8), ("gate1", 8)):
    WCOL[_n] = (_at, _at + _w)
    _at += _w
WSQ = _at
SETUP_LOADS = 5
EXPERT_LOADS = 4


def perceiver(nc, x_d, ctx_d, mask_d, wsq_d, w13_d, w2a_d, w1_d, w2b_d, const_d, bcol_d, brow_d, b2_d, out_d):
    order = build_order()
    turns = NG // STREAMS
    ring = 8 - STREAMS
    fills = [step for step in order if step[0] in FILLS]
    bank_of = {step: n % ring for n, step in enumerate(fills)}
    bank_fills = [fills[k::ring] for k in range(ring)]

    with ExitStack() as ctx:
        def sb(name, shape, dt=F32):
            return ctx.enter_context(nc.sbuf_tensor(name, shape, dt))

        def each(name, shape, dt=F32):
            return [sb(f"{name}{s}", shape, dt) for s in range(STREAMS)]

        def sem(name):
            return ctx.enter_context(nc.semaphore(name))

        def sems(name):
            return [sem(f"{name}{s}") for s in range(STREAMS)]

        bank = [ctx.enter_context(nc.psum_tensor(f"bank{k}", [128, 512], F32)) for k in range(ring)]
        attn_out = [ctx.enter_context(nc.psum_tensor(f"attn_out{s}", [128, 512], F32)) for s in range(STREAMS)]

        cst = sb("cst", [128, NCONST])
        bcol = sb("bcol", [128, NBCOL])
        brow = sb("brow", [128, NBROW])
        wsq = sb("wsq", [128, WSQ])
        w13 = sb("w13", [128, E_N, 512])
        w2a = sb("w2a", [128, E_N, 2, 128])
        w1 = sb("w1", [128, E_N, 512])
        w2b = sb("w2b", [128, E_N, 4, 128])
        b2 = sb("b2", [E_N, 128])
        jscaled = sb("jscaled", [96, 96])

        def c(name, rows=128):
            a, b = CONST[name]
            return cst[0:rows, a:b]

        def w(name):
            a, b = WCOL[name]
            return wsq[:, a:b]

        def bc(name, rows=128):
            return bcol[0:rows, BCOL[name]:BCOL[name] + 1]

        ident = c("ident")

        xin = each("xin", [128, D])
        ctxT = each("ctxT", [128, GB * KM + GB + U])
        maskb = each("maskb", [128, GB, SK], I32)
        xs = each("xs", [128, D])
        xpb = each("xpb", [128, D])
        mbias = [t.bitcast(F32) for t in (m[:, :, :] for m in maskb)]
        mmin = each("mmin", [128, GB])
        mscale = each("mscale", [128, GB])
        KT = each("KT", [128, 2, GB, SK])
        V = each("V", [128, 2 * GB, 2, 128])
        vtl = each("vtl", [U, 2, 128])
        vtb = each("vtb", [U, 2, 512])
        st6 = each("st6", [128, 6])
        mv = each("mv", [128, 2])
        veps = each("veps", [128, 1])
        rstd = each("rstd", [128, 1])
        xn = each("xn", [128, D])
        xnT = each("xnT", [128, D])
        qs = each("qs", [128, 256])
        BX = each("BX", [128, 2, H, S])
        BQ = [t[:, 0, :, :].rearrange("p (b j) s -> p b j s", b=GB) for t in BX]
        P = each("P", [128, U, SK])
        def over_weights(s, k, rows, *shape):
            names = "a b c"[:2 * len(shape) - 1]
            sizes = dict(zip(names.split(), shape))
            return (P[s][0:rows, :, :].rearrange("p u k -> p (u k)")[:, 512 * k:512 * k + 512]
                    .rearrange(f"p ({names}) -> p {names}", **sizes))

        xnR = [over_weights(s, 0, 128, GB, NGR, S) for s in range(STREAMS)]
        KB = [over_weights(s, 1, 128, GB, NGR, S) for s in range(STREAMS)]
        VB = [over_weights(s, 2, 128, GB, NGR, 32) for s in range(STREAMS)]
        sS = [over_weights(s, 3, 128, U, S) for s in range(STREAMS)]
        sP = [over_weights(s, 4, 128, U, S) for s in range(STREAMS)]
        LQ = [over_weights(s, 5, 96, GB, J, S) for s in range(STREAMS)]
        LK = [over_weights(s, 6, 96, GB, NGR, S) for s in range(STREAMS)]
        th = [[over_weights(s, 4 + e // 2, 128, 2, 256)[:, e % 2, :] for e in range(SLOTS)] for s in range(STREAMS)]
        HT = [[over_weights(s, e, 128, 1, 512)[:, 0, :] for e in range(SLOTS)] for s in range(STREAMS)]
        nmax = each("nmax", [128, U])
        sums = each("sums", [128, U])
        rsum = each("rsum", [128, U])
        wsel = each("wsel", [128, U, J])
        PT = each("PT", [128, 2, 512])
        tT = each("tT", [U, 128])
        On = each("On", [128, 512])
        OT = each("OT", [128, 128])
        p4 = each("p4", [128, 4, 96])
        pa = each("pa", [128, 96])
        pb = each("pb", [128, 96])
        ln6 = each("ln6", [128, 96])
        lsq = each("lsq", [128, 96])
        lss = each("lss", [128, H])
        lnn = each("lnn", [128, H])
        lrn = each("lrn", [128, H])
        lT = each("lT", [96, 128])
        sc = each("sc", [128, E_N])
        sc2 = each("sc2", [128, E_N])
        col = each("col", [128, 4])
        gs = each("gs", [128, 4])
        cmp8 = each("cmp8", [128, E_N, 2, E_N])
        rank = each("rank", [128, E_N])
        comb = each("comb", [128, E_N])
        comT = each("comT", [E_N, 128])

        constants_in, experts_in, jscaled_done = sem("constants_in"), sem("experts_in"), sem("jscaled_done")
        dve_took, pool_took, sp_took = sem("dve_took"), sem("pool_took"), sem("sp_took")
        sums_done = sems("sums_done")
        x_in, ctx_in, mask_in, x_out = sems("x_in"), sems("ctx_in"), sems("mask_in"), sems("x_out")
        mask_bias, mask_min, mask_scale = sems("mask_bias"), sems("mask_min"), sems("mask_scale")
        kT_done, v_done, kvtail_done, vtail_done = sems("kT_done"), sems("v_done"), sems("kvtail_done"), sems("vtail_done")
        stats_done, mean_done, eps_done, rstd_done = sems("stats_done"), sems("mean_done"), sems("eps_done"), sems("rstd_done")
        xn_done, xnT_done, xnR_done = sems("xn_done"), sems("xnT_done"), sems("xnR_done")
        q_done, bx_done, qk_done = sems("q_done"), sems("bx_done"), sems("qk_done")
        bq_done, kb_done, vb_done = sems("bq_done"), sems("kb_done"), sems("vb_done")
        max_done, exp_done = sems("max_done"), sems("exp_done")
        pt_act, pt_vec, pv_done, tail_done = sems("pt_act"), sems("pt_vec"), sems("pv_done"), sems("tail_done")
        attn_done, rsum_done, wsel_done, on_done, oT_done = (
            sems("attn_done"), sems("rsum_done"), sems("wsel_done"), sems("on_done"), sems("oT_done"))
        x_done, xpb_done = sems("x_done"), sems("xpb_done")
        p4_done, lines_step, lss_done, lrn_done, lT_done, lq_done = (
            sems("p4_done"), sems("lines_step"), sems("lss_done"), sems("lrn_done"), sems("lT_done"), sems("lq_done"))
        soft, sexp_done, spt_done = sems("softmax_step"), sems("sexp_done"), sems("spt_done")
        route_step, gate_exp, comb_done, comT_done = sems("route_step"), sems("gate_exp"), sems("comb_done"), sems("comT_done")
        th_done, t_done, h_vec, h_act = sems("th_done"), sems("t_done"), sems("h_vec"), sems("h_act")
        bank_full = [sem(f"bank_full{k}") for k in range(ring)]

        block = ctx.enter_context(nc.Block())

        def at(i, l, n, k):
            return i * (2 * n) + (l * n + k)

        def wait(eng, semaphore, value):
            if not (isinstance(value, int) and value <= 0):
                eng.wait_ge(semaphore, value)

        def group(p, step):
            return p - behind_by(step)

        def there(p, step):
            return not isinstance(p, int) or 0 <= group(p, step) < turns

        def steps(eng, p):
            for n, step in enumerate(order):
                if not isinstance(p, int) and n % FRESH == 0:
                    own = eng.alloc_register()
                    eng.reg_mov(own, p)
                    p = eng.snap(own, donate=True, min_val=2, max_val=turns - 1)
                if there(p, step):
                    yield step, group(p, step) if behind_by(step) else p

        def wait_full(eng, i, step):
            p = i + behind_by(step) if behind_by(step) else i
            mine = bank_fills[bank_of[step]]
            n = mine.index(step)
            if isinstance(p, int):
                value = sum(there(q, x) for q in range(p) for x in mine) + sum(there(p, x) for x in mine[:n + 1])
                eng.wait_ge(bank_full[bank_of[step]], value)
            else:
                missing = sum(behind_by(x) for x in mine)
                eng.wait_ge(bank_full[bank_of[step]], i * len(mine) + (behind_by(step) * len(mine) + n + 1 - missing))

        def read(step):
            kind, s, l, m = step
            return {
                "kproj": (kT_done[s], 4, 2 * l + m + 1), "vproj": (v_done[s], 4, m + 1),
                "kvtail": (kvtail_done[s], 3, 3), "lnT": (xnT_done[s], 6, 3 * l + m + 1),
                "qproj": (q_done[s], 2, l + 1),
                "scores": (max_done[s], 2 * U, m + 1) if l == 0 else (exp_done[s], 2 * U, U + m + 1),
                "ptrans": (pt_act[s] if m % 2 else pt_vec[s], U // 2, l * U // 4 + m // 2 + 1),
                "tailT": (tail_done[s], 2, l + 1), "oT": (oT_done[s], 4, 2 * l + m + 1),
                "oproj": (x_done[s], 21, 10 * l + m + 1), "qk": (qk_done[s], 4, 2 * l + 2),
                "vrep": (vb_done[s], 2, l + 1), "lines": (p4_done[s], 1, 1), "linesT": (lT_done[s], 1, 1),
                "jlines": (lq_done[s], 2, 2), "sscore": (soft[s], 7, 1 + 3 * l),
                "sptrans": (spt_done[s], 2, l + 1), "route": (gate_exp[s], 2, l + 1),
                "up": ((h_vec[s], 12, m + 1) if l == 0 else (h_act[s], 4, m // 2 + 1) if m % 2 else
                       (h_vec[s], 12, 8 + m // 2 + 1)),
                "down": (x_done[s], 21, 10 * l + 3 + m), "wT": (comT_done[s], 1, 1), "wb2": (x_done[s], 21, 21),
            }[kind]

        def pt_ready(i, s, l, m):
            semaphore, n, k = read(("ptrans", s, l, m))
            return semaphore, i * n + k

        def wait_empty(eng, i, step):
            mine = bank_fills[bank_of[step]]
            n = mine.index(step)
            p = i + behind_by(step) if behind_by(step) else i
            back = 0
            while True:
                n -= 1
                if n < 0:
                    n, back = len(mine) - 1, back + 1
                if isinstance(p, int) and p - back < 0:
                    return
                if not isinstance(p, int) or there(p - back, mine[n]):
                    break
            held = mine[n]
            ahead = behind_by(step) - behind_by(held) - back
            semaphore, inc, k = read(held)
            eng.wait_ge(semaphore, i * inc + (ahead * inc + k))

        @block.sync
        def _(sp):
            for dst, src in ((cst[:, :], const_d), (bcol[:, :], bcol_d), (brow[:, :], brow_d), (wsq[:, :], wsq_d),
                             (b2[:, :], b2_d)):
                sp.dma_start(dst, src).then_inc(constants_in, 16)

            def wait_own(semaphore, value):
                wait(sp, semaphore, value)
                sp.sem_inc(sp_took, 1)

            def load_ctx(i, s):
                wait_own(kvtail_done[s], i * 3)
                wait_own(v_done[s], i * 4)
                wait_own(kT_done[s], i * 4)
                sp.dma_start(ctxT[s][:, :], ctx_d[i * STREAMS + s]).then_inc(ctx_in[s], 16)

            def load_x(i, s):
                wait_own(xpb_done[s], i * 4 - 3)
                wait_own(xn_done[s], i * 6 - 5)
                sp.dma_start(xin[s][:, :], x_d[i * STREAMS + s]).then_inc(x_in[s], 16)

            def load_mask(i, s):
                wait_own(max_done[s], i * (2 * U) - U)
                for j in range(J):
                    sp.dma_start(maskb[s][32 * j:32 * j + 32, :, :],
                                 mask_d[i * STREAMS + s].rearrange("b q k -> q b k")).then_inc(mask_in[s], 16)

            def load(i):
                for s in range(0, STREAMS, 2):
                    load_ctx(i, s)
                for s in range(1, STREAMS, 2):
                    load_ctx(i, s)
                    load_x(i, s)
                    load_mask(i, s)
                for s in range(0, STREAMS, 2):
                    load_x(i, s)
                    load_mask(i, s)

            load(0)
            for dst, src in ((w13[:, :, :], w13_d), (w2a[:, :, :, :], w2a_d), (w1[:, :, :], w1_d),
                             (w2b[:, :, :, :], w2b_d)):
                sp.dma_start(dst, src).then_inc(experts_in, 16)
            with sp.Fori(1, turns) as i:
                load(i)
            for s in range(STREAMS):
                sp.wait_ge(x_out[s], turns * 16)

        @block.gpsimd
        def _(pool):
            pool.wait_ge(constants_in, 16 * SETUP_LOADS)
            nc.gpsimd.tensor_scalar(jscaled[:, :], c("jmat", 96), bc("plucker", 96), None,
                                    ALU.mult).then_inc(jscaled_done, 1)

            def taken():
                pool.sem_inc(pool_took, 1)

            def run_pass(p):
                for (kind, s, l, m), i in steps(pool, p):
                    if kind == "mask":
                        pool.wait_ge(mask_in[s], i * 64 + 64)
                        taken()
                        nc.gpsimd.tensor_scalar(mbias[s], maskb[s][:, :, :], 0, BIG, ALU.is_equal,
                                                ALU.mult).then_inc(mask_bias[s], 1)
                    elif kind == "ln":
                        pool.wait_ge(mean_done[s], at(i, l, 3, m + 1))
                        nc.gpsimd.tensor_tensor(veps[s][:, :], mv[s][:, 1:2], c("eps"), ALU.add).then_inc(eps_done[s], 1)
                        pool.wait_ge(eps_done[s], at(i, l, 3, m + 1))
                        nc.gpsimd.tensor_tensor(rstd[s][:, :], veps[s][:, :], c("mhalf"),
                                                ALU.pow).then_inc(rstd_done[s], 1)
                    elif kind == "xpb":
                        if (l, m) == (0, 0):
                            pool.wait_ge(x_in[s], i * 16 + 16)
                        else:
                            pool.wait_ge(x_done[s], i * 21 + (10 * l + m))
                        src = xin[s] if (l, m) == (0, 0) else xs[s]
                        row = BROW[("o" if m == 0 else "so") + str(l)]
                        nc.gpsimd.tensor_tensor(xpb[s][:, :], src[:, :], brow[:, row:row + D],
                                                ALU.add).then_inc(xpb_done[s], 1)
                    elif kind == "bq":
                        pool.wait_ge(q_done[s], at(i, l, 1, 1))
                        if m > 1:
                            pool.wait_ge(max_done[s], at(i, l, U, NGR * (m - 1)))
                        nc.gpsimd.tensor_tensor(
                            BX[s][:, m % 2, :, :], qs[s][:, 32 * m:32 * m + 32].unsqueeze(1).broadcast_to((128, H, S)),
                            c(f"head_x{l}").unsqueeze(2).broadcast_to((128, H, S)), ALU.mult).then_inc(bx_done[s], 1)
                    elif kind == "lines":
                        pool.wait_ge(p4_done[s], i + 1)
                        nc.gpsimd.tensor_tensor(pa[s][:, :], p4[s][:, 0, :], p4[s][:, 1, :],
                                                ALU.mult).then_inc(lines_step[s], 1)
                        nc.gpsimd.tensor_tensor(pb[s][:, :], p4[s][:, 2, :], p4[s][:, 3, :],
                                                ALU.mult).then_inc(lines_step[s], 1)
                        pool.wait_ge(lines_step[s], i * 6 + 2)
                        nc.gpsimd.tensor_tensor(ln6[s][:, :], pa[s][:, :], pb[s][:, :],
                                                ALU.subtract).then_inc(lines_step[s], 1)
                        pool.wait_ge(lines_step[s], i * 6 + 3)
                        nc.gpsimd.tensor_tensor(lsq[s][:, :], ln6[s][:, :], ln6[s][:, :],
                                                ALU.mult).then_inc(lines_step[s], 1)
                    elif kind == "linesN":
                        pool.wait_ge(lss_done[s], i + 1)
                        nc.gpsimd.tensor_tensor(lnn[s][:, :], lss[s][:, :], c("half").broadcast_to((128, H)),
                                                ALU.pow).then_inc(lines_step[s], 1)
                    elif kind == "linesU":
                        pool.wait_ge(lrn_done[s], i * 2 + 2)
                        nc.gpsimd.tensor_tensor(pa[s][:, :].rearrange("p (h c) -> p h c", c=6),
                                                ln6[s][:, :].rearrange("p (h c) -> p h c", c=6),
                                                lrn[s][:, :].unsqueeze(2).broadcast_to((128, H, 6)),
                                                ALU.mult).then_inc(lines_step[s], 1)

            run_pass(0)
            run_pass(1)
            with pool.Fori(2, turns) as p:
                run_pass(p)
            run_pass(turns)

        @block.tensor
        def _(pe):
            pe.wait_ge(constants_in, 16 * SETUP_LOADS)
            pe.wait_ge(jscaled_done, 1)

            def run_pass(p):
                for step, i in steps(pe, p):
                    kind, s, l, m = step
                    if kind in FILLS:
                        ps = bank[bank_of[step]]
                        wait_empty(pe, i, step)
                        full = bank_full[bank_of[step]]
                    if kind == "kproj":
                        pe.wait_ge(ctx_in[s], i * 16 + 16)
                        nc.tensor.matmul(ps[:, :], w(f"k{l}"), ctxT[s][:, m * 512:m * 512 + 512],
                                         start=True, stop=True).then_inc(full, 1)
                    elif kind == "vproj":
                        pe.wait_ge(ctx_in[s], i * 16 + 16)
                        for k in range(2):
                            a = (2 * m + k) * 128
                            ins = nc.tensor.matmul(ps[:, k * 256:k * 256 + 256], ctxT[s][:, a:a + 128], w("v01"),
                                                   start=True, stop=True)
                        ins.then_inc(full, 1)
                    elif kind == "kvtail":
                        pe.wait_ge(ctx_in[s], i * 16 + 16)
                        t = GB * KM
                        nc.tensor.matmul(ps[:, 0:4], w("k0"), ctxT[s][:, t:t + GB], start=True, stop=True)
                        nc.tensor.matmul(ps[:, 4:8], w("k1"), ctxT[s][:, t:t + GB], start=True, stop=True)
                        nc.tensor.matmul(ps[0:U, 16:16 + 256], ctxT[s][:, t + GB:t + GB + U], w("v01"),
                                         start=True, stop=True).then_inc(full, 1)
                    elif kind == "lnT":
                        pe.wait_ge(xn_done[s], at(i, l, 3, m + 1))
                        nc.tensor.transpose(ps[:, 0:128], xn[s][:, :], ident).then_inc(full, 1)
                    elif kind == "qproj":
                        pe.wait_ge(xnT_done[s], at(i, l, 3, 1))
                        nc.tensor.matmul(ps[:, 0:128], w(f"q{l}"), xnT[s][:, :], start=True,
                                         stop=True).then_inc(full, 1)
                    elif kind == "scores":
                        b, g = divmod(m, NGR)
                        if m == 0:
                            pe.wait_ge(kT_done[s], i * 4 + 2 * l + 2)
                            pe.wait_ge(kvtail_done[s], i * 3 + 3)
                        if g == 0:
                            pe.wait_ge(bx_done[s], at(i, l, GB, b + 1))
                        nc.tensor.matmul(ps[:, 0:SK], BX[s][:, b % 2, J * g:J * g + J, :], KT[s][:, l, b, :],
                                         start=True, stop=True).then_inc(full, 1)
                    elif kind == "ptrans":
                        pe.wait_ge(exp_done[s], at(i, l, U, 2 * m + 2))
                        for k in range(4):
                            ins = nc.tensor.transpose(
                                ps[:, k * 128:k * 128 + 128],
                                P[s][:, 2 * m + k // 2, (k % 2) * 128:(k % 2) * 128 + 128], ident)
                        ins.then_inc(full, 1)
                    elif kind == "pv":
                        pe.wait_ge(*pt_ready(i, s, l, m))
                        if m == 0:
                            wait(pe, on_done[s], at(i, l, 2, 0))
                            pe.wait_ge(v_done[s], i * 4 + 4)
                        for k in range(4):
                            u = 2 * m + k // 2
                            b, g = divmod(u, NGR)
                            ins = nc.tensor.matmul(attn_out[s][:, u * 32:u * 32 + 32],
                                                   PT[s][:, m % 2, k * 128:k * 128 + 128],
                                                   V[s][:, 2 * b + k % 2, l, 32 * g:32 * g + 32],
                                                   start=(m == 0 and k == 0), stop=False, skip_group_check=True)
                        ins.then_inc(pv_done[s], 1)
                    elif kind == "tailT":
                        pe.wait_ge(exp_done[s], at(i, l, U, U))
                        nc.tensor.transpose(ps[0:U, 0:128], P[s][:, :, KM], ident).then_inc(full, 1)
                    elif kind == "tailV":
                        pe.wait_ge(tail_done[s], at(i, l, 1, 1))
                        pe.wait_ge(vtail_done[s], i + 1)
                        nc.tensor.matmul(attn_out[s][:, :], tT[s][:, :], vtb[s][:, l, :], start=False, stop=True,
                                         skip_group_check=True).then_inc(attn_done[s], 1)
                    elif kind == "oT":
                        pe.wait_ge(on_done[s], at(i, l, 2, m + 1))
                        for b in range(GB):
                            ins = nc.tensor.matmul(ps[:, 32 * b:32 * b + 32], On[s][:, 128 * b:128 * b + 128],
                                                   c("fold"), start=True, stop=True)
                        ins.then_inc(full, 1)
                    elif kind == "oproj":
                        pe.wait_ge(oT_done[s], at(i, l, 2, m + 1))
                        nc.tensor.matmul(ps[:, 0:128], OT[s][:, :], w(f"{'o' if m == 0 else 'so'}{l}"),
                                         start=True, stop=True).then_inc(full, 1)
                    elif kind == "qk":
                        pe.wait_ge(xnT_done[s], at(i, l, 3, 2))
                        nc.tensor.matmul(ps[:, 0:128], w(f"sq{l}"), xnT[s][:, :], start=True, stop=True)
                        nc.tensor.matmul(ps[:, 128:256], w(f"sk{l}"), xnT[s][:, :], start=True,
                                         stop=True).then_inc(full, 1)
                    elif kind == "vrep":
                        pe.wait_ge(xnR_done[s], at(i, l, 1, 1))
                        for b in range(GB):
                            ins = nc.tensor.matmul(ps[:, 128 * b:128 * b + 128], xnR[s][:, b, :, :], w(f"sv{l}"),
                                                   start=True, stop=True)
                        ins.then_inc(full, 1)
                    elif kind == "lines":
                        pe.wait_ge(xnT_done[s], at(i, l, 3, 2))
                        nc.tensor.matmul(ps[:, 0:384], xnT[s][:, :], w("p4"), start=True,
                                         stop=True).then_inc(full, 1)
                    elif kind == "linesT":
                        pe.wait_ge(lines_step[s], i * 6 + 6)
                        nc.tensor.transpose(ps[0:96, 0:128], pa[s][:, :], ident).then_inc(full, 1)
                    elif kind == "jlines":
                        pe.wait_ge(lT_done[s], i + 1)
                        nc.tensor.matmul(ps[0:96, 0:128], jscaled[:, :], lT[s][:, :], start=True,
                                         stop=True).then_inc(full, 1)
                    elif kind == "sscore":
                        pe.wait_ge(bq_done[s], at(i, l, 1, 1))
                        pe.wait_ge(kb_done[s], at(i, l, 1, 1))
                        if l == 0:
                            pe.wait_ge(lq_done[s], i * 2 + 2)
                        for b in range(GB):
                            o = ps[:, 128 * b:128 * b + 128]
                            ins = nc.tensor.matmul(o, BQ[s][:, b, :, :], KB[s][:, b, :, :], start=True, stop=(l == 1))
                            if l == 0:
                                ins = nc.tensor.matmul(o, LQ[s][:, b, :, :], LK[s][:, b, :, :], start=False,
                                                       stop=True)
                        ins.then_inc(full, 1)
                    elif kind == "sptrans":
                        pe.wait_ge(sexp_done[s], at(i, l, 1, 1))
                        for b in range(GB):
                            ins = nc.tensor.transpose(ps[:, 128 * b:128 * b + 128], sP[s][:, 4 * b:4 * b + 4, :],
                                                      ident)
                        ins.then_inc(full, 1)
                    elif kind == "spv":
                        pe.wait_ge(spt_done[s], at(i, l, 1, 1))
                        pe.wait_ge(vb_done[s], at(i, l, 1, 1))
                        pe.wait_ge(on_done[s], at(i, l, 2, 1))
                        for b in range(GB):
                            ins = nc.tensor.matmul(attn_out[s][:, 128 * b:128 * b + 128], sS[s][:, 4 * b:4 * b + 4, :],
                                                   VB[s][:, b, :, :], start=True, stop=True)
                        ins.then_inc(attn_done[s], 1)
                    elif kind == "route":
                        pe.wait_ge(xnT_done[s], at(i, l, 3, 3))
                        nc.tensor.matmul(ps[:, 0:E_N], xnT[s][:, :], w(f"gate{l}"), start=True,
                                         stop=True).then_inc(full, 1)
                    elif kind == "up":
                        if m == 0:
                            pe.wait_ge(xnT_done[s], at(i, l, 3, 3))
                        if isinstance(i, int) and m == 0:
                            pe.wait_ge(experts_in, 16 * EXPERT_LOADS)
                        wt = w13 if l == 0 else w1
                        for k in range(4):
                            ins = nc.tensor.matmul(ps[:, k * 128:k * 128 + 128], wt[:, m, k * 128:k * 128 + 128],
                                                   xnT[s][:, :], start=True, stop=True)
                        ins.then_inc(full, 1)
                    elif kind == "down":
                        wt, nk = (w2a, 2) if l == 0 else (w2b, 4)
                        semaphore, n, k = read(("up", s, l, m))
                        pe.wait_ge(semaphore, i * n + k)
                        for k in range(nk):
                            ins = nc.tensor.matmul(ps[:, 0:128], HT[s][m % SLOTS][:, k * 128:k * 128 + 128],
                                                   wt[:, m, k, :], start=(k == 0), stop=(k == nk - 1))
                        ins.then_inc(full, 1)
                    elif kind == "wT":
                        pe.wait_ge(comb_done[s], at(i, 1, 1, 1))
                        nc.tensor.transpose(ps[0:E_N, 0:128], comb[s][:, :], ident).then_inc(full, 1)
                    elif kind == "wb2":
                        pe.wait_ge(comT_done[s], i + 1)
                        nc.tensor.matmul(ps[:, 0:128], comT[s][:, :], b2[:, :], start=True,
                                         stop=True).then_inc(full, 1)

            run_pass(0)
            run_pass(1)
            with pe.Fori(2, turns) as p:
                run_pass(p)
            run_pass(turns)

        @block.scalar
        def _(act):
            act.wait_ge(constants_in, 16 * SETUP_LOADS)

            def run_pass(p):
                for step, i in steps(act, p):
                    kind, s, l, m = step
                    if kind in FILLS:
                        ps = bank[bank_of[step]]
                    if kind == "kproj":
                        wait_full(act, i, step)
                        nc.scalar.activation(KT[s][:, l, 2 * m:2 * m + 2, 0:KM],
                                             ps[:, :].rearrange("p (b k) -> p b k", b=2), ACT.Identity,
                                             bias=bc(f"bk{l}")).then_inc(kT_done[s], 1)
                    elif kind == "vproj":
                        wait_full(act, i, step)
                        nc.scalar.copy(V[s][:, 2 * m:2 * m + 2, :, :], ps[:, :]).then_inc(v_done[s], 1)
                    elif kind == "lnT":
                        wait_full(act, i, step)
                        nc.scalar.copy(xnT[s][:, :], ps[:, 0:128]).then_inc(xnT_done[s], 1)
                    elif kind == "xnR":
                        act.wait_ge(xnT_done[s], at(i, l, 3, 2))
                        nc.scalar.copy(xnR[s], xnT[s][:, :].rearrange("p (b s) -> p b s", b=GB).unsqueeze(2)
                                       .broadcast_to((128, GB, NGR, S))).then_inc(xnR_done[s], 1)
                    elif kind == "qproj":
                        wait_full(act, i, step)
                        nc.scalar.activation(qs[s][:, 0:128], ps[:, 0:128], ACT.Identity,
                                             bias=bc(f"bq{l}")).then_inc(q_done[s], 1)
                    elif kind == "scores":
                        act.wait_ge(max_done[s], at(i, l, U, m + 1))
                        if l == 0:
                            nc.scalar.activation(P[s][:, m, :], P[s][:, m, :], ACT.Exp, bias=nmax[s][:, m:m + 1],
                                                 scale=-1.0, accum_out=sums[s][:, m:m + 1]).then_inc(exp_done[s], 1)
                        else:
                            nc.scalar.activation(P[s][:, m, :], ps[:, 0:SK], ACT.Exp, bias=nmax[s][:, m:m + 1],
                                                 accum_out=sums[s][:, m:m + 1]).then_inc(exp_done[s], 1)
                    elif kind == "ptrans" and m % 2:
                        wait_full(act, i, step)
                        if m >= 2:
                            act.wait_ge(pv_done[s], at(i, l, U // 2, m - 1))
                        nc.scalar.copy(PT[s][:, 1, :], ps[:, :]).then_inc(pt_act[s], 1)
                    elif kind == "tailT":
                        wait_full(act, i, step)
                        nc.scalar.copy(tT[s][:, :], ps[0:U, 0:128]).then_inc(tail_done[s], 1)
                    elif kind == "oT":
                        wait_full(act, i, step)
                        nc.scalar.activation(OT[s][:, :], ps[:, 0:128], ACT.Identity,
                                             bias=bc(f"{'b' if m == 0 else 's'}v{l}")).then_inc(oT_done[s], 1)
                    elif kind == "qk":
                        wait_full(act, i, step)
                        nc.scalar.activation(qs[s][:, 0:128], ps[:, 0:128], ACT.Identity,
                                             bias=bc(f"sq{l}")).then_inc(qk_done[s], 1)
                        nc.scalar.activation(qs[s][:, 128:256], ps[:, 128:256], ACT.Identity,
                                             bias=bc(f"sk{l}")).then_inc(qk_done[s], 1)
                    elif kind == "lines":
                        wait_full(act, i, step)
                        nc.scalar.copy(p4[s][:, :, :], ps[:, 0:384]).then_inc(p4_done[s], 1)
                    elif kind == "linesT":
                        wait_full(act, i, step)
                        nc.scalar.copy(lT[s][:, :], ps[0:96, 0:128]).then_inc(lT_done[s], 1)
                    elif kind == "sscore":
                        act.wait_ge(soft[s], i * 7 + 3 + 4 * l)
                        nc.scalar.activation(sP[s][:, :, :], sS[s][:, :, :], ACT.Exp).then_inc(sexp_done[s], 1)
                    elif kind == "sptrans":
                        wait_full(act, i, step)
                        nc.scalar.copy(sS[s][:, :, :], ps[:, :]).then_inc(spt_done[s], 1)
                    elif kind == "route":
                        act.wait_ge(route_step[s], i * ROUTE_N + (1 if l == 0 else ROUTE_0 + 2))
                        src = ps[:, 0:E_N] if l == 0 else sc[s][:, :]
                        nc.scalar.activation(sc2[s][:, :], src, ACT.Exp,
                                             bias=col[s][:, 0:1]).then_inc(gate_exp[s], 1)
                    elif kind == "up":
                        wait_full(act, i, step)
                        if l == 0:
                            if m >= SLOTS:
                                act.wait_ge(t_done[s], i * 8 + m - SLOTS + 1)
                            nc.scalar.activation(th[s][m % SLOTS], ps[:, 0:256], ACT.Tanh,
                                                 scale=0.5).then_inc(th_done[s], 1)
                        elif m % 2:
                            if m >= SLOTS:
                                act.wait_ge(x_done[s], i * 21 + 13 + m - SLOTS)
                            for k in range(4):
                                n = len(BCOL) + 4 * m + k
                                ins = nc.scalar.activation(HT[s][m % SLOTS][:, k * 128:k * 128 + 128],
                                                           ps[:, k * 128:k * 128 + 128], ACT.Relu,
                                                           bias=bcol[:, n:n + 1])
                            ins.then_inc(h_act[s], 1)
                    elif kind == "store":
                        act.wait_ge(x_done[s], i * 21 + 21)
                        act.dma_start(out_d[i * STREAMS + s], xs[s][:, :]).then_inc(x_out[s], 16)
                    elif kind == "wT":
                        wait_full(act, i, step)
                        nc.scalar.copy(comT[s][:, :], ps[0:E_N, 0:128]).then_inc(comT_done[s], 1)

            run_pass(0)
            run_pass(1)
            with act.Fori(2, turns) as p:
                run_pass(p)
            run_pass(turns)

        @block.vector
        def _(dve):
            dve.wait_ge(constants_in, 16 * SETUP_LOADS)

            def taken():
                dve.sem_inc(dve_took, 1)

            def ranks(i, s, start, src, n, const):
                a = src.unsqueeze(1).broadcast_to((128, n, n))
                b = src.unsqueeze(2).broadcast_to((128, n, n))
                cm = cmp8[s][:, 0:n, :, 0:n]
                nc.vector.tensor_tensor(cm[:, :, 0, :], a, b, ALU.is_ge)
                nc.vector.tensor_tensor(cm[:, :, 1, :], a, b, ALU.is_gt).then_inc(route_step[s], 1)
                dve.wait_ge(route_step[s], start + 1)
                nc.vector.tensor_tensor(cm, cm, c(const).rearrange("p (e a f) -> p e a f", e=n, a=2),
                                        ALU.mult).then_inc(route_step[s], 1)
                dve.wait_ge(route_step[s], start + 2)
                nc.vector.tensor_reduce(rank[s][:, 0:n], cm, mybir.AxisListType.XY, ALU.add).then_inc(route_step[s], 1)
                dve.wait_ge(route_step[s], start + 3)

            def run_pass(p):
                for step, i in steps(dve, p):
                    kind, s, l, m = step
                    if kind in FILLS:
                        ps = bank[bank_of[step]]
                    if kind == "mask":
                        dve.wait_ge(mask_bias[s], i + 1)
                        nc.vector.tensor_reduce(mmin[s][:, :], mbias[s], X, ALU.min).then_inc(mask_min[s], 1)
                        dve.wait_ge(mask_min[s], i + 1)
                        nc.vector.tensor_scalar(mscale[s][:, :], mmin[s][:, :], 1.0, 1.0, ALU.is_lt,
                                                ALU.add).then_inc(mask_scale[s], 1)
                    elif kind == "kvtail":
                        wait_full(dve, i, step)
                        for k in range(2):
                            nc.vector.tensor_scalar(KT[s][:, k, :, KM], ps[:, 4 * k:4 * k + 4], bc(f"bk{k}"), None,
                                                    ALU.add).then_inc(kvtail_done[s], 1)
                        nc.vector.tensor_copy(vtl[s][:, :, :], ps[0:U, 16:272]).then_inc(kvtail_done[s], 1)
                        dve.wait_ge(kvtail_done[s], i * 3 + 3)
                        for k in range(2):
                            ins = nc.vector.tensor_tensor(
                                vtb[s][:, k, :].rearrange("p (b f) -> p b f", b=GB),
                                vtl[s][:, k, :].unsqueeze(1).broadcast_to((U, GB, 128)),
                                c("tail_block", U).rearrange("p (b f) -> p b f", b=GB), ALU.mult)
                        ins.then_inc(vtail_done[s], 1)
                    elif kind == "ln":
                        src = xin[s] if (l, m) == (0, 0) else xs[s]
                        if (l, m) == (0, 0):
                            dve.wait_ge(x_in[s], i * 16 + 16)
                        else:
                            dve.wait_ge(x_done[s], i * 21 + (10 * l + m))
                        nc.vector.bn_stats(st6[s][:, :], src[:, :]).then_inc(stats_done[s], 1)
                        dve.wait_ge(stats_done[s], at(i, l, 3, m + 1))
                        taken()
                        nc.vector.bn_aggr(mv[s][:, :], st6[s][:, :]).then_inc(mean_done[s], 1)
                    elif kind == "lnT":
                        src = xin[s] if (l, m) == (0, 0) else xs[s]
                        dve.wait_ge(rstd_done[s], at(i, l, 3, m + 1))
                        nc.vector.tensor_scalar(xn[s][:, :], src[:, :], mv[s][:, 0:1], rstd[s][:, 0:1], ALU.subtract,
                                                ALU.mult).then_inc(xn_done[s], 1)
                    elif kind == "qk":
                        dve.wait_ge(qk_done[s], at(i, l, 2, 1))
                        nc.vector.tensor_tensor(
                            BQ[s],
                            qs[s][:, 0:128].rearrange("p (b s) -> p b s", b=GB).unsqueeze(2).broadcast_to((128, GB, J, S)),
                            c("head_q").unsqueeze(1).unsqueeze(3).broadcast_to((128, GB, J, S)),
                            ALU.mult).then_inc(bq_done[s], 1)
                        dve.wait_ge(qk_done[s], at(i, l, 2, 2))
                        nc.vector.tensor_tensor(
                            KB[s],
                            qs[s][:, 128:256].rearrange("p (b s) -> p b s", b=GB).unsqueeze(2)
                            .broadcast_to((128, GB, NGR, S)),
                            c("quad").unsqueeze(1).unsqueeze(3).broadcast_to((128, GB, NGR, S)),
                            ALU.mult).then_inc(kb_done[s], 1)
                    elif kind == "scores":
                        wait_full(dve, i, step)
                        if l == 0:
                            if m == 0:
                                dve.wait_ge(mask_scale[s], i + 1)
                            taken()
                            b = m // NGR
                            nc.vector.tensor_tensor_reduce(P[s][:, m, :], ps[:, 0:SK], mbias[s][:, b, :],
                                                           mscale[s][:, b:b + 1], LOWEST, ALU.add, ALU.min,
                                                           nmax[s][:, m:m + 1]).then_inc(max_done[s], 1)
                        else:
                            nc.vector.tensor_reduce(nmax[s][:, m:m + 1], ps[:, 0:SK], X, ALU.max,
                                                    negate=True).then_inc(max_done[s], 1)
                    elif kind == "ptrans" and m % 2 == 0:
                        wait_full(dve, i, step)
                        if m >= 2:
                            dve.wait_ge(pv_done[s], at(i, l, U // 2, m - 1))
                        nc.vector.tensor_copy(PT[s][:, 0, :], ps[:, :]).then_inc(pt_vec[s], 1)
                    elif kind == "sel":
                        if m == 0:
                            dve.wait_ge(exp_done[s], at(i, l, U, U))
                        else:
                            dve.wait_ge(sexp_done[s], at(i, l, 1, 1))
                            nc.vector.tensor_reduce(sums[s][:, :], sP[s][:, :, :], X, ALU.add).then_inc(sums_done[s], 1)
                            dve.wait_ge(sums_done[s], at(i, l, 1, 1))
                        nc.vector.reciprocal(rsum[s][:, :], sums[s][:, :]).then_inc(rsum_done[s], 1)
                        dve.wait_ge(rsum_done[s], at(i, l, 2, m + 1))
                        nc.vector.tensor_tensor(wsel[s][:, :, :], rsum[s][:, :].unsqueeze(2).broadcast_to((128, U, J)),
                                                c("quad").unsqueeze(1).broadcast_to((128, U, J)),
                                                ALU.mult).then_inc(wsel_done[s], 1)
                    elif kind == "norm":
                        dve.wait_ge(wsel_done[s], at(i, l, 2, m + 1))
                        dve.wait_ge(attn_done[s], at(i, l, 2, m + 1))
                        nc.vector.tensor_tensor(On[s][:, :].rearrange("p (u d) -> p u d", d=DH),
                                                attn_out[s][:, :].rearrange("p (u d) -> p u d", d=DH),
                                                wsel[s][:, :, :].rearrange("p u j -> p (u j)").unsqueeze(2)
                                                .broadcast_to((128, U * J, DH)), ALU.mult).then_inc(on_done[s], 1)
                    elif kind == "oproj":
                        wait_full(dve, i, step)
                        dve.wait_ge(xpb_done[s], at(i, l, 2, m + 1))
                        if (l, m) == (0, 0):
                            wait(dve, x_out[s], i * 16)
                        nc.vector.tensor_tensor(xs[s][:, :], ps[:, 0:128], xpb[s][:, :], ALU.add).then_inc(x_done[s], 1)
                    elif kind == "vrep":
                        wait_full(dve, i, step)
                        nc.vector.tensor_tensor(VB[s][:, :, :, :], ps[:, :].rearrange("p (b g f) -> p b g f", b=GB, g=NGR),
                                                c("quad").unsqueeze(1).unsqueeze(3).broadcast_to((128, GB, NGR, 32)),
                                                ALU.mult).then_inc(vb_done[s], 1)
                    elif kind == "linesN":
                        dve.wait_ge(lines_step[s], i * 6 + 4)
                        nc.vector.tensor_reduce(lss[s][:, :], lsq[s][:, :].rearrange("p (h c) -> p h c", c=6), X,
                                                ALU.add).then_inc(lss_done[s], 1)
                    elif kind == "linesU":
                        dve.wait_ge(lines_step[s], i * 6 + 5)
                        nc.vector.tensor_scalar(lnn[s][:, :], lnn[s][:, :], 1e-12, None, ALU.max).then_inc(lrn_done[s], 1)
                        dve.wait_ge(lrn_done[s], i * 2 + 1)
                        nc.vector.reciprocal(lrn[s][:, :], lnn[s][:, :]).then_inc(lrn_done[s], 1)
                    elif kind == "linesT":
                        dve.wait_ge(lT_done[s], i + 1)
                        nc.vector.tensor_tensor(
                            LQ[s][:, :, :, :],
                            lT[s][:, :].rearrange("p (b s) -> p b s", b=GB).unsqueeze(2).broadcast_to((96, GB, J, S)),
                            c("head_p", 96).unsqueeze(1).unsqueeze(3).broadcast_to((96, GB, J, S)),
                            ALU.mult).then_inc(lq_done[s], 1)
                    elif kind == "jlines":
                        wait_full(dve, i, step)
                        nc.vector.tensor_tensor(
                            LK[s][:, :, :, :],
                            ps[0:96, 0:128].rearrange("p (b s) -> p b s", b=GB).unsqueeze(2)
                            .broadcast_to((96, GB, NGR, S)),
                            c("group_p", 96).unsqueeze(1).unsqueeze(3).broadcast_to((96, GB, NGR, S)),
                            ALU.mult).then_inc(lq_done[s], 1)
                    elif kind == "sscore":
                        wait_full(dve, i, step)
                        p3 = ps[:, :].rearrange("p (u k) -> p u k", k=S)
                        base = i * 7 + 3 * l
                        if l == 0:
                            nc.vector.tensor_tensor(sS[s][:, :, :], p3,
                                                    c("causal0").unsqueeze(1).broadcast_to((128, U, S)),
                                                    ALU.add).then_inc(soft[s], 1)
                        else:
                            nc.vector.tensor_tensor(sS[s][:, :, :], p3,
                                                    c("tril").unsqueeze(1).broadcast_to((128, U, S)),
                                                    ALU.mult).then_inc(soft[s], 1)
                            dve.wait_ge(soft[s], base + 1)
                            nc.vector.tensor_tensor(sS[s][:, :, :], sS[s][:, :, :],
                                                    c("causal1").unsqueeze(1).broadcast_to((128, U, S)),
                                                    ALU.add).then_inc(soft[s], 1)
                        dve.wait_ge(soft[s], base + 1 + l)
                        nc.vector.tensor_reduce(nmax[s][:, :], sS[s][:, :, :], X, ALU.max).then_inc(soft[s], 1)
                        dve.wait_ge(soft[s], base + 2 + l)
                        nc.vector.tensor_tensor(sS[s][:, :, :], sS[s][:, :, :],
                                                nmax[s][:, :].unsqueeze(2).broadcast_to((128, U, S)),
                                                ALU.subtract).then_inc(soft[s], 1)
                    elif kind == "route":
                        wait_full(dve, i, step)
                        base = i * ROUTE_N + l * ROUTE_0
                        if l == 0:
                            nc.vector.tensor_reduce(col[s][:, 0:1], ps[:, 0:E_N], X, ALU.max,
                                                    negate=True).then_inc(route_step[s], 1)
                        else:
                            nc.vector.tensor_tensor(sc[s][:, :], ps[:, 0:E_N],
                                                    brow[:, BROW["router"]:BROW["router"] + E_N],
                                                    ALU.add).then_inc(route_step[s], 1)
                            dve.wait_ge(route_step[s], base + 1)
                            nc.vector.tensor_reduce(col[s][:, 0:1], sc[s][:, :], X, ALU.max,
                                                    negate=True).then_inc(route_step[s], 1)
                    elif kind == "groups":
                        base = i * ROUTE_N
                        dve.wait_ge(gate_exp[s], at(i, l, 1, 1))
                        nc.vector.tensor_reduce(col[s][:, 1:2], sc2[s][:, :], X, ALU.add).then_inc(route_step[s], 1)
                        dve.wait_ge(route_step[s], base + 2)
                        nc.vector.reciprocal(col[s][:, 2:3], col[s][:, 1:2]).then_inc(route_step[s], 1)
                        dve.wait_ge(route_step[s], base + 3)
                        nc.vector.tensor_scalar(sc[s][:, :], sc2[s][:, :], col[s][:, 2:3], None,
                                                ALU.mult).then_inc(route_step[s], 1)
                        dve.wait_ge(route_step[s], base + 4)
                        nc.vector.tensor_reduce(gs[s][:, :], sc[s][:, :].rearrange("p (g e) -> p g e", e=2), X,
                                                ALU.max).then_inc(route_step[s], 1)
                        dve.wait_ge(route_step[s], base + 5)
                        ranks(i, s, base + 5, gs[s][:, :], 4, "order4")
                        nc.vector.tensor_scalar(gs[s][:, :], rank[s][:, 0:4], 2.0, None,
                                                ALU.is_lt).then_inc(route_step[s], 1)
                        dve.wait_ge(route_step[s], base + 9)
                        nc.vector.tensor_tensor(sc[s][:, :].rearrange("p (g e) -> p g e", e=2),
                                                sc[s][:, :].rearrange("p (g e) -> p g e", e=2),
                                                gs[s][:, :].unsqueeze(2).broadcast_to((128, 4, 2)),
                                                ALU.mult).then_inc(route_step[s], 1)
                    elif kind == "pick":
                        base = i * ROUTE_N + l * ROUTE_0
                        if l == 0:
                            dve.wait_ge(route_step[s], base + 10)
                            ranks(i, s, base + 10, sc[s][:, :], E_N, "order8")
                            nxt = base + 13
                            weights = sc[s]
                        else:
                            ranks(i, s, base + 2, sc[s][:, :], E_N, "order8")
                            dve.wait_ge(gate_exp[s], at(i, l, 1, 1))
                            nxt = base + 5
                            weights = sc2[s]
                        nc.vector.tensor_scalar(rank[s][:, :], rank[s][:, :], 2.0, None,
                                                ALU.is_lt).then_inc(route_step[s], 1)
                        dve.wait_ge(route_step[s], nxt + 1)
                        nc.vector.tensor_tensor(rank[s][:, :], rank[s][:, :], weights[:, :],
                                                ALU.mult).then_inc(route_step[s], 1)
                        dve.wait_ge(route_step[s], nxt + 2)
                        nc.vector.tensor_reduce(col[s][:, 1:2], rank[s][:, :], X, ALU.add).then_inc(route_step[s], 1)
                        dve.wait_ge(route_step[s], nxt + 3)
                        nc.vector.reciprocal(col[s][:, 2:3], col[s][:, 1:2]).then_inc(route_step[s], 1)
                        dve.wait_ge(route_step[s], nxt + 4)
                        nc.vector.tensor_scalar(comb[s][:, :], rank[s][:, :], col[s][:, 2:3], 0.5 if l == 0 else 1.0,
                                                ALU.mult, ALU.mult).then_inc(comb_done[s], 1)
                    elif kind == "up":
                        if l == 0:
                            dve.wait_ge(th_done[s], i * 8 + m + 1)
                            h = HT[s][m % SLOTS][:, 0:256]
                            if m >= SLOTS:
                                dve.wait_ge(x_done[s], i * 21 + 3 + m - SLOTS)
                            nc.vector.scalar_tensor_tensor(h, th[s][m % SLOTS], 1.0, ps[:, 0:256], ALU.add,
                                                           ALU.mult).then_inc(t_done[s], 1)
                            dve.wait_ge(t_done[s], i * 8 + m + 1)
                            nc.vector.tensor_tensor(h, h, ps[:, 256:512], ALU.mult).then_inc(h_vec[s], 1)
                        elif m % 2 == 0:
                            wait_full(dve, i, step)
                            if m >= SLOTS:
                                dve.wait_ge(x_done[s], i * 21 + 13 + m - SLOTS)
                            for k in range(4):
                                n = len(BCOL) + 4 * m + k
                                ins = nc.vector.tensor_scalar(HT[s][m % SLOTS][:, k * 128:k * 128 + 128],
                                                              ps[:, k * 128:k * 128 + 128], bcol[:, n:n + 1], 0.0,
                                                              ALU.add, ALU.max)
                            ins.then_inc(h_vec[s], 1)
                    elif kind == "down":
                        wait_full(dve, i, step)
                        if m == 0:
                            dve.wait_ge(comb_done[s], at(i, l, 1, 1))
                        dve.wait_ge(x_done[s], i * 21 + 10 * l + 2 + m)
                        nc.vector.scalar_tensor_tensor(xs[s][:, :], ps[:, 0:128], comb[s][:, m:m + 1], xs[s][:, :],
                                                       ALU.mult, ALU.add).then_inc(x_done[s], 1)
                    elif kind == "wb2":
                        wait_full(dve, i, step)
                        dve.wait_ge(x_done[s], i * 21 + 20)
                        nc.vector.tensor_tensor(xs[s][:, :], ps[:, 0:128], xs[s][:, :], ALU.add).then_inc(x_done[s], 1)

            run_pass(0)
            run_pass(1)
            with dve.Fori(2, turns) as p:
                run_pass(p)
            run_pass(turns)


ROUTE_0, ROUTE_N = 17, 17 + 9


def constants():
    import numpy as np
    k = np.zeros((128, NCONST), np.float32)
    p = np.arange(128)

    def put(name, value):
        a, b = CONST[name]
        value = np.asarray(value, np.float32)
        k[0:value.shape[0], a:b] = value.reshape(value.shape[0], -1)

    put("ident", np.eye(128))
    own = ((p % 32)[:, None] // DH == np.arange(J)) / np.sqrt(np.float32(DH))
    put("head_q", own)
    whole = (p[:, None] // DH == np.arange(H)) / np.sqrt(np.float32(DH))
    put("head_x0", -whole)
    put("head_x1", whole)
    put("quad", p[:, None] // 32 == np.arange(4))
    put("fold", p[:, None] % 32 == np.arange(32))
    tril = (np.arange(S)[None, :] <= (p % 32)[:, None]).astype(np.float32)
    put("tril", tril)
    put("causal0", (tril - 1.0) * np.float32(LOWEST))
    put("causal1", (tril - 1.0) * np.float32(1e10))
    for name, n in (("order8", E_N), ("order4", 4)):
        e, f = np.arange(n)[:, None], np.arange(n)[None, :]
        put(name, np.broadcast_to(np.stack([f < e, f > e], 1).reshape(1, -1), (128, 2 * n * n)))
    put("tail_block", np.arange(U)[:, None] == np.arange(512)[None, :] // 32)
    j6 = np.array([[0, 0, 0, 0, 0, 1], [0, 0, 0, 0, -1, 0], [0, 0, 0, 1, 0, 0], [0, 0, 1, 0, 0, 0],
                   [0, -1, 0, 0, 0, 0], [1, 0, 0, 0, 0, 0]], np.float32)
    put("jmat", np.kron(np.eye(H), j6.T))
    q = np.arange(96)
    put("head_p", (q % 24)[:, None] // 6 == np.arange(J))
    put("group_p", q[:, None] // 24 == np.arange(NGR))
    put("half", np.full((128, 1), 0.5))
    put("mhalf", np.full((128, 1), -0.5))
    put("eps", np.full((128, 1), EPS))
    return k


def kernel(**inputs):
    import numpy as np
    import concourse.bacc as bacc
    from concourse.bass_utils import run_bass_kernel_spmd

    a = {n: np.asarray(v) for n, v in inputs.items()}
    pi, pj = np.array([0, 0, 0, 1, 1, 2]), np.array([1, 2, 3, 2, 3, 3])
    head = np.arange(H)[:, None] * 3 * DH + np.arange(DH)
    part = [(head + k * DH).reshape(-1) for k in range(3)]
    w1a, b1a = a["L1_attn_W1"], a["L1_attn_b1"]
    wqkv, bqkv = a["L0_attn_Wqkv"], a["L0_attn_bqkv"]
    four = np.arange(H)[:, None] * 4
    p4 = [a[n][:, (four + k).reshape(-1)] for n, k in (("L0_attn_W1p", pi), ("L0_attn_W2p", pj), ("L0_attn_W1p", pj),
                                                      ("L0_attn_W2p", pi))]
    wsq = np.concatenate(
        [a["L0_xattn_Wq"].T, a["L0_xattn_Wk"].T, a["L1_xattn_W_q"].T, a["L1_xattn_W_k"].T, a["L0_xattn_Wv"].T,
         a["L1_xattn_W_v"].T, a["L0_xattn_Wo"].T, a["L1_xattn_W_o"].T,
         wqkv[:, 0:128], wqkv[:, 128:256], wqkv[:, 256:384], a["L0_attn_Wout"],
         w1a[:, part[0]], w1a[:, part[1]], w1a[:, part[2]], a["L1_attn_W2"], *p4, a["L0_ffn_gate_w"].T,
         a["L1_ffn_W_router"]], 1)
    bcol = np.concatenate(
        [np.stack([a["L0_xattn_bq"], a["L0_xattn_bk"], a["L0_xattn_bv"], a["L1_xattn_b_q"], a["L1_xattn_b_k"],
                   a["L1_xattn_b_v"], bqkv[0:128], bqkv[128:256], bqkv[256:384],
                   b1a[part[0]], b1a[part[1]], b1a[part[2]],
                   np.resize(np.repeat(a["L0_attn_plucker_scale"], 6), 128)], 1),
         a["L1_ffn_b1"].reshape(4 * E_N, 128).T], 1)
    brow = np.broadcast_to(np.concatenate([a["L0_xattn_bo"], a["L0_attn_bout"], a["L1_xattn_b_o"], a["L1_attn_b2"],
                                           a["L1_ffn_b_router"]])[None, :], (128, NBROW))
    cx = a["ctx_1024"].reshape(NG, GB, SK, D)
    tail = cx[:, :, KM, :].transpose(0, 2, 1)
    ctx = np.concatenate([cx[:, :, :KM, :].transpose(0, 3, 1, 2).reshape(NG, D, GB * KM), tail,
                          np.repeat(tail, NGR, axis=2)], 2)
    arrays = {
        "x": a["x"].reshape(NG, GB * S, D), "ctx": ctx, "mask": a["mask_Bx1xSxS2_ik1"].reshape(NG, GB, S, SK),
        "wsq": wsq,
        "w13": a["L0_ffn_w13_weight"].transpose(2, 0, 1),
        "w2a": a["L0_ffn_w2_weight"].reshape(E_N, D, 2, 128).transpose(3, 0, 2, 1),
        "w1": a["L1_ffn_W1"].transpose(1, 0, 2),
        "w2b": a["L1_ffn_W2"].reshape(E_N, 4, 128, D).transpose(2, 0, 1, 3),
        "const": constants(), "bcol": bcol, "brow": brow, "b2": a["L1_ffn_b2"],
    }
    arrays = {n: np.ascontiguousarray(v) for n, v in arrays.items()}
    nc = bacc.Bacc("TRN2", target_bir_lowering=False, num_devices=1)
    aps = [nc.dram_tensor(f"{n}_in", v.shape, mybir.dt.from_np(v.dtype), kind="ExternalInput").ap() for n, v in arrays.items()]
    out = nc.dram_tensor("out", (NG, GB * S, D), F32, kind="ExternalOutput").ap()
    perceiver(nc, *aps, out)
    r = run_bass_kernel_spmd(nc, [{f"{n}_in": v for n, v in arrays.items()}], core_ids=[0])
    return r.results[0]["out"].reshape(B, S, D)
```
